# Optimizing a Trainium2 kernel written in Bass

```python
import numpy as np
import jax
import jax.numpy as jnp

def _softmax(x, axis=-1):
    return jax.nn.softmax(x, axis=axis)

def _gelu(x):
    return jax.nn.gelu(x, approximate=True)

def _silu(x):
    return jax.nn.silu(x)

def _sigmoid(x):
    return jax.nn.sigmoid(x)

def _layernorm(x, axis=-1, eps=1e-05):
    m = jnp.mean(x, axis=axis, keepdims=True)
    v = jnp.var(x, axis=axis, keepdims=True)
    return (x - m) / jnp.sqrt(v + eps)

def _scatter_add(tgt, idx, src, axis=0):
    return tgt.at[idx].add(src)

def _segment_sum(src, seg, n):
    return jax.ops.segment_sum(src, seg, n)
kernel_name = 'mk_adj_ffn_d2_adj_r2_845830'

def setup_inputs(seed: int=0):
    np.random.seed(seed)
    _w = jnp.asarray

    def _rec_inputs():
        import jax
        import jax.numpy as jnp
        _gk = jax.random.key(seed)
        x = -0.0002928 + 1 * jax.random.normal(jax.random.fold_in(_gk, 1), (2048, 256), jnp.float32)
        _a = jax.random.bernoulli(jax.random.fold_in(_gk, 2), 0.0078125, (2048, 2048))
        _a = jnp.logical_or(_a, jnp.eye(2048, dtype=bool))
        _af = _a.astype(jnp.float32)
        _af = _af * jax.random.uniform(jax.random.fold_in(_gk, 3), (2048, 2048), jnp.float32, 0.05, 1)
        adj = _af
        return (x, adj)
    x, adj = _rec_inputs()

    def _L0_gnn_setup():
        import jax, jax.numpy as jnp
        import numpy as np
        N = 4096
        IN_DIM = 256
        HID = 256
        key = jax.random.key(seed)
        k1, k2, k3, k4 = jax.random.split(key, 4)
        input_features = jax.random.normal(k1, (N, IN_DIM), dtype=jnp.float32)
        adjacency_matrix = jax.random.uniform(k2, (N, N), dtype=jnp.float32)
        Wgcn1 = jax.random.normal(k3, (IN_DIM, HID), dtype=jnp.float32) * (1.0 / np.sqrt(IN_DIM / 2.0))
        bgcn1 = jnp.zeros((HID,), dtype=jnp.float32)
        Wgcn12 = jax.random.normal(k4, (HID, HID), dtype=jnp.float32) * (1.0 / np.sqrt(HID / 2.0))
        bgcn12 = jnp.zeros((HID,), dtype=jnp.float32)
        return {'input_features': input_features, 'adjacency_matrix': adjacency_matrix, 'Wgcn1': Wgcn1, 'bgcn1': bgcn1, 'Wgcn12': Wgcn12, 'bgcn12': bgcn12}
    _L0_gnn_all = _L0_gnn_setup()
    _L0_gnn_in = {k: v for k, v in _L0_gnn_all.items() if k in ('Wgcn1', 'bgcn1', 'Wgcn12', 'bgcn12')}
    del _L0_gnn_all

    def _L0_ffn_setup():
        import jax, jax.numpy as jnp
        import numpy as np
        B, S, D, H, E, K = (2, 1024, 256, 1024, 16, 2)
        LN_EPS = 1e-05
        key = jax.random.key(seed)
        ks = jax.random.split(key, 9)
        s_in = 1.0 / np.sqrt(D)
        s_hid = 1.0 / np.sqrt(H)
        return {'x': jax.random.normal(ks[0], (B, S, D), dtype=jnp.float32), 'Wg': jax.random.normal(ks[1], (D, E), dtype=jnp.float32) * s_in, 'bg': jax.random.normal(ks[2], (E,), dtype=jnp.float32) * 0.01, 'W1': jax.random.normal(ks[3], (E, D, H), dtype=jnp.float32) * s_in, 'b1': jax.random.normal(ks[4], (E, H), dtype=jnp.float32) * 0.01, 'W2': jax.random.normal(ks[5], (E, H, D), dtype=jnp.float32) * s_hid, 'b2': jax.random.normal(ks[6], (E, D), dtype=jnp.float32) * 0.01, 'gamma': jnp.ones((D,), dtype=jnp.float32), 'beta': jnp.zeros((D,), dtype=jnp.float32)}
    _L0_ffn_all = _L0_ffn_setup()
    _L0_ffn_in = {k: v for k, v in _L0_ffn_all.items() if k in ('Wg', 'bg', 'W1', 'b1', 'W2', 'b2', 'gamma', 'beta')}
    del _L0_ffn_all

    def _L1_gnn_setup():
        import jax, jax.numpy as jnp
        import numpy as np
        N = 4096
        DIN = 256
        DOUT = 256
        key = jax.random.key(seed)
        k1, k2, k3 = jax.random.split(key, 3)
        H_in = jax.random.normal(k1, (N, DIN), dtype=jnp.float32)
        u = jax.random.uniform(k2, (N, N), dtype=jnp.float32)
        upper = (u < 0.005).astype(jnp.float32)
        upper = jnp.triu(upper, k=1)
        A = upper + upper.T
        limit = np.sqrt(6.0 / (DIN + DOUT)).astype(np.float32)
        W = jax.random.uniform(k3, (DIN, DOUT), dtype=jnp.float32, minval=-limit, maxval=limit)
        return {'H_in': H_in, 'A': A, 'W': W}
    _L1_gnn_all = _L1_gnn_setup()
    _L1_gnn_in = {k: v for k, v in _L1_gnn_all.items() if k in ('W',)}
    del _L1_gnn_all

    def _L1_ffn_setup():
        import jax, jax.numpy as jnp
        import numpy as np
        B, L, D, H, E, K = (8, 4096, 256, 1024, 8, 2)
        SCALE = 0.02
        key = jax.random.key(seed)
        ks = jax.random.split(key, 6)
        return {'x': jax.random.normal(ks[0], (B, L, D), dtype=jnp.float32), 'Wg': jax.random.normal(ks[1], (D, E), dtype=jnp.float32) * SCALE, 'W1': jax.random.normal(ks[2], (E, D, H), dtype=jnp.float32) * SCALE, 'b1': jax.random.normal(ks[3], (E, H), dtype=jnp.float32) * SCALE, 'W2': jax.random.normal(ks[4], (E, H, D), dtype=jnp.float32) * SCALE, 'b2': jax.random.normal(ks[5], (E, D), dtype=jnp.float32) * SCALE}
    _L1_ffn_all = _L1_ffn_setup()
    _L1_ffn_in = {k: v for k, v in _L1_ffn_all.items() if k in ('Wg', 'W1', 'b1', 'W2', 'b2')}
    del _L1_ffn_all
    return {'x': x, 'adj': adj, 'L0_gnn_Wgcn1': _L0_gnn_in['Wgcn1'], 'L0_gnn_bgcn1': _L0_gnn_in['bgcn1'], 'L0_gnn_Wgcn12': _L0_gnn_in['Wgcn12'], 'L0_gnn_bgcn12': _L0_gnn_in['bgcn12'], 'L0_ffn_Wg': _L0_ffn_in['Wg'], 'L0_ffn_bg': _L0_ffn_in['bg'], 'L0_ffn_W1': _L0_ffn_in['W1'], 'L0_ffn_b1': _L0_ffn_in['b1'], 'L0_ffn_W2': _L0_ffn_in['W2'], 'L0_ffn_b2': _L0_ffn_in['b2'], 'L0_ffn_gamma': _L0_ffn_in['gamma'], 'L0_ffn_beta': _L0_ffn_in['beta'], 'L1_gnn_W': _L1_gnn_in['W'], 'L1_ffn_Wg': _L1_ffn_in['Wg'], 'L1_ffn_W1': _L1_ffn_in['W1'], 'L1_ffn_b1': _L1_ffn_in['b1'], 'L1_ffn_W2': _L1_ffn_in['W2'], 'L1_ffn_b2': _L1_ffn_in['b2']}

def reference(x, adj, L0_gnn_Wgcn1, L0_gnn_bgcn1, L0_gnn_Wgcn12, L0_gnn_bgcn12, L0_ffn_Wg, L0_ffn_bg, L0_ffn_W1, L0_ffn_b1, L0_ffn_W2, L0_ffn_b2, L0_ffn_gamma, L0_ffn_beta, L1_gnn_W, L1_ffn_Wg, L1_ffn_W1, L1_ffn_b1, L1_ffn_W2, L1_ffn_b2):
    import jax
    import jax.numpy as jnp

    def _L0_gnn_ref(input_features, adjacency_matrix, Wgcn1, bgcn1, Wgcn12, bgcn12):
        import jax, jax.numpy as jnp
        import numpy as np
        N = 4096
        IN_DIM = 256
        HID = 256
        d_inv_sqrt = jnp.power(adjacency_matrix.sum(axis=1), -0.5)
        norm_adj = d_inv_sqrt[:, None] * adjacency_matrix * d_inv_sqrt[None, :]
        support = input_features @ Wgcn1
        out = norm_adj @ support + bgcn1
        out = jax.nn.relu(out)
        support = out @ Wgcn12
        out = norm_adj @ support + bgcn12
        return out

    def _L0_ffn_ref(x, Wg, bg, W1, b1, W2, b2, gamma, beta):
        import jax, jax.numpy as jnp
        import numpy as np
        B, S, D, H, E, K = (2, 1024, 256, 1024, 16, 2)
        LN_EPS = 1e-05
        logits = jnp.einsum('bsd,de->bse', x, Wg) + bg
        probs = jax.nn.softmax(logits, axis=-1)
        topk_vals, topk_idx = jax.lax.top_k(probs, K)
        sparse = (jax.nn.one_hot(topk_idx, E, dtype=probs.dtype) * topk_vals[..., None]).sum(axis=-2)
        h = jax.nn.relu(jnp.einsum('bsd,edh->ebsh', x, W1) + b1[:, None, None, :])
        ex = jnp.einsum('ebsh,ehd->ebsd', h, W2) + b2[:, None, None, :]
        out = jnp.einsum('bse,ebsd->bsd', sparse, ex) + x
        mu = out.mean(axis=-1, keepdims=True)
        var = ((out - mu) ** 2).mean(axis=-1, keepdims=True)
        out = (out - mu) * jax.lax.rsqrt(var + LN_EPS) * gamma + beta
        return out

    def _L1_gnn_ref(H_in, A, W):
        import jax, jax.numpy as jnp
        import numpy as np
        N = 4096
        DIN = 256
        DOUT = 256
        A_ = A + jnp.eye(A.shape[0], dtype=A.dtype)
        d_inv_sqrt = jax.lax.rsqrt(A_.sum(axis=1))
        A_norm = A_ * d_inv_sqrt[:, None] * d_inv_sqrt[None, :]
        H_out = jnp.matmul(jnp.matmul(A_norm, H_in), W)
        return jax.nn.relu(H_out)

    def _L1_ffn_ref(x, Wg, W1, b1, W2, b2):
        import jax, jax.numpy as jnp
        import numpy as np
        B, L, D, H, E, K = (8, 4096, 256, 1024, 8, 2)
        SCALE = 0.02
        b, l, d = x.shape
        xt = x.reshape(-1, d)
        T = xt.shape[0]
        gate = jax.nn.softmax(xt @ Wg, axis=-1)
        topv, topi = jax.lax.top_k(gate, K)
        topv = topv / (jnp.sum(topv, axis=-1, keepdims=True) + 1e-06)
        scores = jnp.zeros((T, E), dtype=xt.dtype).at[jnp.arange(T)[:, None], topi].set(topv)
        out = jnp.zeros_like(xt)
        for e in range(E):
            h = jax.nn.gelu(xt @ W1[e] + b1[e], approximate=False)
            ye = h @ W2[e] + b2[e]
            out = out + ye * scores[:, e:e + 1]
        return out.reshape(b, l, d)
    x = x + _L0_gnn_ref(_layernorm(x, axis=-1), adj, L0_gnn_Wgcn1, L0_gnn_bgcn1, L0_gnn_Wgcn12, L0_gnn_bgcn12)
    x = x + _L0_ffn_ref(_layernorm(x, axis=-1)[None], L0_ffn_Wg, L0_ffn_bg, L0_ffn_W1, L0_ffn_b1, L0_ffn_W2, L0_ffn_b2, L0_ffn_gamma, L0_ffn_beta)[0]
    x = x + _L1_gnn_ref(_layernorm(x, axis=-1), adj, L1_gnn_W)
    x = x + _L1_ffn_ref(_layernorm(x, axis=-1)[None], L1_ffn_Wg, L1_ffn_W1, L1_ffn_b1, L1_ffn_W2, L1_ffn_b2)[0]
    return x

_drawn_inputs = setup_inputs


def setup_inputs(seed=0):
    import zlib

    import numpy as np

    out = dict(_drawn_inputs(seed))
    spreads = {'L0_gnn_bgcn1': (0.0, 0.1),
     'L0_gnn_bgcn12': (0.0, 0.1),
     'L0_ffn_gamma': (1.0, 0.2),
     'L0_ffn_beta': (0.0, 0.1)}
    factors = {'L0_ffn_bg': 8.0,
     'L0_ffn_b1': 43.639,
     'L0_ffn_b2': 33.355,
     'L1_ffn_b1': 22.345,
     'L1_ffn_b2': 7.914}
    for name, (base, spread) in spreads.items():
        noise = np.random.default_rng([zlib.crc32(name.encode()), seed]).standard_normal(out[name].shape)
        drawn = base * np.exp(spread * noise) if base else spread * noise
        out[name] = jnp.asarray(drawn.astype(out[name].dtype))
    for name, factor in factors.items():
        out[name] = (out[name] * factor).astype(out[name].dtype)
    return out
```

```python
from contextlib import ExitStack

import concourse.bass as bass
from concourse import mybir

F32 = mybir.dt.float32
F32R = mybir.dt.float32r
BF16 = mybir.dt.bfloat16
I32 = mybir.dt.int32
ALU = mybir.AluOpType
ACT = mybir.ActivationFunctionType
AX = mybir.AxisListType
ds = bass.ds

P = 128
BANK = 512
LN_EPS = 1e-5
LOWEST = -3.0e38


def moe_gnn_kernel(nc, x, adj, wgcn1, bgcn1, wgcn12, bgcn12, wg0, bg0, w1_0, b1_0, w2_0, b2_0, gamma, beta,
                   wgnn, wg1, w1_1, b1_1, w2_1, b2_1, out):
    N, D = x.shape
    KD = D // P
    NT = N // P
    WIDE = 512
    NB = N // WIDE
    UB = WIDE // P
    H = w1_0.shape[2]
    HC = H // P
    EXPERTS = [w1_0.shape[0], w1_1.shape[0]]
    EMAX = max(EXPERTS)
    TILES = [(2 * N + P * E - 1) // P for E in EXPERTS]
    TMAX = max(TILES)
    WG, BG = [wg0, wg1], [bg0, None]
    W1, B1, W2, B2 = [w1_0, w1_1], [b1_0, b1_1], [w2_0, w2_1], [b2_0, b2_1]
    HB = H // BANK
    HCB = HC // HB

    adjT_d = nc.dram_tensor("adjT_d", [N, N], F32, kind="Internal").ap()
    xn_d = nc.dram_tensor("xn_d", [N, D], F32, kind="Internal").ap()
    y_d = [nc.dram_tensor(f"y{l}_d", [2 * N, D], F32, kind="Internal").ap() for l in range(2)]

    ctx = ExitStack()
    with ctx:
        base = ((nc.sbuf_base + 63) // 64) * 64
        top = [base]

        def sb(name, shape, dt, at=None):
            size = 1
            for s in shape[1:]:
                size *= s
            size *= 2 if dt == BF16 else 4
            off = top[0] if at is None else at
            t = nc.alloc_sbuf_tensor_at(name, shape, dt, offset=off)
            end = (off + size + 63) // 64 * 64
            if at is None:
                top[0] = end
            return t, end

        def lasting(name, shape, dt):
            return sb(name, shape, dt)[0]

        R = lasting("R", [P, NT, D], F32)
        ident = lasting("ident", [P, P], F32)[:]
        before = lasting("before", [P, P], BF16)
        ones = lasting("ones", [P, P], BF16)
        iota = lasting("iota", [P, P], BF16)
        pid = lasting("pid", [P, 1], F32)
        dec = lasting("dec", [P, EMAX], F32)
        keep = lasting("keep", [P, EMAX, NT], F32)
        thr = lasting("thr", [P, NT], F32)
        code = lasting("code", [P, 2, NT], F32)
        half = lasting("half", [P, NT], F32)
        bgcn_bc = lasting("bgcn_bc", [P, 2, D], F32)
        bg_bc = lasting("bg_bc", [P, EMAX], F32)
        wgate = lasting("wgate", [P, KD, 2, EMAX], F32)
        dis = lasting("dis", [P, 2, NT], F32)
        deg = lasting("deg", [P, 2, NT], F32)
        stats = lasting("stats", [P, UB, 6], F32)
        mvb = lasting("mvb", [P, UB, 2], F32)
        mv = lasting("mv", [P, NT, 2], F32)
        vare = lasting("vare", [P, NT], F32)
        rstd = lasting("rstd", [P, NT], F32)
        L = lasting("L", [P, NT, EMAX], F32)
        gate = lasting("gate", [P, 2, NT], F32)
        table = lasting("table", [1, 2, TMAX + 1], I32)
        idx = lasting("idx", [P, 2, TMAX], I32)
        idx_use = lasting("idx_use", [P, 2], I32)
        shared = top[0]

        cur = [shared]

        def in_set(name, shape, dt):
            t, cur[0] = sb(name, shape, dt, at=cur[0])
            return t

        AT = in_set("AT", [P, NT, N], F32)
        Xhi = in_set("Xhi", [P, NT, D], F32R)
        Xlo = in_set("Xlo", [P, NT, D], F32R)
        Ahi = in_set("Ahi", [P, 2, WIDE], F32R)
        Alo = in_set("Alo", [P, 2, WIDE], F32R)
        Ghi = in_set("Ghi", [P, KD, WIDE], F32R)
        Glo = in_set("Glo", [P, KD, WIDE], F32R)
        Whi = in_set("Whi", [P, KD, D], F32R)
        Wlo = in_set("Wlo", [P, KD, D], F32R)
        gnn_end = cur[0]
        STG = 4
        stage_off = shared + NT * N * 4
        stage = [sb(f"stage{u}", [P, N], F32, at=stage_off + u * N * 4)[0] for u in range(STG)]
        assert STG * N * 4 <= 2 * NT * D * 4
        cur[0] = gnn_end
        xnb = sb("xnb", [P, UB, D], F32, at=gnn_end - 2 * KD * D * 4 - 2 * KD * WIDE * 4)[0]
        xnT = in_set("xnT", [P, 2, BANK], F32)
        Wraw = sb("Wraw", [P, KD, D], F32, at=cur[0] - 2 * BANK * 4)[0]
        assert cur[0] <= nc.sbuf_usable_end, (cur[0], nc.sbuf_usable_end)
        cur[0] = gnn_end - 2 * KD * D * 4 - 2 * KD * WIDE * 4
        iota_i = in_set("iota_i", [P, P], I32)
        pid_i = in_set("pid_i", [P, 1], I32)
        dec_i = in_set("dec_i", [P, EMAX], I32)
        thr_i = in_set("thr_i", [P, NT], I32)
        code_i = in_set("code_i", [P, 2, NT], I32)

        cur[0] = shared
        raw1 = in_set("raw1", [P, KD, H], F32)
        raw2 = in_set("raw2", [P, HC, D], F32)
        XN = in_set("XN", [P, NT, D], F32)
        w1hi = in_set("w1hi", [P, 2, KD, H], F32R)
        w1lo = in_set("w1lo", [P, 2, KD, H], F32R)
        w2hi = in_set("w2hi", [P, 2, HC, D], F32R)
        w2lo = in_set("w2lo", [P, 2, HC, D], F32R)
        hThi = in_set("hThi", [P, HC, P], F32R)
        hTlo = in_set("hTlo", [P, HC, P], F32R)
        assert cur[0] <= shared + NT * N * 4
        cur[0] = shared + NT * N * 4
        b1_bc = in_set("b1_bc", [P, 4, H], F32)
        b2_bc = in_set("b2_bc", [P, 4, D], F32)
        hrow = in_set("hrow", [P, H], F32)
        xg = in_set("xg", [P, D], F32)
        xThi = in_set("xThi", [P, KD, P], F32R)
        xTlo = in_set("xTlo", [P, KD, P], F32R)
        y_sb = in_set("y_sb", [P, D], F32)
        gb_bc = in_set("gb_bc", [P, 2, D], F32)
        assert cur[0] <= gnn_end
        cur[0] = shared + NT * N * 4
        oh = [in_set(f"oh{k}", [P, NT, EMAX], F32) for k in range(2)]
        L2 = in_set("L2", [P, NT, EMAX], F32)
        rt = in_set("rt", [P, NT, EMAX], F32)
        ex = in_set("ex", [P, NT, EMAX], F32)
        mx = [in_set(f"mx{k}", [P, NT], F32) for k in range(2)]
        pick = in_set("pick", [P, NT], F32)
        zsum = in_set("zsum", [P, NT], F32)
        zrec = in_set("zrec", [P, NT], F32)
        e2 = in_set("e2", [P, NT], F32)
        gsum = in_set("gsum", [P, NT], F32)
        M = in_set("M", [P, EMAX, NT], BF16)
        incl = in_set("incl", [P, EMAX, NT], F32)
        more = in_set("more", [P, EMAX, NT], F32)
        tiles_e = in_set("tiles_e", [P, EMAX], F32)
        tend = in_set("tend", [P, EMAX], F32)
        tstart = in_set("tstart", [P, EMAX], F32)
        pos = in_set("pos", [P, 2, NT], F32)
        pos_i = in_set("pos_i", [P, 2, NT], I32)
        rt_i = in_set("rt_i", [P, 2, 2, NT], I32)
        rt_f = in_set("rt_f", [P, 2, 2, NT], F32)
        Brow = in_set("Brow", [P, NT, P], BF16)
        Acol = in_set("Acol", [P, NT, TMAX], BF16)
        Arhs = in_set("Arhs", [P, NT, 2, TMAX], BF16)
        Brow2 = in_set("Brow2", [P, NT, P], BF16)
        Arhs2 = in_set("Arhs2", [P, NT, 2, TMAX], BF16)
        F_sb = in_set("F_sb", [P, 2, TMAX], F32)
        sl = in_set("sl", [P, 4, TMAX], F32)
        tcmp = in_set("tcmp", [1, TMAX, EMAX], F32)
        tsum = in_set("tsum", [1, 2, TMAX], F32)
        assert cur[0] <= nc.sbuf_usable_end
        comb_off = shared + NT * N * 4 + 2 * NT * D * 4
        Yc, _ = sb("Yc", [P, UB, 2, D], F32, at=comb_off)
        assert comb_off + UB * 2 * D * 4 <= shared + NT * N * 4 + 2 * NT * D * 4 + 2 * 2 * WIDE * 4
        SG, SJ = 4, 2
        strm = [sb(f"strm{s}", [P, SJ, WIDE], F32, at=shared + s * SJ * WIDE * 4)[0] for s in range(SG)]
        assert SG * SJ * WIDE * 4 <= (KD * H + HC * D) * 4
        cur[0] = shared + (KD * H + HC * D) * 4 + NT * D * 4
        U_sb = in_set("U_sb", [P, 2, D], F32)
        loops = in_set("loops", [P, 2 * NB - 1, P], F32)

        PS = ctx.enter_context(nc.psum_tensor("PS", [P, 8, BANK], F32))
        U_PS, XT_PS, LG_PS = (4, 5), (6, 4), 7
        H_PS, HT_PS, XG_PS, Y_PS = (0, 1), (2, 3), 4, 5
        RANK_PS, TOT_PS, SLOT_PS = 4, 5, 6

        names = {}

        def S(name):
            if name not in names:
                names[name] = ctx.enter_context(nc.semaphore(name))
            return names[name]

        class Chain:

            def __init__(self, eng, sem, start=0):
                self.eng, self.sem, self.start, self.n = eng, sem, start, 0

            def done(self, ins):
                ins.then_inc(self.sem, 1)
                self.n += 1
                self.eng.wait_ge(self.sem, self.start + self.n)

        def step_apart(eng):
            eng.sem_inc(S("apart_pool" if eng is nc.gpsimd or "Gp" in type(eng).__name__ else "apart_dve"), 1)

        def per_token(ap, n):
            return ap.unsqueeze(2).to_broadcast([P, ap.shape[1], n])

        adjT_tiles = adjT_d.rearrange("(j p) i -> p j i", p=P)
        x_tiles = x.rearrange("(t p) d -> p t d", p=P)
        xn_tiles = xn_d.rearrange("(t p) d -> p t d", p=P)
        out_tiles = out.rearrange("(t p) d -> p t d", p=P)
        y_tiles = [y.rearrange("(k t p) d -> p t k d", p=P, k=2) for y in y_d]
        Wg = [wgcn1, wgcn12, wgnn]

        block = ctx.enter_context(nc.Block())

        @block.sync
        def _(sp):
            sp.dma_start(R[:], x_tiles).then_inc(S("x_in"), 16)

            for u in range(STG):
                sp.dma_start(stage[u][:], adj[u * P:(u + 1) * P, :]).then_inc(S(f"stage_in{u}"), 16)
            bc = lambda row, n: row.rearrange("(a n) -> a n", a=1).to_broadcast([P, n])
            sp.dma_start(bgcn_bc[:, 0, :], bc(bgcn1, D)).then_inc(S("const_in"), 16)
            sp.dma_start(bgcn_bc[:, 1, :], bc(bgcn12, D)).then_inc(S("const_in"), 16)
            sp.dma_start(bg_bc[:], bc(bg0, EXPERTS[0])).then_inc(S("const_in"), 16)
            for l in range(2):
                sp.dma_start(wgate[:, :, l, 0:EXPERTS[l]], WG[l].rearrange("(k p) e -> p k e", p=P)).then_inc(S("const_in"), 16)
            sp.dma_start(Wraw[:], Wg[0].rearrange("(k p) d -> p k d", p=P)).then_inc(S("wg_in"), 16)
            with sp.Fori(1, NT // STG) as i:
                for u in range(STG):
                    sp.wait_ge(S(f"stage_read{u}"), i)
                    sp.wait_ge(S("at_psum"), 4 * ((i - 1) * STG + u + 1))
                    sp.dma_start(stage[u][:], adj[ds((i * STG + u) * P, P), :]).then_inc(S(f"stage_in{u}"), 16)

            sp.wait_ge(S("at_copied"), 4 * NT)
            sp.dma_start(adjT_tiles, AT[:]).then_inc(S("at_out"), 16)

            sp.wait_ge(S("wg_split"), 1)
            sp.dma_start(Wraw[:], Wg[1].rearrange("(k p) d -> p k d", p=P)).then_inc(S("wg_in"), 16)
            sp.wait_ge(S("xlo1"), NB)
            sp.dma_start(R[:], x_tiles).then_inc(S("x_again"), 16)
            for l in range(2):
                sp.sem_inc(S(f"xn_out{l}"), 16)
            sp.wait_ge(S("xn_out_ready0"), 1)
            sp.dma_start(xn_tiles[:, 0:UB, :], xnb[:]).then_inc(S("xn_out0"), 16)
            with sp.Fori(1, NB) as ib:
                sp.wait_ge(S("xn_out_ready0"), ib + 1)
                sp.dma_start(xn_tiles[:, ds(ib * UB, UB), :], xnb[:]).then_inc(S("xn_out0"), 16)

            def expert_loads(l):
                E = EXPERTS[l]
                w1v = W1[l].rearrange("e (k p) h -> p e k h", p=P)
                w2v = W2[l].rearrange("e (c p) d -> p e c d", p=P)

                def load(e, slot, first=False):
                    if not first:
                        sp.wait_ge(S(f"w1_split{l}"), KD * e)
                    sp.dma_start(raw1[:], w1v[:, ds(e, 1), :, :].rearrange("p a k h -> p (a k) h")).then_inc(S(f"w1_in{l}"), 16)
                    sp.dma_start(b1_bc[:, slot, :], B1[l][ds(e, 1), :].to_broadcast([P, H])).then_inc(S(f"w1_in{l}"), 16)
                    if not first:
                        sp.wait_ge(S(f"w2_split{l}"), 2 * e)
                    sp.dma_start(raw2[:], w2v[:, ds(e, 1), :, :].rearrange("p a c d -> p (a c) d")).then_inc(S(f"w2_in{l}"), 16)
                    sp.dma_start(b2_bc[:, slot, :], B2[l][ds(e, 1), :].to_broadcast([P, D])).then_inc(S(f"w2_in{l}"), 16)

                for e in range(4):
                    load(e, e, first=e == 0)
                with sp.Fori(1, E // 4) as q:
                    for s in range(4):
                        load(q * 4 + s, s)

            sp.wait_ge(S("a_free1"), NT * NB + 2)
            sp.wait_ge(S("at_out"), 16)
            sp.wait_ge(S("xn_out0"), 16 * (NB + 1))
            sp.dma_start(XN[:], xn_tiles).then_inc(S("xn_in"), 16)
            sp.wait_ge(S("routed0"), 1)
            sp.dma_start(gb_bc[:, 0, :], bc(gamma, D)).then_inc(S("xn_in"), 16)
            sp.dma_start(gb_bc[:, 1, :], bc(beta, D)).then_inc(S("xn_in"), 16)
            expert_loads(0)

            def combine_loads(l):
                sp.wait_ge(S(f"y_out{l}"), 16 * TILES[l])
                for k in range(2):
                    sp.dma_start(Yc[:, :, k, :], y_tiles[l][:, 0:UB, k, :]).then_inc(S(f"yc_in{l}"), 16)
                with sp.Fori(1, NB) as ib:
                    sp.wait_ge(S(f"yc_read{l}"), ib)
                    for k in range(2):
                        sp.dma_start(Yc[:, :, k, :], y_tiles[l][:, ds(ib * UB, UB), k, :]).then_inc(S(f"yc_in{l}"), 16)

            combine_loads(0)
            sp.wait_ge(S("wg_split"), 2)
            sp.dma_start(Wraw[:], Wg[2].rearrange("(k p) d -> p k d", p=P)).then_inc(S("wg_in"), 16)
            GPB = NT // SJ

            def stream(ib, q, s):
                sp.dma_start(strm[s][:], adjT_tiles[:, q * SG * SJ + s * SJ:q * SG * SJ + (s + 1) * SJ,
                                                    ds(ib * WIDE, WIDE)]).then_inc(S(f"strm_in{s}"), 16)

            for s in range(SG):
                stream(0, 0, s)
            for q in range(1, GPB // SG):
                for s in range(SG):
                    sp.wait_ge(S("alo2"), SJ * (SG * (q - 1) + s + 1))
                    stream(0, q, s)
            with sp.Fori(1, NB) as ib:
                for q in range(GPB // SG):
                    for s in range(SG):
                        sp.wait_ge(S("alo2"), ib * NT + SJ * (SG * (q - 1) + s + 1))
                        stream(ib, q, s)
                sp.wait_ge(S("xn_out_ready1"), ib)
                sp.dma_start(xn_tiles[:, ds((ib - 1) * UB, UB), :], xnb[:]).then_inc(S("xn_out1"), 16)
            sp.wait_ge(S("xn_out_ready1"), NB)
            sp.dma_start(xn_tiles[:, (NB - 1) * UB:, :], xnb[:]).then_inc(S("xn_out1"), 16)
            sp.wait_ge(S("a_free2"), NT * NB + 2)
            sp.wait_ge(S("routed1"), 1)
            expert_loads(1)
            combine_loads(1)
            sp.wait_ge(S("final"), NB)
            sp.dma_start(out_tiles, R[:]).then_inc(S("out_done"), 16)
            sp.wait_ge(S("out_done"), 16)

        @block.gpsimd
        def _(pool):
            c = Chain(pool, S("pool_const"))
            c.done(pool.memset(ident, 0.0))
            c.done(pool.affine_select(out=ident, in_=ident, compare_op=ALU.not_equal, fill=1.0, base=0,
                                      pattern=[[-1, P]], channel_multiplier=1))
            c.done(pool.memset(half[:], -0.5))
            pool.sem_inc(S("consts"), 1)
            c.done(pool.memset(ones[:], 1.0))
            c.done(pool.memset(before[:], 0.0))
            c.done(pool.affine_select(out=before[:], in_=before[:], compare_op=ALU.is_gt, fill=-1.0, base=0,
                                      pattern=[[1, P]], channel_multiplier=-1))
            c.done(pool.memset(keep[:], 1.0))
            c.done(pool.affine_select(out=keep[:], in_=keep[:], compare_op=ALU.not_equal, fill=0.0, base=0,
                                      pattern=[[0, EMAX], [1, NT]], channel_multiplier=0))
            c.done(pool.iota(iota_i[:], pattern=[[1, P]], base=0, channel_multiplier=0))
            c.done(pool.iota(pid_i[:], pattern=[[0, 1]], base=0, channel_multiplier=1))
            c.done(pool.iota(dec_i[:], pattern=[[-1, EMAX]], base=EMAX, channel_multiplier=0))
            c.done(pool.iota(thr_i[:], pattern=[[P, NT]], base=0, channel_multiplier=0))
            c.done(pool.iota(code_i[:], pattern=[[NT, 2], [1, NT]], base=1, channel_multiplier=0))
            c.done(pool.tensor_copy(iota[:], iota_i[:]))
            c.done(pool.tensor_copy(pid[:], pid_i[:]))
            c.done(pool.tensor_copy(dec[:], dec_i[:]))
            c.done(pool.tensor_copy(thr[:], thr_i[:]))
            c.done(pool.tensor_copy(code[:], code_i[:]))
            c.done(pool.memset(thr[:, 0:1], -1.0))
            pool.sem_inc(S("consts"), 1)

            pool.wait_ge(S("deg_ready"), 1)
            pool.tensor_tensor(dis[:, 0, :], deg[:, 0, :], half[:], ALU.pow).then_inc(S("dis"), 1)
            pool.tensor_tensor(dis[:, 1, :], deg[:, 1, :], half[:], ALU.pow).then_inc(S("dis"), 1)
            pool.tensor_tensor(rstd[:], vare[:], half[:], ALU.pow).then_inc(S("dis"), 1)

            def residual(p, l):

                def self_loop(ib, j):
                    q, s = divmod(j // SJ, SG)
                    if j % SJ == 0:
                        pool.wait_ge(S(f"strm_in{s}"), 16 * (ib * (NT // SJ // SG) + q + 1))
                    step_apart(pool)
                    part = strm[s][:, j % SJ, (j % UB) * P:(j % UB + 1) * P]
                    pool.tensor_tensor(part, part, loops[:, ds(ib + (NB - 1 - j // UB), 1), :].rearrange("p a n -> p (a n)"),
                                       ALU.add).then_inc(S("looped"), 1)

                def add(ib, u):
                    tile = R[:, ds(UB * ib + u, 1), :].rearrange("p a d -> p (a d)")
                    pool.wait_ge(S(f"u_sb{p}"), UB * ib + u + 3)
                    if p == 1:
                        pool.wait_ge(S("const_in"), 16 * 5)
                    step_apart(pool)
                    pool.tensor_tensor(tile, tile, bgcn_bc[:, 1, :] if p == 1 else U_sb[:, u % 2, :],
                                       ALU.add).then_inc(S(f"res{p}"), 1)

                def sigma(ib):
                    pool.wait_ge(S(f"vare{l}"), ib + 1)
                    step_apart(pool)
                    pool.tensor_tensor(rstd[:, ds(UB * ib, UB)], vare[:, ds(UB * ib, UB)], half[:, 0:UB],
                                       ALU.pow).then_inc(S(f"rstd{l}"), 1)

                def block_end(ib):
                    for u in range(UB):
                        add(ib, u)
                    sigma(ib)

                if p == 1:
                    with pool.Fori(0, NB) as ib:
                        block_end(ib)
                    return
                pool.wait_ge(S("cmb_vare"), 2)
                pool.memset(loops[:], 0.0).then_inc(S("loops"), 1)
                pool.wait_ge(S("loops"), 1)
                pool.tensor_copy(loops[:, NB - 1, :], ident).then_inc(S("loops"), 1)
                pool.wait_ge(S("loops"), 2)
                for j in range(NT):
                    self_loop(0, j)
                with pool.Fori(1, NB) as ib:
                    for j in range(NT):
                        self_loop(ib, j)
                        if 6 <= j < 6 + UB:
                            add(ib - 1, j - 6)
                        if j == 6 + UB:
                            sigma(ib - 1)
                block_end(NB - 1)

            def expert_moves(l):
                T = TILES[l]

                def gather(t):
                    pool.tensor_copy(idx_use[:, 0:1], idx[:, 0, ds(t, 1)]).then_inc(S(f"idx_g{l}"), 1)
                    pool.wait_ge(S(f"idx_g{l}"), t + 1)
                    step_apart(pool)
                    pool.indirect_dma_start(xg[:], None, xn_d, bass.IndirectOffsetOnAxis(idx_use[:, 0:1], 0),
                                            bounds_check=N - 1, oob_is_err=True).then_inc(S(f"xg_in{l}"), 16)

                def scatter(t, first=False):
                    if not first:
                        pool.wait_ge(S(f"y_out{l}"), 16 * t)
                    pool.tensor_copy(idx_use[:, 1:2], idx[:, 1, ds(t, 1)]).then_inc(S(f"idx_s{l}"), 1)
                    pool.wait_ge(S(f"idx_s{l}"), t + 1)
                    pool.wait_ge(S(f"y_ready{l}"), t + 1)
                    step_apart(pool)
                    pool.indirect_dma_start(y_d[l], bass.IndirectOffsetOnAxis(idx_use[:, 1:2], 0), y_sb[:], None,
                                            bounds_check=2 * N - 1, oob_is_err=False).then_inc(S(f"y_out{l}"), 16)

                pool.wait_ge(S(f"routed{l}"), 1)
                pool.wait_ge(S(f"xn_out{l}"), 16 * (NB + 1))
                gather(0)
                pool.wait_ge(S(f"xg_in{l}"), 16)
                pool.wait_ge(S(f"xt_done{l}"), 1)
                gather(1)
                pool.wait_ge(S(f"xg_in{l}"), 32)
                pool.wait_ge(S(f"xt_done{l}"), 2)
                gather(2)
                scatter(0, first=True)
                with pool.Fori(2, T - 1) as t:
                    pool.wait_ge(S(f"xg_in{l}"), 16 * (t + 1))
                    pool.wait_ge(S(f"xt_done{l}"), t + 1)
                    gather(t + 1)
                    scatter(t - 1)
                scatter(T - 2)
                scatter(T - 1)

            residual(1, 0)
            expert_moves(0)
            pool.wait_ge(S("cmb_vare"), 1)
            pool.tensor_tensor(rstd[:], vare[:], half[:], ALU.pow).then_inc(S("cmb_rstd"), 1)
            pool.wait_ge(S("cmb_vare"), 2)
            pool.tensor_tensor(rstd[:], vare[:], half[:], ALU.pow).then_inc(S("cmb_rstd"), 1)
            residual(2, 1)
            expert_moves(1)

        @block.scalar
        def _(act):
            with act.Fori(0, NT) as r:
                for q in range(4):
                    act.wait_ge(S("at_psum"), 4 * r + q + 1)
                    act.activation(AT[:, 4 * q:4 * q + 4, ds(r * P, P)],
                                   PS[:, 4 + q, :].rearrange("p (j i) -> p j i", j=4), ACT.Copy).then_inc(S("at_copied"), 1)

            def split_x(p, src):
                for q in range(NB):
                    act.wait_ge(S(f"x_scaled{p}"), q + 1)
                    act.activation(Xhi[:, UB * q:UB * q + UB, :], src[:, UB * q:UB * q + UB, :],
                                   ACT.Copy).then_inc(S(f"xhi{p}"), 1)

            def split_w(p):
                act.wait_ge(S("wg_in"), 16 * (p + 1))
                act.activation(Whi[:], Wraw[:], ACT.Copy).then_inc(S("whi"), 1)

            def gnn(p):
                def steps(ib, mid=None):
                    for j in range(NT):
                        if p == 2:
                            act.wait_ge(S("looped"), NT * ib + j + 1)
                        act.wait_ge(S(f"a_free{p}"), NT * ib + j + 1)
                        src = strm[(j // SJ) % SG][:, j % SJ, :] if p == 2 else \
                            AT[:, j, ds(ib * WIDE, WIDE)]
                        act.activation(Ahi[:, j % 2, :], src, ACT.Copy).then_inc(S(f"ahi{p}"), 1)
                        if mid is not None:
                            mid(j)

                def split_g(ib):
                    act.wait_ge(S(f"a_free{p}"), NT * (ib + 1) + 2)
                    act.wait_ge(S(f"u_done{p}"), UB * ib + 1)
                    if p > 0:
                        act.wait_ge(S(f"xn_out{p - 1}"), 16 * (ib + 1))
                    for d in range(KD):
                        act.activation(Ghi[:, d, :], PS[:, ds((ib % 2) * KD + d, 1), :].rearrange("p a n -> p (a n)"),
                                       ACT.Copy).then_inc(S(f"ghi{p}"), 1)

                def relu(ib, u):
                    act.wait_ge(S(f"u_sb{p}"), UB * ib + u + 3)
                    tile = R[:, ds(UB * ib + u, 1), :].rearrange("p a d -> p (a d)")
                    act.activation(tile, tile, ACT.Relu,
                                   scale=dis[:, 0, ds(UB * ib + u, 1)]).then_inc(S(f"res{p}"), 1)

                def gate_in(l, ib, h):
                    act.wait_ge(S(f"xt_psum{l}"), 2 * ib + h + 1)
                    act.activation(xnT[:, h, :], PS[:, XT_PS[h], :], ACT.Copy).then_inc(S(f"xnT{l}"), 1)

                def after(ib):
                    def mid(j):
                        if j == 1:
                            split_g(ib)
                        if p == 0 and j in (7, 9, 11, 13):
                            relu(ib, (j - 7) // 2)
                        if p > 0 and j in (13, 14):
                            gate_in(p - 1, ib, j - 13)
                    return mid

                steps(0)
                with act.Fori(1, NB) as ib:
                    steps(ib, after(ib - 1))
                end = after(NB - 1)
                for j in range(NT):
                    end(j)

            def experts(l, func):
                E, T = EXPERTS[l], TILES[l]

                def split1(e, k, slot):
                    act.wait_ge(S(f"w1_in{l}"), 32 * (e + 1))
                    act.activation(w1hi[:, slot, k, :], raw1[:, k, :], ACT.Copy).then_inc(S(f"w1_hi{l}"), 1)

                def split2(e, q, slot):
                    act.wait_ge(S(f"w2_in{l}"), 32 * (e + 1))
                    act.activation(w2hi[:, slot, 4 * q:4 * q + 4, :], raw2[:, 4 * q:4 * q + 4, :],
                                   ACT.Copy).then_inc(S(f"w2_hi{l}"), 1)

                def split1_dyn(e, k):
                    act.wait_ge(S(f"w1_in{l}"), 32 * (e + 2))
                    act.activation(w1hi[:, ds((e + 1) % 2, 1), k, :].rearrange("p a h -> p (a h)"), raw1[:, k, :],
                                   ACT.Copy).then_inc(S(f"w1_hi{l}"), 1)

                def split2_dyn(e, q):
                    act.wait_ge(S(f"w2_in{l}"), 32 * (e + 2))
                    act.activation(w2hi[:, ds((e + 1) % 2, 1), 4 * q:4 * q + 4, :].rearrange("p a c d -> p (a c) d"),
                                   raw2[:, 4 * q:4 * q + 4, :], ACT.Copy).then_inc(S(f"w2_hi{l}"), 1)

                def x_hi(t):
                    act.wait_ge(S(f"xt_done{l}"), t + 1)
                    act.activation(xThi[:], PS[:, XG_PS, 0:KD * P].rearrange("p (k t) -> p k t", k=KD),
                                   ACT.Copy).then_inc(S(f"x_hi{l}"), 1)

                def tile(t, first=False, last=False):
                    if first:
                        e = 0
                    else:
                        e = act.value_load(table[0:1, 0, ds(t, 1)], min_val=0, max_val=E - 1)
                        opens = act.value_load(table[0:1, 1, ds(t, 1)], min_val=0, max_val=1)
                    for b in range(HB):
                        act.wait_ge(S(f"h_biased{l}"), HB * t + b + 1)
                        act.activation(hrow[:, b * BANK:(b + 1) * BANK], hrow[:, b * BANK:(b + 1) * BANK],
                                       func).then_inc(S(f"h_act{l}"), 1)
                    if not last:
                        x_hi(t + 1)
                    if first:
                        for k in range(KD):
                            split1_dyn(0, k)
                    else:
                        with act.If(opens == 1):
                            for k in range(KD):
                                split1_dyn(e, k)
                    for b in range(HB):
                        act.wait_ge(S(f"ht_done{l}"), HB * t + b + 1)
                        act.activation(hThi[:, b * HCB:(b + 1) * HCB, :],
                                       PS[:, HT_PS[b], :].rearrange("p (c t) -> p c t", c=HCB),
                                       ACT.Copy).then_inc(S(f"h_hi{l}"), 1)
                    if first:
                        for q in range(2):
                            split2_dyn(0, q)
                    else:
                        with act.If(opens == 1):
                            act.wait_ge(S(f"y_done{l}"), t)
                            for q in range(2):
                                split2_dyn(e, q)
                        act.nop()

                act.wait_ge(S(f"routed{l}"), 1)
                for k in range(KD):
                    split1(0, k, 0)
                for q in range(2):
                    split2(0, q, 0)
                x_hi(0)
                tile(0, first=True)
                with act.Fori(1, T - 1) as t:
                    tile(t)
                tile(T - 1, last=True)

            split_x(0, R)
            split_w(0)
            gnn(0)
            split_x(1, R)
            split_w(1)
            gnn(1)
            act.wait_ge(S("exp_in0"), 1)
            act.activation(ex[:, :, 0:EXPERTS[0]], rt[:, :, 0:EXPERTS[0]], ACT.Exp).then_inc(S("exp_out0"), 1)
            act.activation(e2[:], pick[:], ACT.Exp).then_inc(S("exp_out0"), 1)
            experts(0, ACT.Relu)
            split_x(2, XN)
            split_w(2)
            gnn(2)
            act.wait_ge(S("exp_in1"), 1)
            act.activation(ex[:, :, 0:EXPERTS[1]], rt[:, :, 0:EXPERTS[1]], ACT.Exp).then_inc(S("exp_out1"), 1)
            act.activation(e2[:], pick[:], ACT.Exp).then_inc(S("exp_out1"), 1)
            experts(1, ACT.Gelu)

        @block.vector
        def _(dve):
            def norm_stats(src, u, sem, start):
                ch = Chain(dve, sem, start)
                step_apart(dve)
                ch.done(dve.bn_stats(stats[:, u, :], src))
                step_apart(dve)
                ch.done(dve.bn_aggr(mvb[:, u, :], stats[:, u, :]))

            dve.wait_ge(S("x_in"), 16)
            with dve.Fori(0, NT // STG) as i:
                for u in range(STG):
                    T = i * STG + u
                    norm_stats(R[:, ds(T, 1), :].rearrange("p a d -> p (a d)"), u, S("stat0"), 2 * T + i)
                    dve.wait_ge(S(f"stage_in{u}"), 16 * (i + 1))
                    dve.tensor_reduce(deg[:, 0, ds(T, 1)], stage[u][:], AX.X, ALU.add).then_inc(S(f"stage_read{u}"), 1)
                ch = Chain(dve, S("stat0"), (2 * STG + 1) * i + 2 * STG)
                ch.done(dve.tensor_copy(mv[:, ds(i * STG, STG), :], mvb[:]))
            c = Chain(dve, S("dve_load"))
            for u in range(STG):
                dve.wait_ge(S(f"stage_read{u}"), NT // STG)
            c.done(dve.tensor_scalar(deg[:, 1, :], deg[:, 0, :], 1.0, None, ALU.add))
            c.done(dve.tensor_scalar(vare[:], mv[:, :, 1], LN_EPS, None, ALU.add))
            dve.sem_inc(S("deg_ready"), 1)
            dve.wait_ge(S("dis"), 3)
            c.done(dve.tensor_tensor(rstd[:], rstd[:], dis[:, 0, :], ALU.mult))
            for q in range(NB):
                for u in range(UB):
                    T = q * UB + u
                    ins = dve.tensor_scalar(R[:, T, :], R[:, T, :], mv[:, T, 0:1], rstd[:, T:T + 1], ALU.subtract, ALU.mult)
                    if u < UB - 1:
                        ins.then_inc(S("dve_load"), 1)
                        c.n += 1
                ins.then_inc(S("x_scaled0"), 1)

            def split_x(p, src):
                for q in range(NB):
                    dve.wait_ge(S(f"xhi{p}"), q + 1)
                    dve.tensor_tensor(Xlo[:, UB * q:UB * q + UB, :], src[:, UB * q:UB * q + UB, :],
                                      Xhi[:, UB * q:UB * q + UB, :].bitcast(F32), ALU.subtract).then_inc(S(f"xlo{p}"), 1)

            def split_w(p):
                dve.wait_ge(S("whi"), p + 1)
                dve.tensor_tensor(Wlo[:], Wraw[:], Whi[:].bitcast(F32), ALU.subtract).then_inc(S("wg_split"), 1)

            def gnn(p):
                l = p - 1

                def steps(ib, mid=None):
                    for j in range(NT):
                        dve.wait_ge(S(f"ahi{p}"), NT * ib + j + 1)
                        src = strm[(j // SJ) % SG][:, j % SJ, :] if p == 2 else \
                            AT[:, j, ds(ib * WIDE, WIDE)]
                        dve.tensor_tensor(Alo[:, j % 2, :], src, Ahi[:, j % 2, :].bitcast(F32),
                                          ALU.subtract).then_inc(S(f"alo{p}"), 1)
                        if mid is not None:
                            mid(j)

                def split_g(ib):
                    for d in range(KD):
                        dve.wait_ge(S(f"ghi{p}"), KD * ib + d + 1)
                        dve.tensor_tensor(Glo[:, d, :], PS[:, ds((ib % 2) * KD + d, 1), :].rearrange("p a n -> p (a n)"),
                                          Ghi[:, d, :].bitcast(F32), ALU.subtract).then_inc(S(f"glo{p}"), 1)

                def project(ib, u):
                    T = UB * ib + u
                    dve.wait_ge(S(f"u_done{p}"), T + 2)
                    dve.wait_ge(S(f"res{p}"), T + 1)
                    up = PS[:, U_PS[u % 2], 0:D]
                    if p < 2:
                        tile = R[:, ds(T, 1), :].rearrange("p a d -> p (a d)")
                        if p == 1 and u == 0:
                            dve.wait_ge(S("x_again"), 16)
                        ins = dve.scalar_tensor_tensor(tile, up, dis[:, 0, ds(T, 1)], tile if p else bgcn_bc[:, 0, :],
                                                       ALU.mult, ALU.add)
                    else:
                        ins = dve.tensor_scalar(U_sb[:, u % 2, :], up, dis[:, 1, ds(T, 1)], 0.0, ALU.mult, ALU.max)
                    ins.then_inc(S(f"u_sb{p}"), 1)

                def tile_stats(ib, u):
                    T = UB * ib + u
                    dve.wait_ge(S(f"res{p}"), T + 3)
                    norm_stats(R[:, ds(T, 1), :].rearrange("p a d -> p (a d)"), u, S(f"gstat{p}"), 2 * T)

                def block_var(ib):
                    dve.tensor_scalar(vare[:, ds(UB * ib, UB)], mvb[:, :, 1], LN_EPS, None,
                                      ALU.add).then_inc(S(f"vare{l}"), 1)

                def normalise(ib):
                    dve.wait_ge(S(f"rstd{l}"), ib + 1)
                    for u in range(UB):
                        ins = dve.tensor_scalar(xnb[:, u, :], R[:, ds(UB * ib + u, 1), :].rearrange("p a d -> p (a d)"),
                                                mvb[:, u, 0:1], rstd[:, ds(UB * ib + u, 1)],
                                                ALU.subtract, ALU.mult)
                    ins.then_inc(S(f"xn_out_ready{l}"), 1)

                def logits(ib):
                    E = EXPERTS[l]
                    dve.wait_ge(S(f"lg_psum{l}"), ib + 1)
                    src = PS[:, LG_PS, 0:UB * E].rearrange("p (u e) -> p u e", u=UB)
                    dst = L[:, ds(UB * ib, UB), 0:E]
                    if l == 0:
                        ins = dve.tensor_tensor(dst, src, bg_bc[:, 0:E].unsqueeze(1).to_broadcast([P, UB, E]), ALU.add)
                    else:
                        ins = dve.tensor_copy(dst, src)
                    ins.then_inc(S(f"lg{l}"), 1)

                def after(ib):
                    def mid(j):
                        if j == 1:
                            split_g(ib)
                        if p == 0:
                            if j in (5, 7, 9, 11):
                                project(ib, (j - 5) // 2)
                            return
                        if 5 <= j < 9:
                            project(ib, j - 5)
                        if 7 <= j < 11:
                            tile_stats(ib, j - 7)
                        if j == 10:
                            block_var(ib)
                        if j == 11:
                            normalise(ib)
                        if j == NT - 1:
                            logits(ib)
                    return mid

                steps(0)
                with dve.Fori(1, NB) as ib:
                    steps(ib, after(ib - 1))
                end = after(NB - 1)
                for j in range(NT):
                    end(j)

            def router(l):
                E, T = EXPERTS[l], TILES[l]
                c = Chain(dve, S(f"route{l}"))
                op = c.done
                Lg, L2g, ohg = L[:, :, 0:E], L2[:, :, 0:E], [o[:, :, 0:E] for o in oh]
                rtg, exg = rt[:, :, 0:E], ex[:, :, 0:E]
                first_of = dec[:, EMAX - E:EMAX].unsqueeze(1).to_broadcast([P, NT, E])
                dve.wait_ge(S(f"lg{l}"), NB + 1)

                for k, src in ((0, Lg), (1, L2g)):
                    if k:
                        op(dve.scalar_tensor_tensor(L2g, ohg[0], LOWEST, Lg, ALU.mult, ALU.add))
                    op(dve.tensor_reduce(mx[k][:], src, AX.X, ALU.max))
                    op(dve.tensor_tensor(ohg[k], src, per_token(mx[k][:], E), ALU.is_equal))
                    op(dve.tensor_tensor(rtg, ohg[k], first_of, ALU.mult))
                    op(dve.tensor_reduce(pick[:], rtg, AX.X, ALU.max))
                    op(dve.tensor_tensor(ohg[k], rtg, per_token(pick[:], E), ALU.is_equal))
                Mg = M[:, 0:E, :].rearrange("p e t -> p t e")
                dve.tensor_tensor(Mg, ohg[0], ohg[1], ALU.add).then_inc(S(f"m_ready{l}"), 1)
                op(dve.tensor_tensor(rtg, Lg, per_token(mx[0][:], E), ALU.subtract))
                dve.tensor_tensor(pick[:], mx[1][:], mx[0][:], ALU.subtract).then_inc(S(f"exp_in{l}"), 1)
                dve.wait_ge(S(f"rank{l}"), 1)
                inc2 = incl[:, 0:E, :].rearrange("p e t -> p (e t)")
                op(dve.tensor_tensor_scan(inc2, keep[:, 0:E, :].rearrange("p e t -> p (e t)"), PS[:, TOT_PS, 0:E * NT],
                                          0.0, ALU.mult, ALU.add))
                op(dve.tensor_tensor(more[:, 0:E, :], incl[:, 0:E, NT - 1:NT].to_broadcast([P, E, NT]),
                                     thr[:].unsqueeze(1).to_broadcast([P, E, NT]), ALU.is_gt))
                op(dve.tensor_reduce(tiles_e[:, 0:E], more[:, 0:E, :], AX.X, ALU.add))
                op(dve.tensor_tensor_scan(tend[:, 0:E], ones[:, 0:E], tiles_e[:, 0:E], 0.0, ALU.mult, ALU.add))
                op(dve.tensor_tensor(tstart[:, 0:E], tend[:, 0:E], tiles_e[:, 0:E], ALU.subtract))
                op(dve.tensor_tensor(more[:, 0:E, :].rearrange("p e t -> p (e t)"), PS[:, RANK_PS, 0:E * NT], inc2, ALU.add))
                op(dve.scalar_tensor_tensor(incl[:, 0:E, :], tstart[:, 0:E].unsqueeze(2).to_broadcast([P, E, NT]), float(P),
                                            more[:, 0:E, :], ALU.mult, ALU.add))
                slot_of = incl[:, 0:E, :].rearrange("p e t -> p t e")
                for k in range(2):
                    op(dve.tensor_tensor(L2g, ohg[k], slot_of, ALU.mult))
                    op(dve.tensor_reduce(pos[:, k, :], L2g, AX.X, ALU.add))
                op(dve.tensor_copy(pos_i[:], pos[:]))
                op(dve.tensor_scalar(rt_i[:, 0, :, :], pos_i[:], P - 1, None, ALU.bitwise_and))
                op(dve.tensor_scalar(rt_i[:, 1, :, :], pos_i[:], 7, None, ALU.logical_shift_right))
                op(dve.tensor_copy(rt_f[:], rt_i[:]))
                for k, (B, A) in enumerate(((Brow, Arhs), (Brow2, Arhs2))):
                    op(dve.tensor_tensor(B[:], iota[:].unsqueeze(1).to_broadcast([P, NT, P]),
                                         per_token(rt_f[:, 0, k, :], P), ALU.is_equal))
                    op(dve.tensor_tensor(Acol[:, :, 0:T], iota[:, 0:T].unsqueeze(1).to_broadcast([P, NT, T]),
                                         per_token(rt_f[:, 1, k, :], T), ALU.is_equal))
                    op(dve.tensor_tensor(A[:, :, 0, 0:T], Acol[:, :, 0:T], per_token(code[:, k, :], T), ALU.mult))
                    ins = dve.tensor_scalar(A[:, :, 1, 0:T], Acol[:, :, 0:T], pid[:, 0:1], None, ALU.mult)
                    op(ins)
                    dve.sem_inc(S(f"inv_in{l}"), 1)

                tt = iota[0:1, 0:T].unsqueeze(2).to_broadcast([1, T, E])
                op(dve.tensor_tensor(tcmp[:, 0:T, 0:E], tend[0:1, 0:E].unsqueeze(1).to_broadcast([1, T, E]), tt, ALU.is_le))
                op(dve.tensor_reduce(tsum[:, 0, 0:T], tcmp[:, 0:T, 0:E], AX.X, ALU.add))
                op(dve.tensor_scalar(tsum[:, 0, 0:T], tsum[:, 0, 0:T], float(E - 1), None, ALU.min))
                op(dve.tensor_tensor(tcmp[:, 0:T, 0:E - 1], tstart[0:1, 0:E - 1].unsqueeze(1).to_broadcast([1, T, E - 1]),
                                     iota[0:1, 0:T].unsqueeze(2).to_broadcast([1, T, E - 1]), ALU.is_equal))
                op(dve.tensor_reduce(tsum[:, 1, 0:T], tcmp[:, 0:T, 0:E - 1], AX.X, ALU.add))
                op(dve.tensor_copy(table[:, :, 0:T], tsum[:, :, 0:T]))

                dve.wait_ge(S(f"exp_out{l}"), 2)
                op(dve.tensor_reduce(zsum[:], exg, AX.X, ALU.add))
                op(dve.reciprocal(zrec[:], zsum[:]))
                op(dve.tensor_copy(gate[:, 0, :], zrec[:]))
                op(dve.tensor_tensor(gate[:, 1, :], e2[:], zrec[:], ALU.mult))
                if l == 1:
                    op(dve.tensor_tensor(gsum[:], gate[:, 0, :], gate[:, 1, :], ALU.add))
                    op(dve.tensor_scalar(gsum[:], gsum[:], 1e-6, None, ALU.add))
                    op(dve.reciprocal(zrec[:], gsum[:]))
                    op(dve.tensor_tensor(gate[:], gate[:], zrec[:].unsqueeze(1).to_broadcast([P, 2, NT]), ALU.mult))

                dve.wait_ge(S(f"inv_out{l}"), 1)
                op(dve.tensor_copy(F_sb[:, :, 0:T], PS[:, SLOT_PS, 0:2 * T].rearrange("p (a t) -> p a t", a=2)))
                op(dve.scalar_tensor_tensor(sl[:, 0, 0:T], F_sb[:, 0, 0:T], float(P), F_sb[:, 1, 0:T], ALU.mult, ALU.add))
                op(dve.tensor_scalar(sl[:, 1, 0:T], F_sb[:, 0, 0:T], 0.0, 4.0 * N, ALU.is_equal, ALU.mult))
                op(dve.scalar_tensor_tensor(idx[:, 1, 0:T], sl[:, 0, 0:T], float(-P), sl[:, 1, 0:T], ALU.add, ALU.add))
                op(dve.tensor_scalar(sl[:, 2, 0:T], F_sb[:, 0, 0:T], NT + 0.5, -float(N), ALU.is_gt, ALU.mult))
                op(dve.scalar_tensor_tensor(sl[:, 3, 0:T], sl[:, 0, 0:T], float(-P), sl[:, 2, 0:T], ALU.add, ALU.add))
                op(dve.tensor_scalar(idx[:, 0, 0:T], sl[:, 3, 0:T], 0.0, None, ALU.max))
                dve.sem_inc(S(f"routed{l}"), 1)

            def experts(l):
                E, T = EXPERTS[l], TILES[l]

                def split1(e, k, slot):
                    hi = w1hi[:, slot, k, :]
                    dve.tensor_tensor(w1lo[:, slot, k, :], raw1[:, k, :], hi.bitcast(F32), ALU.subtract).then_inc(S(f"w1_split{l}"), 1)

                def split1_dyn(e, k):
                    dve.wait_ge(S(f"w1_hi{l}"), KD * (e + 1) + k + 1)
                    dve.tensor_tensor(w1lo[:, ds((e + 1) % 2, 1), k, :].rearrange("p a h -> p (a h)"), raw1[:, k, :],
                                      w1hi[:, ds((e + 1) % 2, 1), k, :].rearrange("p a h -> p (a h)").bitcast(F32),
                                      ALU.subtract).then_inc(S(f"w1_split{l}"), 1)

                def split2_dyn(e, q):
                    dve.wait_ge(S(f"w2_hi{l}"), 2 * (e + 1) + q + 1)
                    dve.tensor_tensor(w2lo[:, ds((e + 1) % 2, 1), 4 * q:4 * q + 4, :].rearrange("p a c d -> p (a c) d"),
                                      raw2[:, 4 * q:4 * q + 4, :],
                                      w2hi[:, ds((e + 1) % 2, 1), 4 * q:4 * q + 4, :].rearrange("p a c d -> p (a c) d").bitcast(F32),
                                      ALU.subtract).then_inc(S(f"w2_split{l}"), 1)

                def x_lo(t):
                    dve.wait_ge(S(f"x_hi{l}"), t + 1)
                    dve.tensor_tensor(xTlo[:], PS[:, XG_PS, 0:KD * P].rearrange("p (k t) -> p k t", k=KD),
                                      xThi[:].bitcast(F32), ALU.subtract).then_inc(S(f"x_lo{l}"), 1)

                def add_b2(t, slot, first=False):
                    dve.wait_ge(S(f"y_done{l}"), t + 1)
                    if not first:
                        dve.wait_ge(S(f"y_out{l}"), 16 * t)
                    dve.tensor_tensor(y_sb[:], PS[:, Y_PS, 0:D], b2_bc[:, ds(slot, 1), :].rearrange("p a d -> p (a d)"),
                                      ALU.add).then_inc(S(f"y_ready{l}"), 1)

                def tile(t, first=False, second=False, last=False):
                    if first:
                        e = 0
                    else:
                        e = dve.value_load(table[0:1, 0, ds(t, 1)], min_val=0, max_val=E - 1)
                        e_before = dve.value_load(table[0:1, 0, ds(t - 1, 1)], min_val=0, max_val=E - 1)
                        opens = dve.value_load(table[0:1, 1, ds(t, 1)], min_val=0, max_val=1)
                    for b in range(HB):
                        dve.wait_ge(S(f"h_done{l}"), HB * t + b + 1)
                        bias = b1_bc[:, ds(e % 4, 1), b * BANK:(b + 1) * BANK].rearrange("p a h -> p (a h)")
                        dve.tensor_tensor(hrow[:, b * BANK:(b + 1) * BANK], PS[:, H_PS[b], :], bias,
                                          ALU.add).then_inc(S(f"h_biased{l}"), 1)
                    if not last:
                        x_lo(t + 1)
                    if first:
                        for k in range(KD):
                            split1_dyn(0, k)
                    else:
                        with dve.If(opens == 1):
                            for k in range(KD):
                                split1_dyn(e, k)
                        add_b2(t - 1, e_before % 4, first=second)
                    for b in range(HB):
                        dve.wait_ge(S(f"h_hi{l}"), HB * t + b + 1)
                        dve.tensor_tensor(hTlo[:, b * HCB:(b + 1) * HCB, :],
                                          PS[:, HT_PS[b], :].rearrange("p (c t) -> p c t", c=HCB),
                                          hThi[:, b * HCB:(b + 1) * HCB, :].bitcast(F32),
                                          ALU.subtract).then_inc(S(f"h_lo{l}"), 1)
                    if first:
                        for q in range(2):
                            split2_dyn(0, q)
                    else:
                        with dve.If(opens == 1):
                            for q in range(2):
                                split2_dyn(e, q)
                        dve.nop()
                    return e

                for k in range(KD):
                    dve.wait_ge(S(f"w1_hi{l}"), k + 1)
                    split1(0, k, 0)
                for q in range(2):
                    dve.wait_ge(S(f"w2_hi{l}"), q + 1)
                    dve.tensor_tensor(w2lo[:, 0, 4 * q:4 * q + 4, :], raw2[:, 4 * q:4 * q + 4, :],
                                      w2hi[:, 0, 4 * q:4 * q + 4, :].bitcast(F32), ALU.subtract).then_inc(S(f"w2_split{l}"), 1)
                x_lo(0)
                tile(0, first=True)
                tile(1, second=True)
                with dve.Fori(2, T - 1) as t:
                    tile(t)
                e = tile(T - 1, last=True)
                add_b2(T - 1, e % 4)

            def combine0():
                c = Chain(dve, S("cmb0"))
                dve.wait_ge(S("xn_in"), 48)
                for q in range(NB):
                    dve.wait_ge(S("yc_in0"), 32 * (q + 1))
                    for u in range(UB):
                        T = q * UB + u
                        c.done(dve.scalar_tensor_tensor(XN[:, T, :], Yc[:, u, 0, :], gate[:, 0, T:T + 1], XN[:, T, :], ALU.mult, ALU.add))
                        c.done(dve.scalar_tensor_tensor(XN[:, T, :], Yc[:, u, 1, :], gate[:, 1, T:T + 1], XN[:, T, :], ALU.mult, ALU.add))
                        c.done(dve.bn_stats(stats[:, u, :], XN[:, T, :]))
                        c.done(dve.bn_aggr(mv[:, T, :], stats[:, u, :]))
                    dve.sem_inc(S("yc_read0"), 1)
                c.done(dve.tensor_scalar(vare[:], mv[:, :, 1], LN_EPS, None, ALU.add))
                dve.sem_inc(S("cmb_vare"), 1)
                dve.wait_ge(S("cmb_rstd"), 1)
                for q in range(NB):
                    sl4 = slice(q * UB, (q + 1) * UB)
                    for u in range(UB):
                        T = q * UB + u
                        c.done(dve.tensor_scalar(XN[:, T, :], XN[:, T, :], mv[:, T, 0:1], rstd[:, T:T + 1], ALU.subtract, ALU.mult))
                    bc4 = lambda n: gb_bc[:, n, :].unsqueeze(1).to_broadcast([P, UB, D])
                    c.done(dve.tensor_tensor(XN[:, sl4, :], XN[:, sl4, :], bc4(0), ALU.mult))
                    c.done(dve.tensor_tensor(XN[:, sl4, :], XN[:, sl4, :], bc4(1), ALU.add))
                    c.done(dve.tensor_tensor(R[:, sl4, :], XN[:, sl4, :], R[:, sl4, :], ALU.add))
                    for u in range(UB):
                        T = q * UB + u
                        c.done(dve.bn_stats(stats[:, u, :], R[:, T, :]))
                        c.done(dve.bn_aggr(mv[:, T, :], stats[:, u, :]))
                c.done(dve.tensor_scalar(vare[:], mv[:, :, 1], LN_EPS, None, ALU.add))
                dve.sem_inc(S("cmb_vare"), 1)
                dve.wait_ge(S("cmb_rstd"), 2)
                c.done(dve.tensor_tensor(rstd[:], rstd[:], dis[:, 1, :], ALU.mult))
                for q in range(NB):
                    for u in range(UB):
                        T = q * UB + u
                        c.done(dve.tensor_scalar(XN[:, T, :], R[:, T, :], mv[:, T, 0:1], rstd[:, T:T + 1], ALU.subtract, ALU.mult))
                    dve.sem_inc(S("x_scaled2"), 1)

            def combine1():
                c = Chain(dve, S("cmb1"))
                for q in range(NB):
                    dve.wait_ge(S("yc_in1"), 32 * (q + 1))
                    for u in range(UB):
                        T = q * UB + u
                        for k in range(2):
                            c.done(dve.scalar_tensor_tensor(R[:, T, :], Yc[:, u, k, :], gate[:, k, T:T + 1], R[:, T, :], ALU.mult, ALU.add))
                    dve.sem_inc(S("yc_read1"), 1)
                    dve.sem_inc(S("final"), 1)

            dve.wait_ge(S("const_in"), 16 * 5)
            split_x(0, R)
            split_w(0)
            gnn(0)
            dve.wait_ge(S("res0"), NT + 2)
            for q in range(NB):
                dve.sem_inc(S("x_scaled1"), 1)
            split_x(1, R)
            split_w(1)
            gnn(1)
            router(0)
            experts(0)
            combine0()
            split_x(2, XN)
            split_w(2)
            gnn(2)
            router(1)
            experts(1)
            combine1()

        @block.tensor
        def _(pe):
            pe.wait_ge(S("consts"), 1)
            for l in range(2):
                pe.sem_inc(S(f"lg{l}"), 1)
            for p in range(3):
                pe.sem_inc(S(f"a_free{p}"), 2)
                pe.sem_inc(S(f"u_done{p}"), 1)
                pe.sem_inc(S(f"u_sb{p}"), 2)
                pe.sem_inc(S(f"res{p}"), 2)

            def transposes(i, u, first):
                pe.wait_ge(S(f"stage_in{u}"), 16 * (i + 1))
                r = i * STG + u
                for q in range(4):
                    if not first:
                        pe.wait_ge(S("at_copied"), 4 * r + q - 3)
                    for k in range(4):
                        j = 4 * q + k
                        ins = pe.transpose(PS[:, 4 + q, k * P:(k + 1) * P], stage[u][:, j * P:(j + 1) * P], ident)
                    ins.then_inc(S("at_psum"), 1)

            def rows(i, first):
                for u in range(STG):
                    transposes(i, u, first and u == 0)

            rows(0, True)
            with pe.Fori(1, NT // STG) as i:
                rows(i, False)

            def gnn(p):
                l = p - 1

                def steps(ib, mid=None):
                    for j in range(NT):
                        pe.wait_ge(S(f"alo{p}"), NT * ib + j + 1)
                        for d in range(KD):
                            g = PS[:, ds((ib % 2) * KD + d, 1), :].rearrange("p a n -> p (a n)")
                            dd = slice(d * P, (d + 1) * P)
                            pe.matmul(g, Xhi[:, j, dd], Ahi[:, j % 2, :], start=(j == 0), stop=False)
                            pe.matmul(g, Xhi[:, j, dd], Alo[:, j % 2, :], start=False, stop=False)
                            ins = pe.matmul(g, Xlo[:, j, dd], Ahi[:, j % 2, :], start=False, stop=(j == NT - 1))
                        ins.then_inc(S(f"a_free{p}"), 1)
                        if mid is not None:
                            mid(j)

                def project(ib, u):
                    T = UB * ib + u
                    if u == 0:
                        pe.wait_ge(S(f"glo{p}"), KD * (ib + 1))
                    pe.wait_ge(S(f"u_sb{p}"), T + 1)
                    up = PS[:, U_PS[u % 2], 0:D]
                    tt = slice(u * P, (u + 1) * P)
                    for d in range(KD):
                        pe.matmul(up, Ghi[:, d, tt], Whi[:, d, :], start=(d == 0), stop=False)
                        pe.matmul(up, Ghi[:, d, tt], Wlo[:, d, :], start=False, stop=False)
                        ins = pe.matmul(up, Glo[:, d, tt], Whi[:, d, :], start=False, stop=(d == KD - 1))
                    ins.then_inc(S(f"u_done{p}"), 1)

                def gate_x(ib):
                    pe.wait_ge(S(f"xn_out_ready{l}"), ib + 1)
                    for h in range(2):
                        for n in range(2):
                            for k in range(KD):
                                at = (n * KD + k) * P
                                ins = pe.transpose(PS[:, XT_PS[h], at:at + P], xnb[:, 2 * h + n, k * P:(k + 1) * P], ident)
                        ins.then_inc(S(f"xt_psum{l}"), 1)

                def gate_y(ib):
                    E = EXPERTS[l]
                    pe.wait_ge(S(f"xnT{l}"), 2 * ib + 2)
                    pe.wait_ge(S(f"lg{l}"), ib + 1)
                    for u in range(UB):
                        for k in range(KD):
                            at = ((u % 2) * KD + k) * P
                            ins = pe.matmul(PS[:, LG_PS, u * E:(u + 1) * E], xnT[:, u // 2, at:at + P], wgate[:, k, l, 0:E],
                                            start=(k == 0), stop=(k == KD - 1))
                    ins.then_inc(S(f"lg_psum{l}"), 1)

                def after(ib):
                    def mid(j):
                        if p == 0:
                            if j in (3, 5, 7, 9):
                                project(ib, (j - 3) // 2)
                            return
                        if 3 <= j < 7:
                            project(ib, j - 3)
                        if j == 12:
                            gate_x(ib)
                        if j == NT - 1:
                            gate_y(ib)
                    return mid

                pe.wait_ge(S(f"xlo{p}"), NB)
                pe.wait_ge(S("wg_split"), p + 1)
                steps(0)
                with pe.Fori(1, NB) as ib:
                    steps(ib, after(ib - 1))
                end = after(NB - 1)
                for j in range(NT):
                    end(j)

            def router(l):
                E, T = EXPERTS[l], TILES[l]
                Mg = M[:, 0:E, :].rearrange("p e t -> p (e t)")
                pe.wait_ge(S(f"m_ready{l}"), 1)
                pe.matmul(PS[:, RANK_PS, 0:E * NT], before[:], Mg, start=True, stop=True)
                pe.matmul(PS[:, TOT_PS, 0:E * NT], ones[:], Mg, start=True, stop=True).then_inc(S(f"rank{l}"), 1)
                for k, (B, A) in enumerate(((Brow, Arhs), (Brow2, Arhs2))):
                    pe.wait_ge(S(f"inv_in{l}"), k + 1)
                    for t in range(NT):
                        ins = pe.matmul(PS[:, SLOT_PS, 0:2 * T].rearrange("p (a t) -> p a t", a=2), B[:, t, :],
                                        A[:, t, :, 0:T], start=(k == 0 and t == 0), stop=(k == 1 and t == NT - 1))
                ins.then_inc(S(f"inv_out{l}"), 1)

            def experts(l):
                E, T = EXPERTS[l], TILES[l]

                def up(t, slot):
                    for b in range(HB):
                        cols = slice(b * BANK, (b + 1) * BANK)
                        for k in range(KD):
                            hi = w1hi[:, ds(slot, 1), k, cols].rearrange("p a h -> p (a h)")
                            lo = w1lo[:, ds(slot, 1), k, cols].rearrange("p a h -> p (a h)")
                            pe.matmul(PS[:, H_PS[b], :], xThi[:, k, :], hi, start=(k == 0), stop=False)
                            pe.matmul(PS[:, H_PS[b], :], xThi[:, k, :], lo, start=False, stop=False)
                            ins = pe.matmul(PS[:, H_PS[b], :], xTlo[:, k, :], hi, start=False, stop=(k == KD - 1))
                        ins.then_inc(S(f"h_done{l}"), 1)

                def x_t(t):
                    pe.wait_ge(S(f"xg_in{l}"), 16 * (t + 1))
                    for k in range(KD):
                        ins = pe.transpose(PS[:, XG_PS, k * P:(k + 1) * P], xg[:, k * P:(k + 1) * P], ident)
                    ins.then_inc(S(f"xt_done{l}"), 1)

                def h_t(t):
                    for b in range(HB):
                        pe.wait_ge(S(f"h_act{l}"), HB * t + b + 1)
                        for k in range(HCB):
                            cc = b * HCB + k
                            ins = pe.transpose(PS[:, HT_PS[b], k * P:(k + 1) * P], hrow[:, cc * P:(cc + 1) * P], ident)
                        ins.then_inc(S(f"ht_done{l}"), 1)

                def down(t, slot, first=False):
                    pe.wait_ge(S(f"h_lo{l}"), HB * (t + 1))
                    if not first:
                        pe.wait_ge(S(f"y_ready{l}"), t)
                    for k in range(HC):
                        hi = w2hi[:, ds(slot, 1), k, :].rearrange("p a h -> p (a h)")
                        lo = w2lo[:, ds(slot, 1), k, :].rearrange("p a h -> p (a h)")
                        yp = PS[:, Y_PS, 0:D]
                        pe.matmul(yp, hThi[:, k, :], hi, start=(k == 0), stop=False)
                        pe.matmul(yp, hThi[:, k, :], lo, start=False, stop=False)
                        ins = pe.matmul(yp, hTlo[:, k, :], hi, start=False, stop=(k == HC - 1))
                    ins.then_inc(S(f"y_done{l}"), 1)

                def tile(t, first=False, second=False, last=False):
                    if first:
                        e = 0
                    else:
                        e = pe.value_load(table[0:1, 0, ds(t, 1)], min_val=0, max_val=E - 1)
                        e_before = pe.value_load(table[0:1, 0, ds(t - 1, 1)], min_val=0, max_val=E - 1)
                    pe.wait_ge(S(f"x_lo{l}"), t + 1)
                    pe.wait_ge(S(f"w1_split{l}"), KD * (e + 1))
                    if not first:
                        pe.wait_ge(S(f"h_biased{l}"), HB * t)
                    up(t, e % 2)
                    if not last:
                        x_t(t + 1)
                    if not first:
                        pe.wait_ge(S(f"w2_split{l}"), 2 * (e_before + 1))
                        down(t - 1, e_before % 2, first=second)
                    h_t(t)
                    return e

                pe.wait_ge(S(f"routed{l}"), 1)
                x_t(0)
                tile(0, first=True)
                tile(1, second=True)
                with pe.Fori(2, T - 1) as t:
                    tile(t)
                e = tile(T - 1, last=True)
                pe.wait_ge(S(f"w2_split{l}"), 2 * (e + 1))
                down(T - 1, e % 2)

            gnn(0)
            gnn(1)
            router(0)
            experts(0)
            gnn(2)
            router(1)
            experts(1)


_INS = ['x', 'adj', 'L0_gnn_Wgcn1', 'L0_gnn_bgcn1', 'L0_gnn_Wgcn12', 'L0_gnn_bgcn12', 'L0_ffn_Wg', 'L0_ffn_bg',
        'L0_ffn_W1', 'L0_ffn_b1', 'L0_ffn_W2', 'L0_ffn_b2', 'L0_ffn_gamma', 'L0_ffn_beta', 'L1_gnn_W', 'L1_ffn_Wg',
        'L1_ffn_W1', 'L1_ffn_b1', 'L1_ffn_W2', 'L1_ffn_b2']


def kernel(**inputs):
    import numpy as _np
    import concourse.bacc as _bacc
    from concourse import mybir as _mybir
    from concourse.bass_utils import run_bass_kernel_spmd as _run

    nc = _bacc.Bacc("TRN2", target_bir_lowering=False, num_devices=1)
    arrays, args = {}, []
    for name in _INS:
        a = _np.ascontiguousarray(inputs[name])
        arrays[f"in_{name}_dram"] = a
        args.append(nc.dram_tensor(f"in_{name}_dram", a.shape, _mybir.dt.from_np(a.dtype), kind="ExternalInput").ap())
    out = nc.dram_tensor("out_0_dram", inputs["x"].shape, _mybir.dt.float32, kind="ExternalOutput").ap()
    moe_gnn_kernel(nc, *args, out)
    r = _run(nc, [arrays], core_ids=[0])
    return r.results[0]["out_0_dram"]
```

```python
from contextlib import ExitStack

import concourse.bass as bass
from concourse import mybir

F32 = mybir.dt.float32
F32R = mybir.dt.float32r
BF16 = mybir.dt.bfloat16
I32 = mybir.dt.int32
ALU = mybir.AluOpType
ACT = mybir.ActivationFunctionType
AX = mybir.AxisListType
ds = bass.ds

P = 128
BANK = 512
LN_EPS = 1e-5
LOWEST = -3.0e38


def moe_gnn_kernel(nc, x, adj, wgcn1, bgcn1, wgcn12, bgcn12, wg0, bg0, w1_0, b1_0, w2_0, b2_0, gamma, beta,
                   wgnn, wg1, w1_1, b1_1, w2_1, b2_1, out):
    N, D = x.shape
    KD = D // P
    NT = N // P
    WIDE = 512
    NB = N // WIDE
    UB = WIDE // P
    H = w1_0.shape[2]
    HC = H // P
    EXPERTS = [w1_0.shape[0], w1_1.shape[0]]
    EMAX = max(EXPERTS)
    TILES = [(2 * N + P * E - 1) // P for E in EXPERTS]
    SURE = [max(2 * N // P, E) for E in EXPERTS]
    COLS = [T + 2 for T in TILES]
    TMAX = max(COLS)
    WG, BG = [wg0, wg1], [bg0, None]
    W1, B1, W2, B2 = [w1_0, w1_1], [b1_0, b1_1], [w2_0, w2_1], [b2_0, b2_1]
    HB = H // BANK
    HCB = HC // HB

    adjT_d = nc.dram_tensor("adjT_d", [N, N], F32, kind="Internal").ap()
    xn_d = nc.dram_tensor("xn_d", [N, D], F32, kind="Internal").ap()
    y_d = [nc.dram_tensor(f"y{l}_d", [2 * N, D], F32, kind="Internal").ap() for l in range(2)]

    ctx = ExitStack()
    with ctx:
        base = ((nc.sbuf_base + 63) // 64) * 64
        top = [base]

        def sb(name, shape, dt, at=None):
            size = 1
            for s in shape[1:]:
                size *= s
            size *= 2 if dt == BF16 else 4
            off = top[0] if at is None else at
            t = nc.alloc_sbuf_tensor_at(name, shape, dt, offset=off)
            end = (off + size + 63) // 64 * 64
            if at is None:
                top[0] = end
            return t, end

        def lasting(name, shape, dt):
            return sb(name, shape, dt)[0]

        R = lasting("R", [P, NT, D], F32)
        ident = lasting("ident", [P, P], F32)[:]
        before = lasting("before", [P, P], BF16)
        ones = lasting("ones", [P, P], BF16)
        iota = lasting("iota", [P, P], BF16)
        pid = lasting("pid", [P, 1], F32)
        dec = lasting("dec", [P, EMAX], F32)
        keep = lasting("keep", [P, EMAX, NT], BF16)
        thr = lasting("thr", [P, NT], F32)
        code = lasting("code", [P, 2, NT], F32)
        half = lasting("half", [P, NT], F32)
        bgcn_bc = lasting("bgcn_bc", [P, 2, D], F32)
        bg_bc = lasting("bg_bc", [P, EMAX], F32)
        wgate = lasting("wgate", [P, KD, 2, EMAX], F32)
        dis = lasting("dis", [P, 2, NT], F32)
        deg = lasting("deg", [P, 2, NT], F32)
        stats = lasting("stats", [P, UB, 6], F32)
        mvb = lasting("mvb", [P, UB, 2], F32)
        mv = lasting("mv", [P, NT, 2], F32)
        vare = lasting("vare", [P, NT], F32)
        rstd = lasting("rstd", [P, NT], F32)
        L = lasting("L", [P, NT, EMAX], F32)
        gate = lasting("gate", [P, 2, NT], F32)
        table = lasting("table", [1, 3, TMAX], I32)
        last = lasting("last", [1, 2], I32)
        idx = lasting("idx", [P, 2, TMAX], I32)
        idx_use = lasting("idx_use", [P, 2], I32)
        shared = top[0]

        cur = [shared]

        def in_set(name, shape, dt):
            t, cur[0] = sb(name, shape, dt, at=cur[0])
            return t

        AT = in_set("AT", [P, NT, N], F32)
        Xhi = in_set("Xhi", [P, NT, D], F32R)
        Xlo = in_set("Xlo", [P, NT, D], F32R)
        RING = [2, 2, 4]
        Ahi = in_set("Ahi", [P, 2, WIDE], F32R)
        Alo = in_set("Alo", [P, 2, WIDE], F32R)
        Ghi = in_set("Ghi", [P, KD, WIDE], F32R)
        Glo = in_set("Glo", [P, KD, WIDE], F32R)
        Whi = in_set("Whi", [P, KD, D], F32R)
        Wlo = in_set("Wlo", [P, KD, D], F32R)
        gnn_end = cur[0]
        STG = 4
        stage_off = shared + NT * N * 4
        stage = [sb(f"stage{u}", [P, N], F32, at=stage_off + u * N * 4)[0] for u in range(STG)]
        assert STG * N * 4 <= 2 * NT * D * 4
        cur[0] = gnn_end
        xnb = sb("xnb", [P, UB, D], F32, at=gnn_end - 2 * KD * D * 4 - 2 * KD * WIDE * 4)[0]
        xnT = in_set("xnT", [P, 2, BANK], F32)
        Wraw = sb("Wraw", [P, KD, D], F32, at=cur[0] - 2 * BANK * 4)[0]
        assert cur[0] <= nc.sbuf_usable_end, (cur[0], nc.sbuf_usable_end)
        cur[0] = gnn_end - 2 * KD * D * 4 - 2 * KD * WIDE * 4
        iota_i = in_set("iota_i", [P, P], I32)
        pid_i = in_set("pid_i", [P, 1], I32)
        dec_i = in_set("dec_i", [P, EMAX], I32)
        thr_i = in_set("thr_i", [P, NT], I32)
        code_i = in_set("code_i", [P, 2, NT], I32)

        cur[0] = shared
        raw1 = in_set("raw1", [P, KD, H], F32)
        raw2 = in_set("raw2", [P, HC, D], F32)
        XN = in_set("XN", [P, NT, D], F32)
        w1hi = in_set("w1hi", [P, 2, KD, H], F32R)
        w1lo = in_set("w1lo", [P, 2, KD, H], F32R)
        w2hi = in_set("w2hi", [P, 2, HC, D], F32R)
        w2lo = in_set("w2lo", [P, 2, HC, D], F32R)
        hThi = in_set("hThi", [P, HC, P], F32R)
        hTlo = in_set("hTlo", [P, HC, P], F32R)
        assert cur[0] <= shared + NT * N * 4
        cur[0] = shared + NT * N * 4
        b1_bc = in_set("b1_bc", [P, 4, H], F32)
        b2_bc = in_set("b2_bc", [P, 4, D], F32)
        hrow = in_set("hrow", [P, H], F32)
        xg = in_set("xg", [P, D], F32)
        xThi = in_set("xThi", [P, KD, P], F32R)
        xTlo = in_set("xTlo", [P, KD, P], F32R)
        y_sb = in_set("y_sb", [P, D], F32)
        gb_bc = in_set("gb_bc", [P, 2, D], F32)
        assert cur[0] <= gnn_end
        cur[0] = shared + NT * N * 4
        oh = [in_set(f"oh{k}", [P, NT, EMAX], F32) for k in range(2)]
        L2 = in_set("L2", [P, NT, EMAX], F32)
        rt = in_set("rt", [P, NT, EMAX], F32)
        ex = in_set("ex", [P, NT, EMAX], F32)
        mx = [in_set(f"mx{k}", [P, NT], F32) for k in range(2)]
        pick = in_set("pick", [P, NT], F32)
        zsum = in_set("zsum", [P, NT], F32)
        zrec = in_set("zrec", [P, NT], F32)
        e2 = in_set("e2", [P, NT], F32)
        gsum = in_set("gsum", [P, NT], F32)
        M = in_set("M", [P, EMAX, NT], BF16)
        incl = in_set("incl", [P, EMAX, NT], F32)
        more = in_set("more", [P, EMAX, NT], F32)
        tiles_e = in_set("tiles_e", [P, EMAX], F32)
        tend = in_set("tend", [P, EMAX], F32)
        tstart = in_set("tstart", [P, EMAX], F32)
        pos = in_set("pos", [P, 2, NT], F32)
        pos_i = in_set("pos_i", [P, 2, NT], I32)
        rt_i = in_set("rt_i", [P, 2, 2, NT], I32)
        rt_f = in_set("rt_f", [P, 2, 2, NT], F32)
        Brow = in_set("Brow", [P, NT, P], BF16)
        Acol = in_set("Acol", [P, NT, TMAX], BF16)
        Arhs = in_set("Arhs", [P, NT, 2, TMAX], BF16)
        Brow2 = in_set("Brow2", [P, NT, P], BF16)
        Arhs2 = in_set("Arhs2", [P, NT, 2, TMAX], BF16)
        F_sb = in_set("F_sb", [P, 2, TMAX], F32)
        sl = in_set("sl", [P, 4, TMAX], F32)
        tcmp = in_set("tcmp", [1, TMAX, EMAX], F32)
        tsum = in_set("tsum", [1, 3, TMAX], F32)
        assert cur[0] <= nc.sbuf_usable_end
        SG, SJ = 4, 2
        strm = [sb(f"strm{s}", [P, SJ, WIDE], F32, at=shared + s * SJ * WIDE * 4)[0] for s in range(SG)]
        assert SG * SJ * WIDE * 4 <= (KD * H + HC * D) * 4
        cur[0] = shared + (KD * H + HC * D) * 4 + NT * D * 4
        U_sb = in_set("U_sb", [P, 2, D], F32)
        Ahi2 = in_set("Ahi2", [P, RING[2], WIDE], F32R)
        Alo2 = in_set("Alo2", [P, RING[2], WIDE], F32R)
        Ahis, Alos = [Ahi, Ahi, Ahi2], [Alo, Alo, Alo2]
        Yc = in_set("Yc", [P, NB, 2, UB, D], F32)
        cscale = in_set("cscale", [P, NT], F32)
        cshift = in_set("cshift", [P, NT], F32)
        assert cur[0] <= shared + NT * N * 4
        loops = in_set("loops", [P, 2 * NB - 1, P], F32)

        PS = ctx.enter_context(nc.psum_tensor("PS", [P, 8, BANK], F32))
        U_PS, XT_PS, LG_PS = (4, 5), (6, 4), 7
        H_PS, HT_PS, XG_PS, Y_PS = (0, 1), (2, 3), 4, 5
        RANK_PS, TOT_PS, SLOT_PS = 4, 5, 6

        SPLIT_AT = [(0, 3, 10)] * 2 + [(3, 7, 11)]
        SPLIT_AT_DVE = [(0, 3, 11)] * 2 + [(3, 7, 11)]

        names = {}

        def S(name):
            if name not in names:
                names[name] = ctx.enter_context(nc.semaphore(name))
            return names[name]

        class Chain:

            def __init__(self, eng, sem, start=0):
                self.eng, self.sem, self.start, self.n = eng, sem, start, 0

            def done(self, ins):
                ins.then_inc(self.sem, 1)
                self.n += 1
                self.eng.wait_ge(self.sem, self.start + self.n)

        def step_apart(eng):
            eng.sem_inc(S("apart_pool" if eng is nc.gpsimd or "Gp" in type(eng).__name__ else "apart_dve"), 1)

        def per_token(ap, n):
            return ap.unsqueeze(2).to_broadcast([P, ap.shape[1], n])

        adjT_tiles = adjT_d.rearrange("(j p) i -> p j i", p=P)
        x_tiles = x.rearrange("(t p) d -> p t d", p=P)
        xn_tiles = xn_d.rearrange("(t p) d -> p t d", p=P)
        out_tiles = out.rearrange("(t p) d -> p t d", p=P)
        y_tiles = [y.rearrange("(k t p) d -> p t k d", p=P, k=2) for y in y_d]
        Wg = [wgcn1, wgcn12, wgnn]

        block = ctx.enter_context(nc.Block())

        @block.sync
        def _(sp):
            sp.dma_start(R[:], x_tiles).then_inc(S("x_in"), 16)

            for u in range(STG):
                sp.dma_start(stage[u][:], adj[u * P:(u + 1) * P, :]).then_inc(S(f"stage_in{u}"), 16)
            bc = lambda row, n: row.rearrange("(a n) -> a n", a=1).to_broadcast([P, n])
            sp.dma_start(bgcn_bc[:, 0, :], bc(bgcn1, D)).then_inc(S("const_in"), 16)
            sp.dma_start(bgcn_bc[:, 1, :], bc(bgcn12, D)).then_inc(S("const_in"), 16)
            sp.dma_start(bg_bc[:], bc(bg0, EXPERTS[0])).then_inc(S("const_in"), 16)
            for l in range(2):
                sp.dma_start(wgate[:, :, l, 0:EXPERTS[l]], WG[l].rearrange("(k p) e -> p k e", p=P)).then_inc(S("const_in"), 16)
            sp.dma_start(Wraw[:], Wg[0].rearrange("(k p) d -> p k d", p=P)).then_inc(S("wg_in"), 16)
            with sp.Fori(1, NT // STG) as i:
                for u in range(STG):
                    sp.wait_ge(S(f"stage_read{u}"), i)
                    sp.wait_ge(S("at_psum"), 4 * ((i - 1) * STG + u + 1))
                    sp.dma_start(stage[u][:], adj[ds((i * STG + u) * P, P), :]).then_inc(S(f"stage_in{u}"), 16)

            sp.wait_ge(S("at_copied"), 4 * NT)
            sp.dma_start(adjT_tiles, AT[:]).then_inc(S("at_out"), 16)

            sp.wait_ge(S("wg_split"), 1)
            sp.dma_start(Wraw[:], Wg[1].rearrange("(k p) d -> p k d", p=P)).then_inc(S("wg_in"), 16)
            sp.wait_ge(S("xlo1"), NB)
            sp.dma_start(R[:], x_tiles).then_inc(S("x_again"), 16)
            for l in range(2):
                sp.sem_inc(S(f"xn_out{l}"), 16)
            sp.wait_ge(S("xn_out_ready0"), 1)
            sp.dma_start(xn_tiles[:, 0:UB, :], xnb[:]).then_inc(S("xn_out0"), 16)
            with sp.Fori(1, NB) as ib:
                sp.wait_ge(S("xn_out_ready0"), ib + 1)
                sp.dma_start(xn_tiles[:, ds(ib * UB, UB), :], xnb[:]).then_inc(S("xn_out0"), 16)

            def expert_loads(l):
                E = EXPERTS[l]
                w1v = W1[l].rearrange("e (k p) h -> p e k h", p=P)
                w2v = W2[l].rearrange("e (c p) d -> p e c d", p=P)

                def load(e, slot):
                    sp.wait_ge(S(f"w1_split{l}"), KD * e)
                    sp.dma_start(raw1[:], w1v[:, ds(e, 1), :, :].rearrange("p a k h -> p (a k) h")).then_inc(S(f"w1_in{l}"), 16)
                    sp.dma_start(b1_bc[:, slot, :], B1[l][ds(e, 1), :].to_broadcast([P, H])).then_inc(S(f"w1_in{l}"), 16)
                    sp.wait_ge(S(f"w2_split{l}"), 2 * e)
                    sp.dma_start(raw2[:], w2v[:, ds(e, 1), :, :].rearrange("p a c d -> p (a c) d")).then_inc(S(f"w2_in{l}"), 16)
                    sp.dma_start(b2_bc[:, slot, :], B2[l][ds(e, 1), :].to_broadcast([P, D])).then_inc(S(f"w2_in{l}"), 16)

                sp.dma_start(raw1[:], w1v[:, 0, :, :]).then_inc(S(f"w1_in{l}"), 16)
                sp.dma_start(raw2[:], w2v[:, 0, :, :]).then_inc(S(f"w2_in{l}"), 16)
                sp.wait_ge(S(f"routed{l}"), 1)
                if l == 0:
                    sp.dma_start(gb_bc[:, 0, :], bc(gamma, D)).then_inc(S("gb_in"), 16)
                    sp.dma_start(gb_bc[:, 1, :], bc(beta, D)).then_inc(S("gb_in"), 16)
                sp.dma_start(b1_bc[:, 0, :], B1[l][0:1, :].to_broadcast([P, H])).then_inc(S(f"b_in{l}"), 16)
                sp.dma_start(b2_bc[:, 0, :], B2[l][0:1, :].to_broadcast([P, D])).then_inc(S(f"b_in{l}"), 16)
                for e in range(1, 4):
                    load(e, e)
                    if e == 1 and l == 0:
                        sp.dma_start(XN[:], xn_tiles).then_inc(S("xn_in"), 16)
                with sp.Fori(1, E // 4) as q:
                    for s in range(4):
                        load(q * 4 + s, s)

            sp.wait_ge(S("a_free1"), NT * NB + RING[1])
            sp.wait_ge(S("at_out"), 16)
            sp.wait_ge(S("xn_out0"), 16 * (NB + 1))
            expert_loads(0)

            def combine_loads(l):
                sp.wait_ge(S(f"y_all{l}"), 1)
                for q in range(NB):
                    for k in range(2):
                        sp.dma_start(Yc[:, q, k, :, :], y_tiles[l][:, q * UB:(q + 1) * UB, k, :]).then_inc(S(f"yc{q}_in"), 16)

            combine_loads(0)
            sp.wait_ge(S("wg_split"), 2)
            sp.dma_start(Wraw[:], Wg[2].rearrange("(k p) d -> p k d", p=P)).then_inc(S("wg_in"), 16)
            GPB = NT // SJ

            def stream(ib, q, s):
                sp.dma_start(strm[s][:], adjT_tiles[:, q * SG * SJ + s * SJ:q * SG * SJ + (s + 1) * SJ,
                                                    ds(ib * WIDE, WIDE)]).then_inc(S(f"strm_in{s}"), 16)

            for s in range(SG):
                stream(0, 0, s)
            for q in range(1, GPB // SG):
                for s in range(SG):
                    sp.wait_ge(S("alo2"), SJ * (SG * (q - 1) + s + 1))
                    stream(0, q, s)
            with sp.Fori(1, NB) as ib:
                for q in range(GPB // SG):
                    for s in range(SG):
                        sp.wait_ge(S("alo2"), ib * NT + SJ * (SG * (q - 1) + s + 1))
                        stream(ib, q, s)
                sp.wait_ge(S("xn_out_ready1"), ib)
                sp.dma_start(xn_tiles[:, ds((ib - 1) * UB, UB), :], xnb[:]).then_inc(S("xn_out1"), 16)
            sp.wait_ge(S("xn_out_ready1"), NB)
            sp.dma_start(xn_tiles[:, (NB - 1) * UB:, :], xnb[:]).then_inc(S("xn_out1"), 16)
            sp.wait_ge(S("a_free2"), NT * NB + RING[2])
            expert_loads(1)
            combine_loads(1)
            for q in range(NB):
                sp.wait_ge(S("final"), q + 1)
                sp.dma_start(out_tiles[:, q * UB:(q + 1) * UB, :], R[:, q * UB:(q + 1) * UB, :]).then_inc(S("out_done"), 16)
            sp.wait_ge(S("out_done"), 16 * NB)

        @block.gpsimd
        def _(pool):
            c = Chain(pool, S("pool_const"))
            c.done(pool.memset(ident, 0.0))
            c.done(pool.affine_select(out=ident, in_=ident, compare_op=ALU.not_equal, fill=1.0, base=0,
                                      pattern=[[-1, P]], channel_multiplier=1))
            c.done(pool.memset(half[:], -0.5))
            pool.sem_inc(S("consts"), 1)
            c.done(pool.memset(ones[:], 1.0))
            c.done(pool.memset(before[:], 0.0))
            c.done(pool.affine_select(out=before[:], in_=before[:], compare_op=ALU.is_gt, fill=-1.0, base=0,
                                      pattern=[[1, P]], channel_multiplier=-1))
            c.done(pool.memset(keep[:], 1.0))
            c.done(pool.affine_select(out=keep[:], in_=keep[:], compare_op=ALU.not_equal, fill=0.0, base=0,
                                      pattern=[[0, EMAX], [1, NT]], channel_multiplier=0))
            c.done(pool.iota(iota_i[:], pattern=[[1, P]], base=0, channel_multiplier=0))
            c.done(pool.iota(pid_i[:], pattern=[[0, 1]], base=0, channel_multiplier=1))
            c.done(pool.iota(dec_i[:], pattern=[[-1, EMAX]], base=EMAX, channel_multiplier=0))
            c.done(pool.iota(thr_i[:], pattern=[[P, NT]], base=0, channel_multiplier=0))
            c.done(pool.iota(code_i[:], pattern=[[NT, 2], [1, NT]], base=1, channel_multiplier=0))
            c.done(pool.tensor_copy(iota[:], iota_i[:]))
            c.done(pool.tensor_copy(pid[:], pid_i[:]))
            c.done(pool.tensor_copy(dec[:], dec_i[:]))
            c.done(pool.tensor_copy(thr[:], thr_i[:]))
            c.done(pool.tensor_copy(code[:], code_i[:]))
            c.done(pool.memset(thr[:, 0:1], -1.0))
            pool.sem_inc(S("consts"), 1)

            with pool.Fori(0, NT // STG) as i:
                pool.wait_ge(S("deg_ready"), i + 1)
                step_apart(pool)
                four = ds(i * STG, STG)
                for dst, src in ((dis[:, 0, four], deg[:, 0, four]), (dis[:, 1, four], deg[:, 1, four]),
                                 (rstd[:, four], vare[:, four])):
                    pool.tensor_tensor(dst, src, half[:, 0:STG], ALU.pow).then_inc(S("dis"), 1)

            def residual(p, l):

                def self_loop(ib, j):
                    q, s = divmod(j // SJ, SG)
                    if j % SJ == 0:
                        pool.wait_ge(S(f"strm_in{s}"), 16 * (ib * (NT // SJ // SG) + q + 1))
                    step_apart(pool)
                    part = strm[s][:, j % SJ, (j % UB) * P:(j % UB + 1) * P]
                    pool.tensor_tensor(part, part, loops[:, ds(ib + (NB - 1 - j // UB), 1), :].rearrange("p a n -> p (a n)"),
                                       ALU.add).then_inc(S("looped"), 1)

                def add(ib, u):
                    tile = R[:, ds(UB * ib + u, 1), :].rearrange("p a d -> p (a d)")
                    pool.wait_ge(S(f"u_sb{p}"), UB * ib + u + 3)
                    if p == 1:
                        pool.wait_ge(S("const_in"), 16 * 5)
                    step_apart(pool)
                    pool.tensor_tensor(tile, tile, bgcn_bc[:, 1, :] if p == 1 else U_sb[:, u % 2, :],
                                       ALU.add).then_inc(S(f"res{p}"), 1)

                def sigma(ib):
                    pool.wait_ge(S(f"vare{l}"), ib + 1)
                    step_apart(pool)
                    pool.tensor_tensor(rstd[:, ds(UB * ib, UB)], vare[:, ds(UB * ib, UB)], half[:, 0:UB],
                                       ALU.pow).then_inc(S(f"rstd{l}"), 1)

                def block_end(ib):
                    for u in range(UB):
                        add(ib, u)
                    sigma(ib)

                if p == 1:
                    with pool.Fori(0, NB) as ib:
                        block_end(ib)
                    return
                pool.memset(loops[:], 0.0).then_inc(S("loops"), 1)
                pool.wait_ge(S("loops"), 1)
                pool.tensor_copy(loops[:, NB - 1, :], ident).then_inc(S("loops"), 1)
                pool.wait_ge(S("loops"), 2)

                def weighted_sum(q):
                    pool.wait_ge(S("y_weighted"), q + 1)
                    pool.tensor_tensor(Yc[:, q, 0, :, :], Yc[:, q, 0, :, :], Yc[:, q, 1, :, :],
                                       ALU.add).then_inc(S("y_sum"), 1)

                def comb_sigma(n, q):
                    pool.wait_ge(S("cmb_vare"), n)
                    four = slice(q * UB, (q + 1) * UB)
                    pool.tensor_tensor(rstd[:, four], vare[:, four], half[:, 0:UB], ALU.pow).then_inc(S("cmb_rstd"), 1)

                weighted_sum(0)
                weighted_sum(1)
                comb_sigma(1, 0)
                weighted_sum(2)
                comb_sigma(2, 1)
                comb_sigma(3, 0)
                weighted_sum(3)
                comb_sigma(4, 2)
                comb_sigma(5, 1)
                for j in range(NT):
                    if j == 2:
                        comb_sigma(6, 3)
                        comb_sigma(7, 2)
                    if j == 6:
                        comb_sigma(8, 3)
                    self_loop(0, j)
                with pool.Fori(1, NB) as ib:
                    for j in range(NT):
                        self_loop(ib, j)
                        if 6 <= j < 6 + UB:
                            add(ib - 1, j - 6)
                        if j == 12:
                            sigma(ib - 1)
                block_end(NB - 1)

            def expert_moves(l):
                E, T = EXPERTS[l], TILES[l]

                def gather(t):
                    pool.tensor_copy(idx_use[:, 0:1], idx[:, 0, ds(t, 1)]).then_inc(S(f"idx_g{l}"), 1)
                    pool.wait_ge(S(f"idx_g{l}"), t + 1)
                    step_apart(pool)
                    pool.indirect_dma_start(xg[:], None, xn_d, bass.IndirectOffsetOnAxis(idx_use[:, 0:1], 0),
                                            bounds_check=N - 1, oob_is_err=True).then_inc(S(f"xg_in{l}"), 16)

                def next_gather(t):
                    pool.wait_ge(S(f"xg_in{l}"), 16 * (t + 2))
                    pool.wait_ge(S(f"xt_done{l}"), t + 2)
                    gather(t + 2)

                def scatter(t, first=False):
                    if not first:
                        pool.wait_ge(S(f"y_out{l}"), 16 * t)
                    pool.tensor_copy(idx_use[:, 1:2], idx[:, 1, ds(t, 1)]).then_inc(S(f"idx_s{l}"), 1)
                    pool.wait_ge(S(f"idx_s{l}"), t + 1)
                    pool.wait_ge(S(f"y_ready{l}"), t + 1)
                    step_apart(pool)
                    pool.indirect_dma_start(y_d[l], bass.IndirectOffsetOnAxis(idx_use[:, 1:2], 0), y_sb[:], None,
                                            bounds_check=2 * N - 1, oob_is_err=False).then_inc(S(f"y_out{l}"), 16)

                def split2_dyn(e, q):
                    slot = ds((e + 1) % 2, 1)
                    pool.wait_ge(S(f"w2_hi{l}"), 2 * (e + 1) + q + 1)
                    step_apart(pool)
                    pool.tensor_tensor(w2lo[:, slot, 4 * q:4 * q + 4, :].rearrange("p a c d -> p (a c) d"),
                                       raw2[:, 4 * q:4 * q + 4, :],
                                       w2hi[:, slot, 4 * q:4 * q + 4, :].rearrange("p a c d -> p (a c) d").bitcast(F32),
                                       ALU.subtract).then_inc(S(f"w2_split{l}"), 1)

                def tile(t, second=False):
                    if second:
                        next_gather(t)
                        split2_dyn(0, 0)
                        scatter(t - 1, first=True)
                        split2_dyn(0, 1)
                        return
                    e = pool.value_load(table[0:1, 0, ds(t - 1, 1)], min_val=0, max_val=E - 1)
                    opens = pool.value_load(table[0:1, 1, ds(t - 1, 1)], min_val=0, max_val=1)
                    next_gather(t)
                    with pool.If(opens == 1):
                        split2_dyn(e, 0)
                    scatter(t - 1)
                    with pool.If(opens == 1):
                        split2_dyn(e, 1)
                    pool.nop()

                for k in range(KD):
                    pool.wait_ge(S(f"w1_hi{l}"), k + 1)
                    pool.tensor_tensor(w1lo[:, 0, k, :], raw1[:, k, :], w1hi[:, 0, k, :].bitcast(F32),
                                       ALU.subtract).then_inc(S(f"w1_split{l}"), 1)
                for q in range(2):
                    four = slice(4 * q, 4 * q + 4)
                    pool.wait_ge(S(f"w2_hi{l}"), q + 1)
                    pool.tensor_tensor(w2lo[:, 0, four, :], raw2[:, four, :], w2hi[:, 0, four, :].bitcast(F32),
                                       ALU.subtract).then_inc(S(f"w2_split{l}"), 1)
                pool.wait_ge(S(f"routed{l}"), 1)
                pool.wait_ge(S(f"xn_out{l}"), 16 * (NB + 1))
                gather(0)
                pool.wait_ge(S(f"xg_in{l}"), 16)
                pool.wait_ge(S(f"xt_done{l}"), 1)
                gather(1)
                next_gather(0)
                tile(1, second=True)
                with pool.Fori(2, SURE[l]) as t:
                    tile(t)
                with pool.Fori(SURE[l], T) as t:
                    used = pool.value_load(table[0:1, 2, ds(t, 1)], min_val=0, max_val=1)
                    with pool.If(used == 1):
                        tile(t)
                    pool.nop()
                t = pool.value_load(last[0:1, l:l + 1], min_val=SURE[l] - 1, max_val=T - 1)
                scatter(t)
                pool.wait_ge(S(f"y_out{l}"), 16 * (t + 1))
                pool.wait_ge(S(f"xg_in{l}"), 16 * (t + 3))
                pool.sem_inc(S(f"y_all{l}"), 1)

            residual(1, 0)
            expert_moves(0)
            residual(2, 1)
            expert_moves(1)

        @block.scalar
        def _(act):
            with act.Fori(0, NT) as r:
                for q in range(4):
                    act.wait_ge(S("at_psum"), 4 * r + q + 1)
                    act.activation(AT[:, 4 * q:4 * q + 4, ds(r * P, P)],
                                   PS[:, 4 + q, :].rearrange("p (j i) -> p j i", j=4), ACT.Copy).then_inc(S("at_copied"), 1)

            def split_x(p, src, q):
                if p == 1:
                    act.wait_ge(S("res0"), UB * (q + 1) + 2)
                    act.wait_ge(S("a_free0"), NT * NB + RING[0])
                elif p == 0:
                    act.wait_ge(S("x_scaled0"), NB)
                else:
                    act.wait_ge(S("x_shift"), q + 1)
                    for u in range(UB):
                        T = q * UB + u
                        ins = act.activation(src[:, T, :], R[:, T, :], ACT.Identity, bias=cshift[:, T:T + 1],
                                             scale=cscale[:, T:T + 1])
                    ins.then_inc(S("x_scaled2"), 1)
                    act.wait_ge(S("x_scaled2"), q + 1)
                act.activation(Xhi[:, UB * q:UB * q + UB, :], src[:, UB * q:UB * q + UB, :],
                               ACT.Copy).then_inc(S(f"xhi{p}"), 1)

            def split_w(p):
                act.wait_ge(S("wg_in"), 16 * (p + 1))
                act.activation(Whi[:], Wraw[:], ACT.Copy).then_inc(S("whi"), 1)

            def gnn(p, mid_before=None):
                src_x = XN if p == 2 else R

                def steps(ib, mid=None):
                    for j in range(NT):
                        if p == 2:
                            act.wait_ge(S("looped"), NT * ib + j + 1)
                        if p == 1 and mid is first_mid and j < RING[0]:
                            act.wait_ge(S("a_free0"), NT * NB + j + 1)
                        act.wait_ge(S(f"a_free{p}"), NT * ib + j + 1)
                        src = strm[(j // SJ) % SG][:, j % SJ, :] if p == 2 else \
                            AT[:, j, ds(ib * WIDE, WIDE)]
                        act.activation(Ahis[p][:, j % RING[p], :], src, ACT.Copy).then_inc(S(f"ahi{p}"), 1)
                        if mid is not None:
                            mid(j)

                def split_g(ib, d):
                    if d == 0:
                        act.wait_ge(S(f"a_free{p}"), NT * (ib + 1) + RING[p])
                        act.wait_ge(S(f"u_done{p}"), UB * ib + 1)
                        if p > 0:
                            act.wait_ge(S(f"xn_out{p - 1}"), 16 * (ib + 1))
                    act.activation(Ghi[:, d, :], PS[:, ds((ib % 2) * KD + d, 1), :].rearrange("p a n -> p (a n)"),
                                   ACT.Copy).then_inc(S(f"ghi{p}"), 1)

                def relu(ib, u):
                    act.wait_ge(S(f"u_sb{p}"), UB * ib + u + 3)
                    tile = R[:, ds(UB * ib + u, 1), :].rearrange("p a d -> p (a d)")
                    act.activation(tile, tile, ACT.Relu,
                                   scale=dis[:, 0, ds(UB * ib + u, 1)]).then_inc(S(f"res{p}"), 1)

                def gate_in(l, ib, h):
                    act.wait_ge(S(f"xt_psum{l}"), 2 * ib + h + 1)
                    act.activation(xnT[:, h, :], PS[:, XT_PS[h], :], ACT.Copy).then_inc(S(f"xnT{l}"), 1)

                def after(ib):
                    def mid(j):
                        if 1 <= j <= KD:
                            split_g(ib, j - 1)
                        if p == 0 and 7 <= j < 7 + UB:
                            relu(ib, j - 7)
                        if p > 0 and j == NT - 1:
                            for h in range(2):
                                gate_in(p - 1, ib, h)
                    return mid

                def first_mid(j):
                    if mid_before is not None:
                        mid_before(j)
                    if j in SPLIT_AT[p]:
                        split_x(p, src_x, 1 + SPLIT_AT[p].index(j))
                    if j == NT - 3:
                        split_w(p)

                split_x(p, src_x, 0)
                steps(0, first_mid)
                with act.Fori(1, NB) as ib:
                    steps(ib, after(ib - 1))
                return after(NB - 1)

            def combine0():
                for q in range(NB):
                    act.wait_ge(S(f"yc{q}_in"), 32)
                    for k in range(2):
                        for u in range(UB):
                            part = Yc[:, q, k, u, :]
                            ins = act.activation(part, part, ACT.Copy, scale=gate[:, k, q * UB + u:q * UB + u + 1])
                    ins.then_inc(S("y_weighted"), 1)

            def first_expert(l):
                act.wait_ge(S(f"w1_in{l}"), 16)
                for k in range(KD):
                    act.activation(w1hi[:, 0, k, :], raw1[:, k, :], ACT.Copy).then_inc(S(f"w1_hi{l}"), 1)
                act.wait_ge(S(f"w2_in{l}"), 16)
                for q in range(2):
                    act.activation(w2hi[:, 0, 4 * q:4 * q + 4, :], raw2[:, 4 * q:4 * q + 4, :],
                                   ACT.Copy).then_inc(S(f"w2_hi{l}"), 1)

            def experts(l, func):
                E, T = EXPERTS[l], TILES[l]

                def split1_dyn(e, k):
                    act.wait_ge(S(f"w1_in{l}"), 32 * (e + 1) + 16)
                    act.activation(w1hi[:, ds((e + 1) % 2, 1), k, :].rearrange("p a h -> p (a h)"), raw1[:, k, :],
                                   ACT.Copy).then_inc(S(f"w1_hi{l}"), 1)

                def split2_dyn(e, q):
                    act.wait_ge(S(f"w2_in{l}"), 32 * (e + 1) + 16)
                    act.activation(w2hi[:, ds((e + 1) % 2, 1), 4 * q:4 * q + 4, :].rearrange("p a c d -> p (a c) d"),
                                   raw2[:, 4 * q:4 * q + 4, :], ACT.Copy).then_inc(S(f"w2_hi{l}"), 1)

                def x_hi(t):
                    act.wait_ge(S(f"xt_done{l}"), t + 1)
                    act.activation(xThi[:], PS[:, XG_PS, 0:KD * P].rearrange("p (k t) -> p k t", k=KD),
                                   ACT.Copy).then_inc(S(f"x_hi{l}"), 1)

                def tile(t, first=False):
                    if first:
                        e = 0
                    else:
                        e = act.value_load(table[0:1, 0, ds(t, 1)], min_val=0, max_val=E - 1)
                        opens = act.value_load(table[0:1, 1, ds(t, 1)], min_val=0, max_val=1)
                    for b in range(HB):
                        act.wait_ge(S(f"h_biased{l}"), HB * t + b + 1)
                        act.activation(hrow[:, b * BANK:(b + 1) * BANK], hrow[:, b * BANK:(b + 1) * BANK],
                                       func).then_inc(S(f"h_act{l}"), 1)
                    x_hi(t + 1)
                    if first:
                        split1_dyn(0, 0)
                    else:
                        with act.If(opens == 1):
                            split1_dyn(e, 0)
                    for b in range(HB):
                        act.wait_ge(S(f"ht_done{l}"), HB * t + b + 1)
                        act.activation(hThi[:, b * HCB:(b + 1) * HCB, :],
                                       PS[:, HT_PS[b], :].rearrange("p (c t) -> p c t", c=HCB),
                                       ACT.Copy).then_inc(S(f"h_hi{l}"), 1)
                    if first:
                        for k in range(1, KD):
                            split1_dyn(0, k)
                        for q in range(2):
                            split2_dyn(0, q)
                    else:
                        with act.If(opens == 1):
                            for k in range(1, KD):
                                split1_dyn(e, k)
                            act.wait_ge(S(f"y_done{l}"), t)
                            for q in range(2):
                                split2_dyn(e, q)
                        act.nop()

                x_hi(0)
                tile(0, first=True)
                with act.Fori(1, SURE[l]) as t:
                    tile(t)
                with act.Fori(SURE[l], T) as t:
                    used = act.value_load(table[0:1, 2, ds(t, 1)], min_val=0, max_val=1)
                    with act.If(used == 1):
                        tile(t)
                    act.nop()

            end = gnn(1, gnn(0))
            for j in range(NT):
                end(j)
            first_expert(0)
            act.wait_ge(S("exp_in0"), 1)
            act.activation(ex[:, :, 0:EXPERTS[0]], rt[:, :, 0:EXPERTS[0]], ACT.Exp).then_inc(S("exp_out0"), 1)
            act.activation(e2[:], pick[:], ACT.Exp).then_inc(S("exp_out0"), 1)
            experts(0, ACT.Relu)
            combine0()
            end = gnn(2)
            for j in range(NT):
                end(j)
            act.wait_ge(S("res2"), NT + 2)
            first_expert(1)
            act.wait_ge(S("exp_in1"), 1)
            act.activation(ex[:, :, 0:EXPERTS[1]], rt[:, :, 0:EXPERTS[1]], ACT.Exp).then_inc(S("exp_out1"), 1)
            act.activation(e2[:], pick[:], ACT.Exp).then_inc(S("exp_out1"), 1)
            experts(1, ACT.Gelu)

        @block.vector
        def _(dve):
            def norm_stats(src, u, sem, start):
                ch = Chain(dve, sem, start)
                step_apart(dve)
                ch.done(dve.bn_stats(stats[:, u, :], src))
                step_apart(dve)
                ch.done(dve.bn_aggr(mvb[:, u, :], stats[:, u, :]))

            dve.wait_ge(S("x_in"), 16)
            with dve.Fori(0, NT // STG) as i:
                turn = (2 * STG + 3) * i
                for u in range(STG):
                    T = i * STG + u
                    norm_stats(R[:, ds(T, 1), :].rearrange("p a d -> p (a d)"), u, S("stat0"), turn + 2 * u)
                    dve.wait_ge(S(f"stage_in{u}"), 16 * (i + 1))
                    dve.tensor_reduce(deg[:, 0, ds(T, 1)], stage[u][:], AX.X, ALU.add).then_inc(S(f"stage_read{u}"), 1)
                four = ds(i * STG, STG)
                ch = Chain(dve, S("stat0"), turn + 2 * STG)
                ch.done(dve.tensor_scalar(vare[:, four], mvb[:, :, 1], LN_EPS, None, ALU.add))
                for u in range(STG):
                    dve.wait_ge(S(f"stage_read{u}"), i + 1)
                ch.done(dve.tensor_scalar(deg[:, 1, four], deg[:, 0, four], 1.0, None, ALU.add))
                dve.sem_inc(S("deg_ready"), 1)
                dve.wait_ge(S("dis"), 3 * (i + 1))
                ch.done(dve.tensor_tensor(rstd[:, four], rstd[:, four], dis[:, 0, four], ALU.mult))
                for u in range(STG):
                    T = i * STG + u
                    tile = R[:, ds(T, 1), :].rearrange("p a d -> p (a d)")
                    ins = dve.tensor_scalar(tile, tile, mvb[:, u, 0:1], rstd[:, ds(T, 1)], ALU.subtract, ALU.mult)
                ins.then_inc(S("x_scaled0"), 1)
            dve.wait_ge(S("x_scaled0"), NB)

            def split_x(p, src, q):
                dve.wait_ge(S(f"xhi{p}"), q + 1)
                dve.tensor_tensor(Xlo[:, UB * q:UB * q + UB, :], src[:, UB * q:UB * q + UB, :],
                                  Xhi[:, UB * q:UB * q + UB, :].bitcast(F32), ALU.subtract).then_inc(S(f"xlo{p}"), 1)

            def split_w(p):
                dve.wait_ge(S("whi"), p + 1)
                dve.tensor_tensor(Wlo[:], Wraw[:], Whi[:].bitcast(F32), ALU.subtract).then_inc(S("wg_split"), 1)

            def gnn(p, mid_before=None):
                l = p - 1
                src_x = XN if p == 2 else R

                def steps(ib, mid=None):
                    for j in range(NT):
                        dve.wait_ge(S(f"ahi{p}"), NT * ib + j + 1)
                        src = strm[(j // SJ) % SG][:, j % SJ, :] if p == 2 else \
                            AT[:, j, ds(ib * WIDE, WIDE)]
                        dve.tensor_tensor(Alos[p][:, j % RING[p], :], src, Ahis[p][:, j % RING[p], :].bitcast(F32),
                                          ALU.subtract).then_inc(S(f"alo{p}"), 1)
                        if mid is not None:
                            mid(j)

                def split_g(ib, d):
                    dve.wait_ge(S(f"ghi{p}"), KD * ib + d + 1)
                    dve.tensor_tensor(Glo[:, d, :], PS[:, ds((ib % 2) * KD + d, 1), :].rearrange("p a n -> p (a n)"),
                                      Ghi[:, d, :].bitcast(F32), ALU.subtract).then_inc(S(f"glo{p}"), 1)

                def project(ib, u):
                    T = UB * ib + u
                    dve.wait_ge(S(f"u_done{p}"), T + 2)
                    dve.wait_ge(S(f"res{p}"), T + 1)
                    up = PS[:, U_PS[u % 2], 0:D]
                    if p < 2:
                        tile = R[:, ds(T, 1), :].rearrange("p a d -> p (a d)")
                        if p == 1 and u == 0:
                            dve.wait_ge(S("x_again"), 16)
                        ins = dve.scalar_tensor_tensor(tile, up, dis[:, 0, ds(T, 1)], tile if p else bgcn_bc[:, 0, :],
                                                       ALU.mult, ALU.add)
                    else:
                        ins = dve.tensor_scalar(U_sb[:, u % 2, :], up, dis[:, 1, ds(T, 1)], 0.0, ALU.mult, ALU.max)
                    ins.then_inc(S(f"u_sb{p}"), 1)

                def tile_stats(ib, u):
                    T = UB * ib + u
                    dve.wait_ge(S(f"res{p}"), T + 3)
                    norm_stats(R[:, ds(T, 1), :].rearrange("p a d -> p (a d)"), u, S(f"gstat{p}"), 2 * T)

                def block_var(ib):
                    dve.tensor_scalar(vare[:, ds(UB * ib, UB)], mvb[:, :, 1], LN_EPS, None,
                                      ALU.add).then_inc(S(f"vare{l}"), 1)

                def normalise(ib, h):
                    if h == 0:
                        dve.wait_ge(S(f"rstd{l}"), ib + 1)
                    for u in (2 * h, 2 * h + 1):
                        ins = dve.tensor_scalar(xnb[:, u, :], R[:, ds(UB * ib + u, 1), :].rearrange("p a d -> p (a d)"),
                                                mvb[:, u, 0:1], rstd[:, ds(UB * ib + u, 1)],
                                                ALU.subtract, ALU.mult)
                    if h == 1:
                        ins.then_inc(S(f"xn_out_ready{l}"), 1)

                def after(ib):
                    def mid(j):
                        if 2 <= j < 2 + KD:
                            split_g(ib, j - 2)
                        if 5 <= j < 5 + UB:
                            project(ib, j - 5)
                        if p == 0:
                            return
                        if 7 <= j < 7 + UB:
                            tile_stats(ib, j - 7)
                        if j == 11:
                            block_var(ib)
                        if j in (12, 13):
                            normalise(ib, j - 12)
                    return mid

                def first_mid(j):
                    if mid_before is not None:
                        mid_before(j)
                    if j in SPLIT_AT_DVE[p]:
                        split_x(p, src_x, 1 + SPLIT_AT_DVE[p].index(j))
                    if j == NT - 2:
                        split_w(p)

                split_x(p, src_x, 0)
                steps(0, first_mid)
                with dve.Fori(1, NB) as ib:
                    steps(ib, after(ib - 1))
                return after(NB - 1)

            def router(l):
                E, T = EXPERTS[l], COLS[l]
                c = Chain(dve, S(f"route{l}"))
                op = c.done
                Lg, L2g, ohg = L[:, :, 0:E], L2[:, :, 0:E], [o[:, :, 0:E] for o in oh]
                rtg, exg = rt[:, :, 0:E], ex[:, :, 0:E]
                first_of = dec[:, EMAX - E:EMAX].unsqueeze(1).to_broadcast([P, NT, E])
                dve.wait_ge(S(f"lg_psum{l}"), NB)
                logits = PS[:, LG_PS, 0:NT * E].rearrange("p (t e) -> p t e", t=NT)
                op(dve.tensor_tensor(Lg, logits, bg_bc[:, 0:E].unsqueeze(1).to_broadcast([P, NT, E]), ALU.add)
                   if l == 0 else dve.tensor_copy(Lg, logits))

                for k, src in ((0, Lg), (1, L2g)):
                    if k:
                        op(dve.scalar_tensor_tensor(L2g, ohg[0], LOWEST, Lg, ALU.mult, ALU.add))
                    op(dve.tensor_reduce(mx[k][:], src, AX.X, ALU.max))
                    op(dve.tensor_tensor(ohg[k], src, per_token(mx[k][:], E), ALU.is_equal))
                    op(dve.tensor_tensor(rtg, ohg[k], first_of, ALU.mult))
                    op(dve.tensor_reduce(pick[:], rtg, AX.X, ALU.max))
                    op(dve.tensor_tensor(ohg[k], rtg, per_token(pick[:], E), ALU.is_equal))
                Mg = M[:, 0:E, :].rearrange("p e t -> p t e")
                dve.tensor_tensor(Mg, ohg[0], ohg[1], ALU.add).then_inc(S(f"m_ready{l}"), 1)
                op(dve.tensor_tensor(rtg, Lg, per_token(mx[0][:], E), ALU.subtract))
                dve.tensor_tensor(pick[:], mx[1][:], mx[0][:], ALU.subtract).then_inc(S(f"exp_in{l}"), 1)
                dve.wait_ge(S(f"rank{l}"), 1)
                inc2 = incl[:, 0:E, :].rearrange("p e t -> p (e t)")
                op(dve.tensor_tensor_scan(inc2, keep[:, 0:E, :].rearrange("p e t -> p (e t)"), PS[:, TOT_PS, 0:E * NT],
                                          0.0, ALU.mult, ALU.add))
                op(dve.tensor_tensor(more[:, 0:E, :], incl[:, 0:E, NT - 1:NT].to_broadcast([P, E, NT]),
                                     thr[:].unsqueeze(1).to_broadcast([P, E, NT]), ALU.is_gt))
                op(dve.tensor_reduce(tiles_e[:, 0:E], more[:, 0:E, :], AX.X, ALU.add))
                op(dve.tensor_tensor_scan(tend[:, 0:E], ones[:, 0:E], tiles_e[:, 0:E], 0.0, ALU.mult, ALU.add))
                op(dve.tensor_tensor(tstart[:, 0:E], tend[:, 0:E], tiles_e[:, 0:E], ALU.subtract))
                op(dve.tensor_tensor(more[:, 0:E, :].rearrange("p e t -> p (e t)"), PS[:, RANK_PS, 0:E * NT], inc2, ALU.add))
                op(dve.scalar_tensor_tensor(incl[:, 0:E, :], tstart[:, 0:E].unsqueeze(2).to_broadcast([P, E, NT]), float(P),
                                            more[:, 0:E, :], ALU.mult, ALU.add))
                slot_of = incl[:, 0:E, :].rearrange("p e t -> p t e")
                for k in range(2):
                    op(dve.tensor_tensor(L2g, ohg[k], slot_of, ALU.mult))
                    op(dve.tensor_reduce(pos[:, k, :], L2g, AX.X, ALU.add))
                op(dve.tensor_copy(pos_i[:], pos[:]))
                op(dve.tensor_scalar(rt_i[:, 0, :, :], pos_i[:], P - 1, None, ALU.bitwise_and))
                op(dve.tensor_scalar(rt_i[:, 1, :, :], pos_i[:], 7, None, ALU.logical_shift_right))
                op(dve.tensor_copy(rt_f[:], rt_i[:]))
                for k, (B, A) in enumerate(((Brow, Arhs), (Brow2, Arhs2))):
                    op(dve.tensor_tensor(B[:], iota[:].unsqueeze(1).to_broadcast([P, NT, P]),
                                         per_token(rt_f[:, 0, k, :], P), ALU.is_equal))
                    op(dve.tensor_tensor(Acol[:, :, 0:T], iota[:, 0:T].unsqueeze(1).to_broadcast([P, NT, T]),
                                         per_token(rt_f[:, 1, k, :], T), ALU.is_equal))
                    op(dve.tensor_tensor(A[:, :, 0, 0:T], Acol[:, :, 0:T], per_token(code[:, k, :], T), ALU.mult))
                    ins = dve.tensor_scalar(A[:, :, 1, 0:T], Acol[:, :, 0:T], pid[:, 0:1], None, ALU.mult)
                    op(ins)
                    dve.sem_inc(S(f"inv_in{l}"), 1)

                tt = iota[0:1, 0:T].unsqueeze(2).to_broadcast([1, T, E])
                op(dve.tensor_tensor(tcmp[:, 0:T, 0:E], tend[0:1, 0:E].unsqueeze(1).to_broadcast([1, T, E]), tt, ALU.is_le))
                op(dve.tensor_reduce(tsum[:, 0, 0:T], tcmp[:, 0:T, 0:E], AX.X, ALU.add))
                op(dve.tensor_scalar(tsum[:, 0, 0:T], tsum[:, 0, 0:T], float(E - 1), None, ALU.min))
                op(dve.tensor_tensor(tcmp[:, 0:T, 0:E - 1], tstart[0:1, 0:E - 1].unsqueeze(1).to_broadcast([1, T, E - 1]),
                                     iota[0:1, 0:T].unsqueeze(2).to_broadcast([1, T, E - 1]), ALU.is_equal))
                op(dve.tensor_reduce(tsum[:, 1, 0:T], tcmp[:, 0:T, 0:E - 1], AX.X, ALU.add))
                op(dve.tensor_scalar(tsum[:, 2, 0:T], iota[0:1, 0:T], tend[0:1, E - 1:E], None, ALU.is_lt))
                op(dve.tensor_copy(table[:, :, 0:T], tsum[:, :, 0:T]))
                op(dve.tensor_scalar(last[:, l:l + 1], tend[0:1, E - 1:E], -1.0, None, ALU.add))

                dve.wait_ge(S(f"exp_out{l}"), 2)
                op(dve.tensor_reduce(zsum[:], exg, AX.X, ALU.add))
                op(dve.reciprocal(zrec[:], zsum[:]))
                op(dve.tensor_copy(gate[:, 0, :], zrec[:]))
                op(dve.tensor_tensor(gate[:, 1, :], e2[:], zrec[:], ALU.mult))
                if l == 1:
                    op(dve.tensor_tensor(gsum[:], gate[:, 0, :], gate[:, 1, :], ALU.add))
                    op(dve.tensor_scalar(gsum[:], gsum[:], 1e-6, None, ALU.add))
                    op(dve.reciprocal(zrec[:], gsum[:]))
                    op(dve.tensor_tensor(gate[:], gate[:], zrec[:].unsqueeze(1).to_broadcast([P, 2, NT]), ALU.mult))

                dve.wait_ge(S(f"inv_out{l}"), 1)
                op(dve.tensor_copy(F_sb[:, :, 0:T], PS[:, SLOT_PS, 0:2 * T].rearrange("p (a t) -> p a t", a=2)))
                op(dve.scalar_tensor_tensor(sl[:, 0, 0:T], F_sb[:, 0, 0:T], float(P), F_sb[:, 1, 0:T], ALU.mult, ALU.add))
                op(dve.tensor_scalar(sl[:, 1, 0:T], F_sb[:, 0, 0:T], 0.0, 4.0 * N, ALU.is_equal, ALU.mult))
                op(dve.scalar_tensor_tensor(idx[:, 1, 0:T], sl[:, 0, 0:T], float(-P), sl[:, 1, 0:T], ALU.add, ALU.add))
                op(dve.tensor_scalar(sl[:, 2, 0:T], F_sb[:, 0, 0:T], NT + 0.5, -float(N), ALU.is_gt, ALU.mult))
                op(dve.scalar_tensor_tensor(sl[:, 3, 0:T], sl[:, 0, 0:T], float(-P), sl[:, 2, 0:T], ALU.add, ALU.add))
                op(dve.tensor_scalar(idx[:, 0, 0:T], sl[:, 3, 0:T], 0.0, None, ALU.max))
                dve.sem_inc(S(f"routed{l}"), 1)

            def experts(l):
                E, T = EXPERTS[l], TILES[l]

                def split1_dyn(e, k):
                    dve.wait_ge(S(f"w1_hi{l}"), KD * (e + 1) + k + 1)
                    dve.tensor_tensor(w1lo[:, ds((e + 1) % 2, 1), k, :].rearrange("p a h -> p (a h)"), raw1[:, k, :],
                                      w1hi[:, ds((e + 1) % 2, 1), k, :].rearrange("p a h -> p (a h)").bitcast(F32),
                                      ALU.subtract).then_inc(S(f"w1_split{l}"), 1)

                def x_lo(t):
                    dve.wait_ge(S(f"x_hi{l}"), t + 1)
                    dve.tensor_tensor(xTlo[:], PS[:, XG_PS, 0:KD * P].rearrange("p (k t) -> p k t", k=KD),
                                      xThi[:].bitcast(F32), ALU.subtract).then_inc(S(f"x_lo{l}"), 1)

                def add_b2(t, slot, first=False):
                    dve.wait_ge(S(f"y_done{l}"), t + 1)
                    if not first:
                        dve.wait_ge(S(f"y_out{l}"), 16 * t)
                    dve.tensor_tensor(y_sb[:], PS[:, Y_PS, 0:D], b2_bc[:, ds(slot, 1), :].rearrange("p a d -> p (a d)"),
                                      ALU.add).then_inc(S(f"y_ready{l}"), 1)

                def tile(t, first=False, second=False):
                    if first:
                        e = 0
                    else:
                        e = dve.value_load(table[0:1, 0, ds(t, 1)], min_val=0, max_val=E - 1)
                        e_before = dve.value_load(table[0:1, 0, ds(t - 1, 1)], min_val=0, max_val=E - 1)
                        opens = dve.value_load(table[0:1, 1, ds(t, 1)], min_val=0, max_val=1)
                    for b in range(HB):
                        dve.wait_ge(S(f"h_done{l}"), HB * t + b + 1)
                        if first and b == 0:
                            dve.wait_ge(S(f"b_in{l}"), 32)
                        bias = b1_bc[:, ds(e % 4, 1), b * BANK:(b + 1) * BANK].rearrange("p a h -> p (a h)")
                        dve.tensor_tensor(hrow[:, b * BANK:(b + 1) * BANK], PS[:, H_PS[b], :], bias,
                                          ALU.add).then_inc(S(f"h_biased{l}"), 1)
                    x_lo(t + 1)
                    if first:
                        split1_dyn(0, 0)
                    else:
                        with dve.If(opens == 1):
                            split1_dyn(e, 0)
                        add_b2(t - 1, e_before % 4, first=second)
                    for b in range(HB):
                        dve.wait_ge(S(f"h_hi{l}"), HB * t + b + 1)
                        dve.tensor_tensor(hTlo[:, b * HCB:(b + 1) * HCB, :],
                                          PS[:, HT_PS[b], :].rearrange("p (c t) -> p c t", c=HCB),
                                          hThi[:, b * HCB:(b + 1) * HCB, :].bitcast(F32),
                                          ALU.subtract).then_inc(S(f"h_lo{l}"), 1)
                    if first:
                        for k in range(1, KD):
                            split1_dyn(0, k)
                    else:
                        with dve.If(opens == 1):
                            for k in range(1, KD):
                                split1_dyn(e, k)
                        dve.nop()

                if l == 0:
                    dve.wait_ge(S("gb_in"), 32)
                    dve.tensor_tensor(R[:], R[:], gb_bc[:, 1, :].unsqueeze(1).to_broadcast([P, NT, D]),
                                      ALU.add).then_inc(S("r_beta"), 1)
                x_lo(0)
                tile(0, first=True)
                tile(1, second=True)
                with dve.Fori(2, SURE[l]) as t:
                    tile(t)
                with dve.Fori(SURE[l], T) as t:
                    used = dve.value_load(table[0:1, 2, ds(t, 1)], min_val=0, max_val=1)
                    with dve.If(used == 1):
                        tile(t)
                    dve.nop()
                t = dve.value_load(last[0:1, l:l + 1], min_val=SURE[l] - 1, max_val=T - 1)
                add_b2(t, (E - 1) % 4)

            cc = Chain(dve, S("cmb0"))

            def block_stats(src, q):
                tiles = range(q * UB, (q + 1) * UB)
                for u, T in enumerate(tiles):
                    ins = dve.bn_stats(stats[:, u, :], src[:, T, :])
                cc.done(ins)
                for u, T in enumerate(tiles):
                    ins = dve.bn_aggr(mv[:, T, :], stats[:, u, :])
                cc.done(ins)
                four = slice(q * UB, (q + 1) * UB)
                dve.tensor_scalar(vare[:, four], mv[:, four, 1], LN_EPS, None, ALU.add).then_inc(S("cmb_vare"), 1)

            def comb_a(q):
                four = slice(q * UB, (q + 1) * UB)
                dve.wait_ge(S("y_sum"), q + 1)
                cc.done(dve.tensor_tensor(XN[:, four, :], XN[:, four, :], Yc[:, q, 0, :, :], ALU.add))
                block_stats(XN, q)

            def comb_b(q, n):
                dve.wait_ge(S("cmb_rstd"), n)
                tiles = range(q * UB, (q + 1) * UB)
                for T in tiles:
                    ins = dve.scalar_tensor_tensor(XN[:, T, :], XN[:, T, :], mv[:, T, 0:1], gb_bc[:, 0, :],
                                                   ALU.subtract, ALU.mult)
                cc.done(ins)
                for T in tiles:
                    ins = dve.scalar_tensor_tensor(R[:, T, :], XN[:, T, :], rstd[:, T:T + 1], R[:, T, :],
                                                   ALU.mult, ALU.add)
                cc.done(ins)
                block_stats(R, q)

            def comb_c(q, n):
                dve.wait_ge(S("cmb_rstd"), n)
                four = slice(q * UB, (q + 1) * UB)
                cc.done(dve.tensor_tensor(cscale[:, four], rstd[:, four], dis[:, 1, four], ALU.mult))
                dve.scalar_tensor_tensor(cshift[:, four], mv[:, four, 0], -1.0, cscale[:, four],
                                         ALU.mult, ALU.mult).then_inc(S("x_shift"), 1)

            def combine0():
                dve.wait_ge(S("xn_in"), 16)
                dve.wait_ge(S("r_beta"), 1)
                comb_a(0)
                comb_a(1)
                comb_b(0, 1)
                comb_a(2)
                comb_b(1, 2)
                comb_c(0, 3)

            def combine0_rest(j):
                if j == 0:
                    comb_a(3)
                    comb_b(2, 4)
                    comb_c(1, 5)
                if j == 3:
                    comb_b(3, 6)
                    comb_c(2, 7)
                if j == 8:
                    comb_c(3, 8)

            def combine1():
                c = Chain(dve, S("cmb1"))
                for q in range(NB):
                    dve.wait_ge(S(f"yc{q}_in"), 64)
                    for k in range(2):
                        for u in range(UB):
                            T = q * UB + u
                            ins = dve.scalar_tensor_tensor(R[:, T, :], Yc[:, q, k, u, :], gate[:, k, T:T + 1], R[:, T, :],
                                                           ALU.mult, ALU.add)
                        if k == 0:
                            c.done(ins)
                    ins.then_inc(S("final"), 1)

            end = gnn(1, gnn(0))
            for j in range(NT):
                end(j)
            router(0)
            experts(0)
            combine0()
            end = gnn(2, combine0_rest)
            for j in range(NT):
                end(j)
            router(1)
            experts(1)
            combine1()

        @block.tensor
        def _(pe):
            pe.wait_ge(S("consts"), 1)
            for p in range(3):
                pe.sem_inc(S(f"a_free{p}"), RING[p])
                pe.sem_inc(S(f"u_done{p}"), 1)
                pe.sem_inc(S(f"u_sb{p}"), 2)
                pe.sem_inc(S(f"res{p}"), 2)

            def transposes(i, u, first):
                pe.wait_ge(S(f"stage_in{u}"), 16 * (i + 1))
                r = i * STG + u
                for q in range(4):
                    if not first:
                        pe.wait_ge(S("at_copied"), 4 * r + q - 3)
                    for k in range(4):
                        j = 4 * q + k
                        ins = pe.transpose(PS[:, 4 + q, k * P:(k + 1) * P], stage[u][:, j * P:(j + 1) * P], ident)
                    ins.then_inc(S("at_psum"), 1)

            def rows(i, first):
                for u in range(STG):
                    transposes(i, u, first and u == 0)

            rows(0, True)
            with pe.Fori(1, NT // STG) as i:
                rows(i, False)

            def gnn(p, mid_before=None):
                l = p - 1

                def steps(ib, mid=None):
                    for j in range(NT):
                        if mid is first_mid and j % UB == 0:
                            pe.wait_ge(S(f"xlo{p}"), j // UB + 1)
                        hi, lo = Ahis[p][:, j % RING[p], :], Alos[p][:, j % RING[p], :]
                        g = [PS[:, ds((ib % 2) * KD + d, 1), :].rearrange("p a n -> p (a n)") for d in range(KD)]
                        dd = [slice(d * P, (d + 1) * P) for d in range(KD)]
                        pe.wait_ge(S(f"ahi{p}"), NT * ib + j + 1)
                        for d in range(KD):
                            pe.matmul(g[d], Xhi[:, j, dd[d]], hi, start=(j == 0), stop=False)
                            pe.matmul(g[d], Xlo[:, j, dd[d]], hi, start=False, stop=False)
                        pe.wait_ge(S(f"alo{p}"), NT * ib + j + 1)
                        for d in range(KD):
                            ins = pe.matmul(g[d], Xhi[:, j, dd[d]], lo, start=False, stop=(j == NT - 1))
                        ins.then_inc(S(f"a_free{p}"), 1)
                        if mid is not None:
                            mid(j)

                def project(ib, u):
                    T = UB * ib + u
                    if u == 0:
                        pe.wait_ge(S(f"glo{p}"), KD * (ib + 1))
                    pe.wait_ge(S(f"u_sb{p}"), T + 1)
                    up = PS[:, U_PS[u % 2], 0:D]
                    tt = slice(u * P, (u + 1) * P)
                    for d in range(KD):
                        pe.matmul(up, Ghi[:, d, tt], Whi[:, d, :], start=(d == 0), stop=False)
                        pe.matmul(up, Ghi[:, d, tt], Wlo[:, d, :], start=False, stop=False)
                        ins = pe.matmul(up, Glo[:, d, tt], Whi[:, d, :], start=False, stop=(d == KD - 1))
                    ins.then_inc(S(f"u_done{p}"), 1)

                def gate_x(ib):
                    pe.wait_ge(S(f"xn_out_ready{l}"), ib + 1)
                    for h in range(2):
                        for n in range(2):
                            for k in range(KD):
                                at = (n * KD + k) * P
                                ins = pe.transpose(PS[:, XT_PS[h], at:at + P], xnb[:, 2 * h + n, k * P:(k + 1) * P], ident)
                        ins.then_inc(S(f"xt_psum{l}"), 1)

                def gate_y(ib):
                    E = EXPERTS[l]
                    pe.wait_ge(S(f"xnT{l}"), 2 * ib + 2)
                    for u in range(UB):
                        for k in range(KD):
                            at = ((u % 2) * KD + k) * P
                            ins = pe.matmul(PS[:, LG_PS, ds((ib * UB + u) * E, E)], xnT[:, u // 2, at:at + P], wgate[:, k, l, 0:E],
                                            start=(k == 0), stop=(k == KD - 1))
                    ins.then_inc(S(f"lg_psum{l}"), 1)

                def after(ib):
                    def mid(j):
                        if 3 <= j < 3 + UB:
                            project(ib, j - 3)
                        if p > 0 and j == 13:
                            gate_x(ib)
                        if p > 0 and j == NT - 1:
                            gate_y(ib)
                    return mid

                def first_mid(j):
                    if mid_before is not None:
                        mid_before(j)
                    if j == NT - 1:
                        pe.wait_ge(S("wg_split"), p + 1)

                steps(0, first_mid)
                with pe.Fori(1, NB) as ib:
                    steps(ib, after(ib - 1))
                return after(NB - 1)

            def router(l):
                E, T = EXPERTS[l], COLS[l]
                Mg = M[:, 0:E, :].rearrange("p e t -> p (e t)")
                pe.wait_ge(S(f"m_ready{l}"), 1)
                pe.matmul(PS[:, RANK_PS, 0:E * NT], before[:], Mg, start=True, stop=True)
                pe.matmul(PS[:, TOT_PS, 0:E * NT], ones[:], Mg, start=True, stop=True).then_inc(S(f"rank{l}"), 1)
                for k, (B, A) in enumerate(((Brow, Arhs), (Brow2, Arhs2))):
                    pe.wait_ge(S(f"inv_in{l}"), k + 1)
                    for t in range(NT):
                        ins = pe.matmul(PS[:, SLOT_PS, 0:2 * T].rearrange("p (a t) -> p a t", a=2), B[:, t, :],
                                        A[:, t, :, 0:T], start=(k == 0 and t == 0), stop=(k == 1 and t == NT - 1))
                ins.then_inc(S(f"inv_out{l}"), 1)

            def experts(l):
                E, T = EXPERTS[l], TILES[l]

                def up(t, slot):
                    for b in range(HB):
                        cols = slice(b * BANK, (b + 1) * BANK)
                        for k in range(KD):
                            hi = w1hi[:, ds(slot, 1), k, cols].rearrange("p a h -> p (a h)")
                            lo = w1lo[:, ds(slot, 1), k, cols].rearrange("p a h -> p (a h)")
                            pe.matmul(PS[:, H_PS[b], :], xThi[:, k, :], hi, start=(k == 0), stop=False)
                            pe.matmul(PS[:, H_PS[b], :], xThi[:, k, :], lo, start=False, stop=False)
                            ins = pe.matmul(PS[:, H_PS[b], :], xTlo[:, k, :], hi, start=False, stop=(k == KD - 1))
                        ins.then_inc(S(f"h_done{l}"), 1)

                def x_t(t):
                    pe.wait_ge(S(f"xg_in{l}"), 16 * (t + 1))
                    for k in range(KD):
                        ins = pe.transpose(PS[:, XG_PS, k * P:(k + 1) * P], xg[:, k * P:(k + 1) * P], ident)
                    ins.then_inc(S(f"xt_done{l}"), 1)

                def h_t(t):
                    for b in range(HB):
                        pe.wait_ge(S(f"h_act{l}"), HB * t + b + 1)
                        for k in range(HCB):
                            cc = b * HCB + k
                            ins = pe.transpose(PS[:, HT_PS[b], k * P:(k + 1) * P], hrow[:, cc * P:(cc + 1) * P], ident)
                        ins.then_inc(S(f"ht_done{l}"), 1)

                def down(t, slot, first=False):
                    pe.wait_ge(S(f"h_lo{l}"), HB * (t + 1))
                    if not first:
                        pe.wait_ge(S(f"y_ready{l}"), t)
                    for k in range(HC):
                        hi = w2hi[:, ds(slot, 1), k, :].rearrange("p a h -> p (a h)")
                        lo = w2lo[:, ds(slot, 1), k, :].rearrange("p a h -> p (a h)")
                        yp = PS[:, Y_PS, 0:D]
                        pe.matmul(yp, hThi[:, k, :], hi, start=(k == 0), stop=False)
                        pe.matmul(yp, hThi[:, k, :], lo, start=False, stop=False)
                        ins = pe.matmul(yp, hTlo[:, k, :], hi, start=False, stop=(k == HC - 1))
                    ins.then_inc(S(f"y_done{l}"), 1)

                def tile(t, first=False, second=False):
                    e_next = pe.value_load(table[0:1, 0, ds(t + 1, 1)], min_val=0, max_val=E - 1)
                    if not first:
                        e_before = pe.value_load(table[0:1, 0, ds(t - 1, 1)], min_val=0, max_val=E - 1)
                    x_t(t + 1)
                    if not first:
                        pe.wait_ge(S(f"w2_split{l}"), 2 * (e_before + 1))
                        down(t - 1, e_before % 2, first=second)
                    h_t(t)
                    pe.wait_ge(S(f"x_lo{l}"), t + 2)
                    pe.wait_ge(S(f"w1_split{l}"), KD * (e_next + 1))
                    pe.wait_ge(S(f"h_biased{l}"), HB * (t + 1))
                    up(t + 1, e_next % 2)

                pe.wait_ge(S(f"routed{l}"), 1)
                x_t(0)
                pe.wait_ge(S(f"x_lo{l}"), 1)
                pe.wait_ge(S(f"w1_split{l}"), KD)
                up(0, 0)
                tile(0, first=True)
                tile(1, second=True)
                with pe.Fori(2, SURE[l]) as t:
                    tile(t)
                with pe.Fori(SURE[l], T) as t:
                    used = pe.value_load(table[0:1, 2, ds(t, 1)], min_val=0, max_val=1)
                    with pe.If(used == 1):
                        tile(t)
                    pe.nop()
                t = pe.value_load(last[0:1, l:l + 1], min_val=SURE[l] - 1, max_val=T - 1)
                pe.wait_ge(S(f"w2_split{l}"), 2 * E)
                down(t, (E - 1) % 2)

            end = gnn(1, gnn(0))
            for j in range(NT):
                end(j)
            router(0)
            experts(0)
            end = gnn(2)
            for j in range(NT):
                end(j)
            router(1)
            experts(1)


_INS = ['x', 'adj', 'L0_gnn_Wgcn1', 'L0_gnn_bgcn1', 'L0_gnn_Wgcn12', 'L0_gnn_bgcn12', 'L0_ffn_Wg', 'L0_ffn_bg',
        'L0_ffn_W1', 'L0_ffn_b1', 'L0_ffn_W2', 'L0_ffn_b2', 'L0_ffn_gamma', 'L0_ffn_beta', 'L1_gnn_W', 'L1_ffn_Wg',
        'L1_ffn_W1', 'L1_ffn_b1', 'L1_ffn_W2', 'L1_ffn_b2']


def kernel(**inputs):
    import numpy as _np
    import concourse.bacc as _bacc
    from concourse import mybir as _mybir
    from concourse.bass_utils import run_bass_kernel_spmd as _run

    nc = _bacc.Bacc("TRN2", target_bir_lowering=False, num_devices=1)
    arrays, args = {}, []
    for name in _INS:
        a = _np.ascontiguousarray(inputs[name])
        arrays[f"in_{name}_dram"] = a
        args.append(nc.dram_tensor(f"in_{name}_dram", a.shape, _mybir.dt.from_np(a.dtype), kind="ExternalInput").ap())
    out = nc.dram_tensor("out_0_dram", inputs["x"].shape, _mybir.dt.float32, kind="ExternalOutput").ap()
    moe_gnn_kernel(nc, *args, out)
    r = _run(nc, [arrays], core_ids=[0])
    return r.results[0]["out_0_dram"]
```

```python
from contextlib import ExitStack

import concourse.bass as bass
from concourse import mybir

F32 = mybir.dt.float32
F32R = mybir.dt.float32r
BF16 = mybir.dt.bfloat16
I32 = mybir.dt.int32
ALU = mybir.AluOpType
ACT = mybir.ActivationFunctionType
AX = mybir.AxisListType
ds = bass.ds

P = 128
BANK = 512
LN_EPS = 1e-5
LOWEST = -3.0e38


def moe_gnn_kernel(nc, x, adj, wgcn1, bgcn1, wgcn12, bgcn12, wg0, bg0, w1_0, b1_0, w2_0, b2_0, gamma, beta,
                   wgnn, wg1, w1_1, b1_1, w2_1, b2_1, out):
    N, D = x.shape
    KD = D // P
    NT = N // P
    WIDE = 512
    NB = N // WIDE
    UB = WIDE // P
    H = w1_0.shape[2]
    HC = H // P
    EXPERTS = [w1_0.shape[0], w1_1.shape[0]]
    EMAX = max(EXPERTS)
    TILES = [(2 * N + P * E - 1) // P for E in EXPERTS]
    SURE = [max(2 * N // P, E) for E in EXPERTS]
    assert all(s % 2 == 0 for s in SURE)
    PEEL = [(s // 2 - 1) % 2 for s in SURE]
    RUN = 2
    RUNS = [(T - s + 2 * RUN - 1) // (2 * RUN) for T, s in zip(TILES, SURE)]
    COLS = [s + 2 * r * RUN + 4 for s, r in zip(SURE, RUNS)]
    TMAX = max(COLS)
    WG, BG = [wg0, wg1], [bg0, None]
    W1, B1, W2, B2 = [w1_0, w1_1], [b1_0, b1_1], [w2_0, w2_1], [b2_0, b2_1]
    HB = H // BANK
    HCB = HC // HB

    adjT_d = nc.dram_tensor("adjT_d", [N, N], F32, kind="Internal").ap()
    xn_d = nc.dram_tensor("xn_d", [N, D], F32, kind="Internal").ap()
    y_d = [nc.dram_tensor(f"y{l}_d", [2 * N, D], F32, kind="Internal").ap() for l in range(2)]

    ctx = ExitStack()
    with ctx:
        base = ((nc.sbuf_base + 63) // 64) * 64
        top = [base]

        def sb(name, shape, dt, at=None):
            size = 1
            for s in shape[1:]:
                size *= s
            size *= 2 if dt == BF16 else 4
            off = top[0] if at is None else at
            t = nc.alloc_sbuf_tensor_at(name, shape, dt, offset=off)
            end = (off + size + 63) // 64 * 64
            if at is None:
                top[0] = end
            return t, end

        def lasting(name, shape, dt):
            return sb(name, shape, dt)[0]

        R = lasting("R", [P, NT, D], F32)
        ident = lasting("ident", [P, P], F32)[:]
        before = lasting("before", [P, P], BF16)
        ones = lasting("ones", [P, P], BF16)
        iota = lasting("iota", [P, P], BF16)
        pid = lasting("pid", [P, 1], F32)
        dec = lasting("dec", [P, EMAX], F32)
        keep = lasting("keep", [P, EMAX, NT], BF16)
        thr = lasting("thr", [P, NT], F32)
        code = lasting("code", [P, 2, NT], BF16)
        half = lasting("half", [P, NT], F32)
        bgcn_bc = lasting("bgcn_bc", [P, 2, D], F32)
        bg_bc = lasting("bg_bc", [P, EMAX], F32)
        wgate = lasting("wgate", [P, KD, 2, EMAX], F32)
        to_pow = lasting("to_pow", [P, 3, NT], F32)[:]
        powers = lasting("powers", [P, 3, NT], F32)[:]
        deg, vare, dis, rstd = to_pow[:, 0:2, :], to_pow[:, 2, :], powers[:, 0:2, :], powers[:, 2, :]
        stats = lasting("stats", [P, UB, 6], F32)
        mvb = lasting("mvb", [P, UB, 2], F32)
        mv = lasting("mv", [P, NT, 2], F32)
        L = lasting("L", [P, NT, EMAX], F32)
        gate = lasting("gate", [P, 2, NT], F32)
        table = lasting("table", [1, 2, TMAX], I32)
        last = lasting("last", [1, 2], I32)
        idx = lasting("idx", [P, 2, TMAX], I32)
        idx_use = lasting("idx_use", [P, 2, 2], I32)
        shared = top[0]

        cur = [shared]

        def in_set(name, shape, dt):
            t, cur[0] = sb(name, shape, dt, at=cur[0])
            return t

        AT = in_set("AT", [P, NT, N], F32)
        Xhi = in_set("Xhi", [P, NT, D], F32R)
        Xlo = in_set("Xlo", [P, NT, D], F32R)
        RING = [2, 2, 4]
        Ahi = in_set("Ahi", [P, 2, WIDE], F32R)
        Alo = in_set("Alo", [P, 2, WIDE], F32R)
        Ghi = in_set("Ghi", [P, KD, WIDE], F32R)
        Glo = in_set("Glo", [P, KD, WIDE], F32R)
        Whi = in_set("Whi", [P, KD, D], F32R)
        Wlo = in_set("Wlo", [P, KD, D], F32R)
        gnn_end = cur[0]
        STG = 4
        stage_off = shared + NT * N * 4
        stage = [sb(f"stage{u}", [P, N], F32, at=stage_off + u * N * 4)[0] for u in range(STG)]
        assert STG * N * 4 <= 2 * NT * D * 4
        cur[0] = gnn_end
        xnb = sb("xnb", [P, UB, D], F32, at=gnn_end - 2 * KD * D * 4 - 2 * KD * WIDE * 4)[0]
        xnT = in_set("xnT", [P, 2, BANK], F32)
        Wraw = sb("Wraw", [P, KD, D], F32, at=cur[0] - 2 * BANK * 4)[0]
        assert cur[0] <= nc.sbuf_usable_end, (cur[0], nc.sbuf_usable_end)
        cur[0] = gnn_end - 2 * KD * D * 4 - 2 * KD * WIDE * 4
        iota_i = in_set("iota_i", [P, P], I32)
        pid_i = in_set("pid_i", [P, 1], I32)
        dec_i = in_set("dec_i", [P, EMAX], I32)
        thr_i = in_set("thr_i", [P, NT], I32)
        code_i = in_set("code_i", [P, 2, NT], I32)

        cur[0] = shared
        raw1 = in_set("raw1", [P, KD, H], F32)
        raw2 = in_set("raw2", [P, HC, D], F32)
        XN = in_set("XN", [P, NT, D], F32)
        w1hi = in_set("w1hi", [P, 2, KD, H], F32R)
        w1lo = in_set("w1lo", [P, 2, KD, H], F32R)
        w2hi = in_set("w2hi", [P, 2, HC, D], F32R)
        w2lo = in_set("w2lo", [P, 2, HC, D], F32R)
        hThi = in_set("hThi", [P, HC, P], F32R)
        hTlo = in_set("hTlo", [P, HC, P], F32R)
        assert cur[0] <= shared + NT * N * 4
        cur[0] = shared + NT * N * 4
        b1_bc = in_set("b1_bc", [P, 4, H], F32)
        b2_bc = in_set("b2_bc", [P, 4, D], F32)
        hrow = in_set("hrow", [P, H], F32)
        xg = [in_set(f"xg{odd}", [P, D], F32) for odd in range(2)]
        xThi = in_set("xThi", [P, KD, P], F32R)
        xTlo = in_set("xTlo", [P, KD, P], F32R)
        y_sb = [in_set(f"y_sb{odd}", [P, D], F32) for odd in range(2)]
        gb_bc = in_set("gb_bc", [P, 2, D], F32)
        assert cur[0] <= gnn_end
        cur[0] = shared + NT * N * 4
        oh = [in_set(f"oh{k}", [P, NT, EMAX], F32) for k in range(2)]
        L2 = in_set("L2", [P, NT, EMAX], F32)
        rt = in_set("rt", [P, NT, EMAX], F32)
        assert cur[0] - (shared + NT * N * 4) <= H * 4
        tcmp = in_set("tcmp", [1, TMAX, EMAX], F32)
        tsum = in_set("tsum", [1, 3, TMAX], F32)
        lastf = in_set("lastf", [1, 1], F32)
        tend = in_set("tend", [P, EMAX], F32)
        tstart = in_set("tstart", [P, EMAX], F32)
        assert cur[0] - (shared + NT * N * 4) <= 4 * H * 4
        ex = in_set("ex", [P, NT, EMAX], F32)
        mx = [in_set(f"mx{k}", [P, NT], F32) for k in range(2)]
        pick = in_set("pick", [P, NT], F32)
        zsum = in_set("zsum", [P, NT], F32)
        zrec = in_set("zrec", [P, NT], F32)
        e2 = in_set("e2", [P, NT], F32)
        gsum = in_set("gsum", [P, NT], F32)
        M = in_set("M", [P, EMAX, NT], BF16)
        incl = in_set("incl", [P, EMAX, NT], F32)
        more = in_set("more", [P, EMAX, NT], F32)
        tiles_e = in_set("tiles_e", [P, EMAX], F32)
        pos = in_set("pos", [P, 2, NT], F32)
        pos_i = in_set("pos_i", [P, 2, NT], I32)
        rt_i = in_set("rt_i", [P, 2, 2, NT], I32)
        rt_f = in_set("rt_f", [P, 2, 2, NT], BF16)
        Brow = in_set("Brow", [P, NT, P], BF16)
        Acol = in_set("Acol", [P, NT, TMAX], BF16)
        Arhs = in_set("Arhs", [P, NT, 2, TMAX], BF16)
        Brow2 = in_set("Brow2", [P, NT, P], BF16)
        Arhs2 = in_set("Arhs2", [P, NT, 2, TMAX], BF16)
        F_sb = in_set("F_sb", [P, 2, TMAX], F32)
        sl = in_set("sl", [P, 4, TMAX], F32)
        assert cur[0] <= nc.sbuf_usable_end
        SG, SJ = 4, 2
        strm = [sb(f"strm{s}", [P, SJ, WIDE], F32, at=shared + s * SJ * WIDE * 4)[0] for s in range(SG)]
        assert SG * SJ * WIDE * 4 <= (KD * H + HC * D) * 4
        cur[0] = shared + (KD * H + HC * D) * 4 + NT * D * 4
        U_sb = in_set("U_sb", [P, 2, D], F32)
        Ahi2 = in_set("Ahi2", [P, RING[2], WIDE], F32R)
        Alo2 = in_set("Alo2", [P, RING[2], WIDE], F32R)
        Ahis, Alos = [Ahi, Ahi, Ahi2], [Alo, Alo, Alo2]
        Yc = in_set("Yc", [P, NB, 2, UB, D], F32)
        cscale = in_set("cscale", [P, NT], F32)
        cshift = in_set("cshift", [P, NT], F32)
        assert cur[0] <= shared + NT * N * 4
        loops = in_set("loops", [P, 2 * NB - 1, P], F32)

        PS = ctx.enter_context(nc.psum_tensor("PS", [P, 8, BANK], F32))
        U_PS, XT_PS, LG_PS = (4, 5), (6, 4), 7
        H_PS, HT_PS, Y_PS, XG_PS = (0, 1), (2, 3), 5, (6, 7)
        LAST_LG_PS = NB % 2 * KD
        RANK_PS, TOT_PS, SLOT_PS = 4, 5, 6

        SPLIT_AT = [(0, 3, 10)] * 2 + [(3, 7, 11)]
        SPLIT_AT_DVE = [(0, 3, 11)] * 2 + [(3, 7, 11)]

        names = {}

        def S(name):
            if name not in names:
                names[name] = ctx.enter_context(nc.semaphore(name))
            return names[name]

        class Chain:

            def __init__(self, eng, sem, start=0):
                self.eng, self.sem, self.start, self.n = eng, sem, start, 0

            def done(self, ins):
                ins.then_inc(self.sem, 1)
                self.n += 1
                self.eng.wait_ge(self.sem, self.start + self.n)

        def tile_at(pair, odd, n):
            return pair + (odd + n) // 2, (odd + n) % 2

        def look(eng, l, t):
            v = eng.value_load(table[0:1, 0, ds(t, 1)], min_val=0, max_val=2 * EXPERTS[l] - 1)
            return v // 2, v % 2

        def step_apart(eng):
            eng.sem_inc(S("apart_pool" if eng is nc.gpsimd or "Gp" in type(eng).__name__ else "apart_dve"), 1)

        def per_token(ap, n):
            return ap.unsqueeze(2).to_broadcast([P, ap.shape[1], n])

        adjT_tiles = adjT_d.rearrange("(j p) i -> p j i", p=P)
        x_tiles = x.rearrange("(t p) d -> p t d", p=P)
        xn_tiles = xn_d.rearrange("(t p) d -> p t d", p=P)
        out_tiles = out.rearrange("(t p) d -> p t d", p=P)
        y_tiles = [y.rearrange("(k t p) d -> p t k d", p=P, k=2) for y in y_d]
        Wg = [wgcn1, wgcn12, wgnn]

        block = ctx.enter_context(nc.Block())

        @block.sync
        def _(sp):
            for u in range(STG):
                sp.dma_start(stage[u][:], adj[u * P:(u + 1) * P, :]).then_inc(S(f"stage_in{u}"), 16)
            sp.dma_start(R[:], x_tiles).then_inc(S("x_in"), 16)
            bc = lambda row, n: row.rearrange("(a n) -> a n", a=1).to_broadcast([P, n])
            sp.dma_start(bgcn_bc[:, 0, :], bc(bgcn1, D)).then_inc(S("const_in"), 16)
            sp.dma_start(bgcn_bc[:, 1, :], bc(bgcn12, D)).then_inc(S("const_in"), 16)
            sp.dma_start(bg_bc[:], bc(bg0, EXPERTS[0])).then_inc(S("const_in"), 16)
            for l in range(2):
                sp.dma_start(wgate[:, :, l, 0:EXPERTS[l]], WG[l].rearrange("(k p) e -> p k e", p=P)).then_inc(S("const_in"), 16)
            sp.dma_start(Wraw[:], Wg[0].rearrange("(k p) d -> p k d", p=P)).then_inc(S("wg_in"), 16)
            with sp.Fori(1, NT // STG) as i:
                for u in range(STG):
                    sp.wait_ge(S(f"stage_read{u}"), i)
                    sp.wait_ge(S("at_psum"), 4 * ((i - 1) * STG + u + 1))
                    sp.dma_start(stage[u][:], adj[ds((i * STG + u) * P, P), :]).then_inc(S(f"stage_in{u}"), 16)

            sp.wait_ge(S("at_copied"), 4 * NT)
            sp.dma_start(adjT_tiles, AT[:]).then_inc(S("at_out"), 16)

            sp.wait_ge(S("wg_split"), 1)
            sp.dma_start(Wraw[:], Wg[1].rearrange("(k p) d -> p k d", p=P)).then_inc(S("wg_in"), 16)
            sp.wait_ge(S("xlo1"), NB)
            sp.dma_start(R[:], x_tiles).then_inc(S("x_again"), 16)
            for l in range(2):
                sp.sem_inc(S(f"xn_out{l}"), 16)
            sp.wait_ge(S("xn_out_ready0"), 1)
            sp.dma_start(xn_tiles[:, 0:UB, :], xnb[:]).then_inc(S("xn_out0"), 16)
            with sp.Fori(1, NB) as ib:
                sp.wait_ge(S("xn_out_ready0"), ib + 1)
                sp.dma_start(xn_tiles[:, ds(ib * UB, UB), :], xnb[:]).then_inc(S("xn_out0"), 16)

            def expert_loads(l):
                E = EXPERTS[l]
                w1v = W1[l].rearrange("e (k p) h -> p e k h", p=P)
                w2v = W2[l].rearrange("e (c p) d -> p e c d", p=P)

                def load(e, slot):
                    sp.wait_ge(S(f"w1_split{l}"), KD * e)
                    sp.dma_start(raw1[:], w1v[:, ds(e, 1), :, :].rearrange("p a k h -> p (a k) h")).then_inc(S(f"w1_in{l}"), 16)
                    sp.dma_start(b1_bc[:, slot, :], B1[l][ds(e, 1), :].to_broadcast([P, H])).then_inc(S(f"w1_in{l}"), 16)
                    sp.wait_ge(S(f"w2_split{l}"), 2 * e)
                    sp.dma_start(raw2[:], w2v[:, ds(e, 1), :, :].rearrange("p a c d -> p (a c) d")).then_inc(S(f"w2_in{l}"), 16)
                    sp.dma_start(b2_bc[:, slot, :], B2[l][ds(e, 1), :].to_broadcast([P, D])).then_inc(S(f"w2_in{l}"), 16)

                sp.dma_start(raw1[:], w1v[:, 0, :, :]).then_inc(S(f"w1_in{l}"), 16)
                sp.dma_start(raw2[:], w2v[:, 0, :, :]).then_inc(S(f"w2_in{l}"), 16)
                sp.wait_ge(S("slots"), l + 1)
                sp.wait_ge(S(f"xg0_in{l}"), 16)
                if l == 0:
                    sp.dma_start(gb_bc[:, 0, :], bc(gamma, D)).then_inc(S("gb_in"), 16)
                    sp.dma_start(gb_bc[:, 1, :], bc(beta, D)).then_inc(S("gb_in"), 16)
                sp.dma_start(b1_bc[:, 0, :], B1[l][0:1, :].to_broadcast([P, H])).then_inc(S(f"b_in{l}"), 16)
                sp.dma_start(b2_bc[:, 0, :], B2[l][0:1, :].to_broadcast([P, D])).then_inc(S(f"b_in{l}"), 16)
                sp.wait_ge(S("routed"), l + 1)
                sp.wait_ge(S(f"xg0_in{l}"), 32)
                sp.wait_ge(S(f"xg1_in{l}"), 16)
                for e in range(1, 4):
                    load(e, e)
                    if e > 1 and l == 0:
                        half_n = slice((e - 2) * NT // 2, (e - 1) * NT // 2)
                        sp.dma_start(XN[:, half_n, :], xn_tiles[:, half_n, :]).then_inc(S("xn_in"), 16)
                with sp.Fori(1, E // 4) as q:
                    for s in range(4):
                        load(q * 4 + s, s)

            sp.wait_ge(S("a_free1"), NT * NB + RING[1])
            sp.wait_ge(S("at_out"), 16)
            sp.wait_ge(S("xn_out0"), 16 * (NB + 1))
            expert_loads(0)

            def combine_loads(l):
                sp.wait_ge(S("y_all"), l + 1)
                for q in range(NB):
                    for k in range(2):
                        sp.dma_start(Yc[:, q, k, :, :], y_tiles[l][:, q * UB:(q + 1) * UB, k, :]).then_inc(S(f"yc{q}_in"), 16)

            combine_loads(0)
            sp.wait_ge(S("wg_split"), 2)
            sp.dma_start(Wraw[:], Wg[2].rearrange("(k p) d -> p k d", p=P)).then_inc(S("wg_in"), 16)
            GPB = NT // SJ

            def stream(ib, q, s):
                sp.dma_start(strm[s][:], adjT_tiles[:, q * SG * SJ + s * SJ:q * SG * SJ + (s + 1) * SJ,
                                                    ds(ib * WIDE, WIDE)]).then_inc(S(f"strm_in{s}"), 16)

            for s in range(SG):
                stream(0, 0, s)
            for q in range(1, GPB // SG):
                for s in range(SG):
                    sp.wait_ge(S("alo2"), SJ * (SG * (q - 1) + s + 1))
                    stream(0, q, s)
            with sp.Fori(1, NB) as ib:
                for q in range(GPB // SG):
                    for s in range(SG):
                        sp.wait_ge(S("alo2"), ib * NT + SJ * (SG * (q - 1) + s + 1))
                        stream(ib, q, s)
                sp.wait_ge(S("xn_out_ready1"), ib)
                sp.dma_start(xn_tiles[:, ds((ib - 1) * UB, UB), :], xnb[:]).then_inc(S("xn_out1"), 16)
            sp.wait_ge(S("xn_out_ready1"), NB)
            sp.dma_start(xn_tiles[:, (NB - 1) * UB:, :], xnb[:]).then_inc(S("xn_out1"), 16)
            sp.wait_ge(S("a_free2"), NT * NB + RING[2])
            expert_loads(1)
            combine_loads(1)
            for q in range(NB):
                sp.wait_ge(S("final"), q + 1)
                sp.dma_start(out_tiles[:, q * UB:(q + 1) * UB, :], R[:, q * UB:(q + 1) * UB, :]).then_inc(S("out_done"), 16)
            sp.wait_ge(S("out_done"), 16 * NB)

        @block.gpsimd
        def _(pool):
            c = Chain(pool, S("pool_const"))
            c.done(pool.memset(ident, 0.0))
            c.done(pool.affine_select(out=ident, in_=ident, compare_op=ALU.not_equal, fill=1.0, base=0,
                                      pattern=[[-1, P]], channel_multiplier=1))
            c.done(pool.memset(half[:], -0.5))
            pool.sem_inc(S("consts"), 1)
            c.done(pool.memset(ones[:], 1.0))
            c.done(pool.memset(before[:], 0.0))
            c.done(pool.affine_select(out=before[:], in_=before[:], compare_op=ALU.is_gt, fill=-1.0, base=0,
                                      pattern=[[1, P]], channel_multiplier=-1))
            c.done(pool.memset(keep[:], 1.0))
            c.done(pool.affine_select(out=keep[:], in_=keep[:], compare_op=ALU.not_equal, fill=0.0, base=0,
                                      pattern=[[0, EMAX], [1, NT]], channel_multiplier=0))
            c.done(pool.iota(iota_i[:], pattern=[[1, P]], base=0, channel_multiplier=0))
            c.done(pool.iota(pid_i[:], pattern=[[0, 1]], base=0, channel_multiplier=1))
            c.done(pool.iota(dec_i[:], pattern=[[-1, EMAX]], base=EMAX, channel_multiplier=0))
            c.done(pool.iota(thr_i[:], pattern=[[P, NT]], base=0, channel_multiplier=0))
            c.done(pool.iota(code_i[:], pattern=[[NT, 2], [1, NT]], base=1, channel_multiplier=0))
            c.done(pool.tensor_copy(iota[:], iota_i[:]))
            c.done(pool.tensor_copy(pid[:], pid_i[:]))
            c.done(pool.tensor_copy(dec[:], dec_i[:]))
            c.done(pool.tensor_copy(thr[:], thr_i[:]))
            c.done(pool.tensor_copy(code[:], code_i[:]))
            c.done(pool.memset(thr[:, 0:1], -1.0))
            pool.sem_inc(S("consts"), 1)

            with pool.Fori(0, NT // STG) as i:
                pool.wait_ge(S("deg_ready"), i + 1)
                step_apart(pool)
                four = ds(i * STG, STG)
                pool.tensor_tensor(powers[:, :, four], to_pow[:, :, four],
                                   half[:, 0:3 * STG].rearrange("p (a t) -> p a t", a=3), ALU.pow).then_inc(S("dis"), 1)

            def residual(p, l):

                def self_loop(ib, j):
                    q, s = divmod(j // SJ, SG)
                    if j % SJ == 0:
                        pool.wait_ge(S(f"strm_in{s}"), 16 * (ib * (NT // SJ // SG) + q + 1))
                    step_apart(pool)
                    part = strm[s][:, j % SJ, (j % UB) * P:(j % UB + 1) * P]
                    pool.tensor_tensor(part, part, loops[:, ds(ib + (NB - 1 - j // UB), 1), :].rearrange("p a n -> p (a n)"),
                                       ALU.add).then_inc(S("looped"), 1)

                def add(ib, u):
                    tile = R[:, ds(UB * ib + u, 1), :].rearrange("p a d -> p (a d)")
                    pool.wait_ge(S(f"u_sb{p}"), UB * ib + u + 3)
                    if p == 1:
                        pool.wait_ge(S("const_in"), 16 * 5)
                    step_apart(pool)
                    pool.tensor_tensor(tile, tile, bgcn_bc[:, 1, :] if p == 1 else U_sb[:, u % 2, :],
                                       ALU.add).then_inc(S(f"res{p}"), 1)

                def sigma(ib):
                    pool.wait_ge(S(f"vare{l}"), ib + 1)
                    step_apart(pool)
                    pool.tensor_tensor(rstd[:, ds(UB * ib, UB)], vare[:, ds(UB * ib, UB)], half[:, 0:UB],
                                       ALU.pow).then_inc(S(f"rstd{l}"), 1)

                def block_end(ib):
                    for u in range(UB):
                        add(ib, u)
                    sigma(ib)

                if p == 1:
                    with pool.Fori(0, NB) as ib:
                        block_end(ib)
                    return
                pool.memset(loops[:], 0.0).then_inc(S("loops"), 1)
                pool.wait_ge(S("loops"), 1)
                pool.tensor_copy(loops[:, NB - 1, :], ident).then_inc(S("loops"), 1)
                pool.wait_ge(S("loops"), 2)

                def weighted_sum(q):
                    pool.wait_ge(S("y_weighted"), q)
                    pool.tensor_tensor(Yc[:, q, 0, :, :], Yc[:, q, 0, :, :], Yc[:, q, 1, :, :],
                                       ALU.add).then_inc(S("y_sum"), 1)

                def times_gamma(q):
                    four = slice(q * UB, (q + 1) * UB)
                    pool.wait_ge(S("y_normed"), q + 1)
                    pool.tensor_tensor(XN[:, four, :], XN[:, four, :], gb_bc[:, 0, :].unsqueeze(1).to_broadcast([P, UB, D]),
                                       ALU.mult).then_inc(S("y_gamma"), 1)

                def comb_sigma(n, q):
                    pool.wait_ge(S("cmb_vare"), n)
                    four = slice(q * UB, (q + 1) * UB)
                    pool.tensor_tensor(rstd[:, four], vare[:, four], half[:, 0:UB], ALU.pow).then_inc(S("cmb_rstd"), 1)

                comb_sigma(1, 0)
                weighted_sum(1)
                weighted_sum(2)
                times_gamma(0)
                comb_sigma(2, 1)
                weighted_sum(3)
                comb_sigma(3, 2)
                times_gamma(1)
                comb_sigma(4, 0)
                comb_sigma(5, 3)
                for j in range(NT):
                    if j == 2:
                        comb_sigma(6, 1)
                        times_gamma(2)
                    if j == 4:
                        times_gamma(3)
                    if j == 6:
                        comb_sigma(7, 2)
                    if j == 8:
                        comb_sigma(8, 3)
                    self_loop(0, j)
                with pool.Fori(1, NB) as ib:
                    for j in range(NT):
                        self_loop(ib, j)
                        if 6 <= j < 6 + UB:
                            add(ib - 1, j - 6)
                        if j == 12:
                            sigma(ib - 1)
                block_end(NB - 1)

            def expert_moves(l):
                E, T = EXPERTS[l], TILES[l]

                def gather(pair, odd):
                    if not isinstance(pair, int) or pair > 0:
                        pool.wait_ge(S(f"xg{odd}_in{l}"), 16 * pair)
                        pool.wait_ge(S(f"xt_done{l}"), 2 * pair + odd - 1)
                    t = 2 * pair + odd
                    pool.tensor_copy(idx_use[:, 0, odd:odd + 1], idx[:, 0, ds(t, 1)]).then_inc(S(f"idx_g{l}"), 1)
                    pool.wait_ge(S(f"idx_g{l}"), t + 1)
                    step_apart(pool)
                    pool.indirect_dma_start(xg[odd][:], None, xn_d, bass.IndirectOffsetOnAxis(idx_use[:, 0, odd:odd + 1], 0),
                                            bounds_check=N - 1, oob_is_err=True).then_inc(S(f"xg{odd}_in{l}"), 16)

                def scatter(pair, odd):
                    if not isinstance(pair, int) or pair > 0:
                        pool.wait_ge(S(f"y{odd}_out{l}"), 16 * pair)
                    t = 2 * pair + odd
                    pool.tensor_copy(idx_use[:, 1, odd:odd + 1], idx[:, 1, ds(t, 1)]).then_inc(S(f"idx_s{l}"), 1)
                    pool.wait_ge(S(f"idx_s{l}"), t + 1)
                    pool.wait_ge(S(f"y_ready{l}"), t + 1)
                    step_apart(pool)
                    pool.indirect_dma_start(y_d[l], bass.IndirectOffsetOnAxis(idx_use[:, 1, odd:odd + 1], 0), y_sb[odd][:], None,
                                            bounds_check=2 * N - 1, oob_is_err=False).then_inc(S(f"y{odd}_out{l}"), 16)

                def split2_dyn(e, q):
                    slot = ds((e + 1) % 2, 1)
                    pool.wait_ge(S(f"w2_hi{l}"), 2 * (e + 1) + q + 1)
                    step_apart(pool)
                    pool.tensor_tensor(w2lo[:, slot, 4 * q:4 * q + 4, :].rearrange("p a c d -> p (a c) d"),
                                       raw2[:, 4 * q:4 * q + 4, :],
                                       w2hi[:, slot, 4 * q:4 * q + 4, :].rearrange("p a c d -> p (a c) d").bitcast(F32),
                                       ALU.subtract).then_inc(S(f"w2_split{l}"), 1)

                def tile(pair, odd, second=False):
                    if second:
                        gather(*tile_at(pair, odd, 3))
                        split2_dyn(0, 0)
                        scatter(*tile_at(pair, odd, -1))
                        split2_dyn(0, 1)
                        return
                    t = 2 * pair + odd
                    e, opens = look(pool, l, t - 1)
                    gather(*tile_at(pair, odd, 3))
                    with pool.If(opens == 1):
                        split2_dyn(e, 0)
                    scatter(*tile_at(pair, odd, -1))
                    with pool.If(opens == 1):
                        split2_dyn(e, 1)
                    pool.nop()

                for k in range(KD):
                    pool.wait_ge(S(f"w1_hi{l}"), k + 1)
                    pool.tensor_tensor(w1lo[:, 0, k, :], raw1[:, k, :], w1hi[:, 0, k, :].bitcast(F32),
                                       ALU.subtract).then_inc(S(f"w1_split{l}"), 1)
                for q in range(2):
                    four = slice(4 * q, 4 * q + 4)
                    pool.wait_ge(S(f"w2_hi{l}"), q + 1)
                    pool.tensor_tensor(w2lo[:, 0, four, :], raw2[:, four, :], w2hi[:, 0, four, :].bitcast(F32),
                                       ALU.subtract).then_inc(S(f"w2_split{l}"), 1)
                pool.wait_ge(S("slots"), l + 1)
                pool.wait_ge(S(f"xn_out{l}"), 16 * (NB + 1))
                for n in range(4):
                    gather(*tile_at(0, 0, n))
                tile(0, 1, second=True)
                pool.wait_ge(S("routed"), l + 1)
                for n in range(2 * PEEL[l]):
                    tile(1 + n // 2, n % 2)
                with pool.Fori(1 + PEEL[l], SURE[l] // 2, 2) as first_pair:
                    for n in range(4):
                        tile(first_pair + n // 2, n % 2)
                with pool.Fori(0, RUNS[l]) as r:
                    run_used = pool.value_load(table[0:1, 1, ds(r * (2 * RUN) + SURE[l], 1)], min_val=0, max_val=1)
                    with pool.If(run_used == 1):
                        with pool.Fori(0, RUN) as i:
                            pair = r * RUN + SURE[l] // 2 + i
                            used = pool.value_load(table[0:1, 1, ds(pair * 2, 1)], min_val=0, max_val=1)
                            with pool.If(used == 1):
                                for odd in range(2):
                                    tile(pair, odd)
                            pool.nop()
                    pool.nop()
                pair = pool.value_load(last[0:1, l:l + 1], min_val=SURE[l] // 2 - 1, max_val=SURE[l] // 2 + RUN * RUNS[l] - 1)
                scatter(pair, 1)
                for odd in range(2):
                    pool.wait_ge(S(f"y{odd}_out{l}"), 16 * (pair + 1))
                    pool.wait_ge(S(f"xg{odd}_in{l}"), 16 * (pair + 3 - odd))
                pool.sem_inc(S("y_all"), 1)

            residual(1, 0)
            expert_moves(0)
            residual(2, 1)
            expert_moves(1)

        @block.scalar
        def _(act):
            def copy_out(r, cols):
                for q in range(4):
                    act.wait_ge(S("at_psum"), 4 * r + q + 1)
                    act.activation(AT[:, 4 * q:4 * q + 4, cols],
                                   PS[:, 4 + q, :].rearrange("p (j i) -> p j i", j=4), ACT.Copy).then_inc(S("at_copied"), 1)

            copy_out(0, slice(0, P))
            with act.Fori(1, NT) as r:
                copy_out(r, ds(r * P, P))

            def split_x(p, src, q):
                if p == 1:
                    act.wait_ge(S("res0"), UB * (q + 1) + 2)
                    act.wait_ge(S("a_free0"), NT * NB + RING[0])
                elif p == 0:
                    act.wait_ge(S("x_scaled0"), q + 1)
                    if q == 0:
                        for u in range(STG):
                            act.wait_ge(S(f"stage_read{u}"), NT // STG)
                else:
                    act.wait_ge(S("x_shift"), q + 1)
                    for u in range(UB):
                        T = q * UB + u
                        ins = act.activation(src[:, T, :], R[:, T, :], ACT.Identity, bias=cshift[:, T:T + 1],
                                             scale=cscale[:, T:T + 1])
                    ins.then_inc(S("x_scaled2"), 1)
                    act.wait_ge(S("x_scaled2"), q + 1)
                act.activation(Xhi[:, UB * q:UB * q + UB, :], src[:, UB * q:UB * q + UB, :],
                               ACT.Copy).then_inc(S(f"xhi{p}"), 1)

            def split_w(p):
                act.wait_ge(S("wg_in"), 16 * (p + 1))
                act.activation(Whi[:], Wraw[:], ACT.Copy).then_inc(S("whi"), 1)

            def gnn(p, mid_before=None):
                src_x = XN if p == 2 else R

                def steps(ib, mid=None):
                    for j in range(NT):
                        if p == 2:
                            act.wait_ge(S("looped"), NT * ib + j + 1)
                        if p == 1 and mid is first_mid and j < RING[0]:
                            act.wait_ge(S("a_free0"), NT * NB + j + 1)
                        act.wait_ge(S(f"a_free{p}"), NT * ib + j + 1)
                        src = strm[(j // SJ) % SG][:, j % SJ, :] if p == 2 else \
                            AT[:, j, ds(ib * WIDE, WIDE)]
                        act.activation(Ahis[p][:, j % RING[p], :], src, ACT.Copy).then_inc(S(f"ahi{p}"), 1)
                        if mid is not None:
                            mid(j)

                def split_g(ib, d):
                    if d == 0:
                        act.wait_ge(S(f"a_free{p}"), NT * (ib + 1) + RING[p])
                        act.wait_ge(S(f"u_done{p}"), UB * ib + 1)
                        if p > 0:
                            act.wait_ge(S(f"xn_out{p - 1}"), 16 * (ib + 1))
                    act.activation(Ghi[:, d, :], PS[:, ds((ib % 2) * KD + d, 1), :].rearrange("p a n -> p (a n)"),
                                   ACT.Copy).then_inc(S(f"ghi{p}"), 1)

                def relu(ib, u):
                    act.wait_ge(S(f"u_sb{p}"), UB * ib + u + 3)
                    tile = R[:, ds(UB * ib + u, 1), :].rearrange("p a d -> p (a d)")
                    act.activation(tile, tile, ACT.Relu,
                                   scale=dis[:, 0, ds(UB * ib + u, 1)]).then_inc(S(f"res{p}"), 1)

                def gate_in(l, ib, h):
                    act.wait_ge(S(f"xt_psum{l}"), 2 * ib + h + 1)
                    act.activation(xnT[:, h, :], PS[:, XT_PS[h], :], ACT.Copy).then_inc(S(f"xnT{l}"), 1)

                def after(ib):
                    def mid(j):
                        if 1 <= j <= KD:
                            split_g(ib, j - 1)
                        if p == 0 and 7 <= j < 7 + UB:
                            relu(ib, j - 7)
                        if p > 0 and j == NT - 1:
                            for h in range(2):
                                gate_in(p - 1, ib, h)
                    return mid

                def first_mid(j):
                    if mid_before is not None:
                        mid_before(j)
                    if j in SPLIT_AT[p]:
                        split_x(p, src_x, 1 + SPLIT_AT[p].index(j))
                    if j == NT - 3:
                        split_w(p)

                split_x(p, src_x, 0)
                steps(0, first_mid)
                with act.Fori(1, NB) as ib:
                    steps(ib, after(ib - 1))
                return after(NB - 1)

            def weight(q):
                act.wait_ge(S(f"yc{q}_in"), 32)
                for k in range(2):
                    for u in range(UB):
                        part = Yc[:, q, k, u, :]
                        ins = act.activation(part, part, ACT.Copy, scale=gate[:, k, q * UB + u:q * UB + u + 1])
                ins.then_inc(S("y_weighted"), 1)

            def layer_norm(q):
                act.wait_ge(S("y_shift"), q + 1)
                for T in range(q * UB, (q + 1) * UB):
                    ins = act.activation(XN[:, T, :], XN[:, T, :], ACT.Identity, bias=cshift[:, T:T + 1],
                                         scale=rstd[:, T:T + 1])
                ins.then_inc(S("y_normed"), 1)

            def combine0():
                weight(1)
                weight(2)
                layer_norm(0)
                weight(3)
                layer_norm(1)

            def combine0_rest(j):
                if j < 2:
                    layer_norm(2 + j)

            def first_expert(l):
                act.wait_ge(S(f"w1_in{l}"), 16)
                for k in range(KD):
                    act.activation(w1hi[:, 0, k, :], raw1[:, k, :], ACT.Copy).then_inc(S(f"w1_hi{l}"), 1)
                act.wait_ge(S(f"w2_in{l}"), 16)
                for q in range(2):
                    act.activation(w2hi[:, 0, 4 * q:4 * q + 4, :], raw2[:, 4 * q:4 * q + 4, :],
                                   ACT.Copy).then_inc(S(f"w2_hi{l}"), 1)

            def experts(l, func):
                E, T = EXPERTS[l], TILES[l]

                def split1_dyn(e, k):
                    act.wait_ge(S(f"w1_in{l}"), 32 * (e + 1) + 16)
                    act.activation(w1hi[:, ds((e + 1) % 2, 1), k, :].rearrange("p a h -> p (a h)"), raw1[:, k, :],
                                   ACT.Copy).then_inc(S(f"w1_hi{l}"), 1)

                def split2_dyn(e, q):
                    act.wait_ge(S(f"w2_in{l}"), 32 * (e + 1) + 16)
                    act.activation(w2hi[:, ds((e + 1) % 2, 1), 4 * q:4 * q + 4, :].rearrange("p a c d -> p (a c) d"),
                                   raw2[:, 4 * q:4 * q + 4, :], ACT.Copy).then_inc(S(f"w2_hi{l}"), 1)

                def x_hi(t, odd):
                    act.wait_ge(S(f"xt_done{l}"), t + 1)
                    act.activation(xThi[:], PS[:, XG_PS[odd], 0:KD * P].rearrange("p (k t) -> p k t", k=KD),
                                   ACT.Copy).then_inc(S(f"x_hi{l}"), 1)

                def tile(pair, odd, first=False, seen=None, ahead=False):
                    t = 2 * pair + odd
                    if not first:
                        e, opens = seen or look(act, l, t)
                    for b in range(HB):
                        act.wait_ge(S(f"h_biased{l}"), HB * t + b + 1)
                        act.activation(hrow[:, b * BANK:(b + 1) * BANK], hrow[:, b * BANK:(b + 1) * BANK],
                                       func).then_inc(S(f"h_act{l}"), 1)
                    x_hi(t + 1, 1 - odd)
                    seen = look(act, l, t + 1) if ahead else None
                    if first:
                        for k in range(KD):
                            split1_dyn(0, k)
                    else:
                        with act.If(opens == 1):
                            for k in range(KD):
                                split1_dyn(e, k)
                    for b in range(HB):
                        act.wait_ge(S(f"ht_done{l}"), HB * t + b + 1)
                        act.activation(hThi[:, b * HCB:(b + 1) * HCB, :],
                                       PS[:, HT_PS[b], :].rearrange("p (c t) -> p c t", c=HCB),
                                       ACT.Copy).then_inc(S(f"h_hi{l}"), 1)
                    if first:
                        for q in range(2):
                            split2_dyn(0, q)
                    else:
                        with act.If(opens == 1):
                            act.wait_ge(S(f"y_done{l}"), t)
                            for q in range(2):
                                split2_dyn(e, q)
                        act.nop()
                    return seen

                x_hi(0, 0)
                tile(0, 0, first=True)
                act.wait_ge(S("routed"), l + 1)
                tile(0, 1)
                seen = None
                for n in range(2 * PEEL[l]):
                    seen = tile(1 + n // 2, n % 2, seen=seen)
                with act.Fori(1 + PEEL[l], SURE[l] // 2, 2) as first_pair:
                    seen = None
                    for n in range(4):
                        seen = tile(first_pair + n // 2, n % 2, seen=seen, ahead=n < 3)
                with act.Fori(0, RUNS[l]) as r:
                    run_used = act.value_load(table[0:1, 1, ds(r * (2 * RUN) + SURE[l], 1)], min_val=0, max_val=1)
                    with act.If(run_used == 1):
                        with act.Fori(0, RUN) as i:
                            pair = r * RUN + SURE[l] // 2 + i
                            used = act.value_load(table[0:1, 1, ds(pair * 2, 1)], min_val=0, max_val=1)
                            with act.If(used == 1):
                                seen = None
                                for odd in range(2):
                                    seen = tile(pair, odd, seen=seen, ahead=odd == 0)
                            act.nop()
                    act.nop()

            end = gnn(1, gnn(0))
            for j in range(NT):
                end(j)
            first_expert(0)
            act.wait_ge(S("exp_in"), 1)
            act.activation(ex[:, :, 0:EXPERTS[0]], rt[:, :, 0:EXPERTS[0]], ACT.Exp).then_inc(S("exp_out"), 1)
            act.activation(e2[:], pick[:], ACT.Exp).then_inc(S("exp_out"), 1)
            experts(0, ACT.Relu)
            combine0()
            end = gnn(2, combine0_rest)
            for j in range(NT):
                end(j)
            act.wait_ge(S("res2"), NT + 2)
            first_expert(1)
            act.wait_ge(S("exp_in"), 2)
            act.activation(ex[:, :, 0:EXPERTS[1]], rt[:, :, 0:EXPERTS[1]], ACT.Exp).then_inc(S("exp_out"), 1)
            act.activation(e2[:], pick[:], ACT.Exp).then_inc(S("exp_out"), 1)
            experts(1, ACT.Gelu)

        @block.vector
        def _(dve):
            def norm_stats(src, u, sem, start):
                ch = Chain(dve, sem, start)
                step_apart(dve)
                ch.done(dve.bn_stats(stats[:, u, :], src))
                step_apart(dve)
                ch.done(dve.bn_aggr(mvb[:, u, :], stats[:, u, :]))

            def sums(i):
                for u in range(STG):
                    dve.wait_ge(S(f"stage_in{u}"), 16 * (i + 1))
                    dve.tensor_reduce(deg[:, 0, ds(i * STG + u, 1)], stage[u][:], AX.X, ALU.add).then_inc(S(f"stage_read{u}"), 1)

            def degrees(i):
                for u in range(STG):
                    dve.wait_ge(S(f"stage_read{u}"), i + 1)
                four = ds(i * STG, STG)
                dve.tensor_scalar(deg[:, 1, four], deg[:, 0, four], 1.0, None, ALU.add).then_inc(S("deg_ready"), 1)

            def scale(i):
                four = ds(i * STG, STG)
                dve.wait_ge(S("dis"), i + 1)
                dve.tensor_tensor(rstd[:, four], rstd[:, four], dis[:, 0, four], ALU.mult).then_inc(S("x_factor"), 1)
                dve.wait_ge(S("x_factor"), i + 1)
                for u in range(STG):
                    T = i * STG + u
                    tile = R[:, ds(T, 1), :].rearrange("p a d -> p (a d)")
                    ins = dve.tensor_scalar(tile, tile, mv[:, ds(T, 1), 0:1].rearrange("p a b -> p (a b)"),
                                            rstd[:, ds(T, 1)], ALU.subtract, ALU.mult)
                ins.then_inc(S("x_scaled0"), 1)

            sums(0)
            c = Chain(dve, S("x_stat"))
            dve.wait_ge(S("x_in"), 16)
            for q in range(NB):
                for u in range(UB):
                    ins = dve.bn_stats(stats[:, u, :], R[:, q * UB + u, :])
                c.done(ins)
                for u in range(UB):
                    ins = dve.bn_aggr(mv[:, q * UB + u, :], stats[:, u, :])
                c.done(ins)
            c.done(dve.tensor_scalar(vare, mv[:, :, 1], LN_EPS, None, ALU.add))
            degrees(0)
            with dve.Fori(1, NT // STG) as i:
                sums(i)
                degrees(i)
                scale(i - 1)

            def scale_last(j):
                if j == 0:
                    scale(NT // STG - 1)

            def split_x(p, src, q):
                dve.wait_ge(S(f"xhi{p}"), q + 1)
                dve.tensor_tensor(Xlo[:, UB * q:UB * q + UB, :], src[:, UB * q:UB * q + UB, :],
                                  Xhi[:, UB * q:UB * q + UB, :].bitcast(F32), ALU.subtract).then_inc(S(f"xlo{p}"), 1)

            def split_w(p):
                dve.wait_ge(S("whi"), p + 1)
                dve.tensor_tensor(Wlo[:], Wraw[:], Whi[:].bitcast(F32), ALU.subtract).then_inc(S("wg_split"), 1)

            def gnn(p, mid_before=None):
                l = p - 1
                src_x = XN if p == 2 else R

                def steps(ib, mid=None):
                    for j in range(NT):
                        dve.wait_ge(S(f"ahi{p}"), NT * ib + j + 1)
                        src = strm[(j // SJ) % SG][:, j % SJ, :] if p == 2 else \
                            AT[:, j, ds(ib * WIDE, WIDE)]
                        dve.tensor_tensor(Alos[p][:, j % RING[p], :], src, Ahis[p][:, j % RING[p], :].bitcast(F32),
                                          ALU.subtract).then_inc(S(f"alo{p}"), 1)
                        if mid is not None:
                            mid(j)

                def split_g(ib, d):
                    dve.wait_ge(S(f"ghi{p}"), KD * ib + d + 1)
                    dve.tensor_tensor(Glo[:, d, :], PS[:, ds((ib % 2) * KD + d, 1), :].rearrange("p a n -> p (a n)"),
                                      Ghi[:, d, :].bitcast(F32), ALU.subtract).then_inc(S(f"glo{p}"), 1)

                def project(ib, u):
                    T = UB * ib + u
                    dve.wait_ge(S(f"u_done{p}"), T + 2)
                    dve.wait_ge(S(f"res{p}"), T + 1)
                    up = PS[:, U_PS[u % 2], 0:D]
                    if p < 2:
                        tile = R[:, ds(T, 1), :].rearrange("p a d -> p (a d)")
                        if p == 1 and u == 0:
                            dve.wait_ge(S("x_again"), 16)
                        ins = dve.scalar_tensor_tensor(tile, up, dis[:, 0, ds(T, 1)], tile if p else bgcn_bc[:, 0, :],
                                                       ALU.mult, ALU.add)
                    else:
                        ins = dve.tensor_scalar(U_sb[:, u % 2, :], up, dis[:, 1, ds(T, 1)], 0.0, ALU.mult, ALU.max)
                    ins.then_inc(S(f"u_sb{p}"), 1)

                def tile_stats(ib, u):
                    T = UB * ib + u
                    dve.wait_ge(S(f"res{p}"), T + 3)
                    norm_stats(R[:, ds(T, 1), :].rearrange("p a d -> p (a d)"), u, S(f"gstat{p}"), 2 * T)

                def block_var(ib):
                    dve.tensor_scalar(vare[:, ds(UB * ib, UB)], mvb[:, :, 1], LN_EPS, None,
                                      ALU.add).then_inc(S(f"vare{l}"), 1)

                def normalise(ib, h):
                    if h == 0:
                        dve.wait_ge(S(f"rstd{l}"), ib + 1)
                    for u in (2 * h, 2 * h + 1):
                        ins = dve.tensor_scalar(xnb[:, u, :], R[:, ds(UB * ib + u, 1), :].rearrange("p a d -> p (a d)"),
                                                mvb[:, u, 0:1], rstd[:, ds(UB * ib + u, 1)],
                                                ALU.subtract, ALU.mult)
                    if h == 1:
                        ins.then_inc(S(f"xn_out_ready{l}"), 1)

                def after(ib):
                    def mid(j):
                        if 2 <= j < 2 + KD:
                            split_g(ib, j - 2)
                        if 5 <= j < 5 + UB:
                            project(ib, j - 5)
                        if p == 0:
                            return
                        if 7 <= j < 7 + UB:
                            tile_stats(ib, j - 7)
                        if j == 11:
                            block_var(ib)
                        if j in (12, 13):
                            normalise(ib, j - 12)
                    return mid

                def first_mid(j):
                    if mid_before is not None:
                        mid_before(j)
                    if j in SPLIT_AT_DVE[p]:
                        split_x(p, src_x, 1 + SPLIT_AT_DVE[p].index(j))
                    if j == NT - 2:
                        split_w(p)

                split_x(p, src_x, 0)
                steps(0, first_mid)
                with dve.Fori(1, NB) as ib:
                    steps(ib, after(ib - 1))
                return after(NB - 1)

            def router(l):
                E, T = EXPERTS[l], COLS[l]
                c = Chain(dve, S(f"route{l}"))
                op = c.done
                Lg, L2g, ohg = L[:, :, 0:E], L2[:, :, 0:E], [o[:, :, 0:E] for o in oh]
                rtg, exg = rt[:, :, 0:E], ex[:, :, 0:E]

                for tiles, blocks in ((slice(0, NT - UB), NB - 1), (slice(NT - UB, NT), NB)):
                    n = tiles.stop - tiles.start
                    first_of = dec[:, EMAX - E:EMAX].unsqueeze(1).to_broadcast([P, n, E])
                    Lt, L2t, oht, rtt = Lg[:, tiles, :], L2g[:, tiles, :], [o[:, tiles, :] for o in ohg], rtg[:, tiles, :]
                    dve.wait_ge(S(f"lg_psum{l}"), blocks)
                    logits = PS[:, LG_PS if blocks < NB else LAST_LG_PS, tiles.start * E:tiles.stop * E].rearrange("p (t e) -> p t e", t=n)
                    op(dve.tensor_tensor(Lt, logits, bg_bc[:, 0:E].unsqueeze(1).to_broadcast([P, n, E]), ALU.add)
                       if l == 0 else dve.tensor_copy(Lt, logits))
                    for k, src in ((0, Lt), (1, L2t)):
                        if k:
                            op(dve.scalar_tensor_tensor(L2t, oht[0], LOWEST, Lt, ALU.mult, ALU.add))
                        op(dve.tensor_reduce(mx[k][:, tiles], src, AX.X, ALU.max))
                        op(dve.tensor_tensor(oht[k], src, per_token(mx[k][:, tiles], E), ALU.is_equal))
                        op(dve.tensor_tensor(rtt, oht[k], first_of, ALU.mult))
                        op(dve.tensor_reduce(pick[:, tiles], rtt, AX.X, ALU.max))
                        op(dve.tensor_tensor(oht[k], rtt, per_token(pick[:, tiles], E), ALU.is_equal))
                    ins = dve.tensor_tensor(M[:, 0:E, tiles].rearrange("p e t -> p t e"), oht[0], oht[1], ALU.add)
                    if blocks < NB:
                        op(ins)
                ins.then_inc(S("m_ready"), 1)
                op(dve.tensor_tensor(rtg, Lg, per_token(mx[0][:], E), ALU.subtract))
                dve.tensor_tensor(pick[:], mx[1][:], mx[0][:], ALU.subtract).then_inc(S("exp_in"), 1)
                dve.wait_ge(S("rank"), l + 1)
                inc2 = incl[:, 0:E, :].rearrange("p e t -> p (e t)")
                op(dve.tensor_tensor_scan(inc2, keep[:, 0:E, :].rearrange("p e t -> p (e t)"), PS[:, TOT_PS, 0:E * NT],
                                          0.0, ALU.mult, ALU.add))
                op(dve.tensor_tensor(more[:, 0:E, :], incl[:, 0:E, NT - 1:NT].to_broadcast([P, E, NT]),
                                     thr[:].unsqueeze(1).to_broadcast([P, E, NT]), ALU.is_gt))
                op(dve.tensor_reduce(tiles_e[:, 0:E], more[:, 0:E, :], AX.X, ALU.add))
                op(dve.tensor_tensor_scan(tend[:, 0:E], ones[:, 0:E], tiles_e[:, 0:E], 0.0, ALU.mult, ALU.add))
                op(dve.tensor_tensor(tstart[:, 0:E], tend[:, 0:E], tiles_e[:, 0:E], ALU.subtract))
                op(dve.tensor_tensor(more[:, 0:E, :].rearrange("p e t -> p (e t)"), PS[:, RANK_PS, 0:E * NT], inc2, ALU.add))
                op(dve.scalar_tensor_tensor(incl[:, 0:E, :], tstart[:, 0:E].unsqueeze(2).to_broadcast([P, E, NT]), float(P),
                                            more[:, 0:E, :], ALU.mult, ALU.add))
                slot_of = incl[:, 0:E, :].rearrange("p e t -> p t e")
                for k in range(2):
                    op(dve.tensor_tensor(L2g, ohg[k], slot_of, ALU.mult))
                    op(dve.tensor_reduce(pos[:, k, :], L2g, AX.X, ALU.add))
                op(dve.tensor_copy(pos_i[:], pos[:]))
                op(dve.tensor_scalar(rt_i[:, 0, :, :], pos_i[:], P - 1, None, ALU.bitwise_and))
                op(dve.tensor_scalar(rt_i[:, 1, :, :], pos_i[:], 7, None, ALU.logical_shift_right))
                op(dve.tensor_copy(rt_f[:], rt_i[:]))
                for k, (B, A) in enumerate(((Brow, Arhs), (Brow2, Arhs2))):
                    op(dve.tensor_tensor(B[:], iota[:].unsqueeze(1).to_broadcast([P, NT, P]),
                                         per_token(rt_f[:, 0, k, :], P), ALU.is_equal))
                    op(dve.tensor_tensor(Acol[:, :, 0:T], iota[:, 0:T].unsqueeze(1).to_broadcast([P, NT, T]),
                                         per_token(rt_f[:, 1, k, :], T), ALU.is_equal))
                    op(dve.tensor_tensor(A[:, :, 0, 0:T], Acol[:, :, 0:T], per_token(code[:, k, :], T), ALU.mult))
                    op(dve.tensor_scalar(A[:, :, 1, 0:T], Acol[:, :, 0:T], pid[:, 0:1], None, ALU.mult))
                    dve.sem_inc(S("inv_in"), 1)

                dve.wait_ge(S("exp_out"), 2 * (l + 1))
                op(dve.tensor_reduce(zsum[:], exg, AX.X, ALU.add))
                op(dve.reciprocal(zrec[:], zsum[:]))
                op(dve.tensor_copy(gate[:, 0, :], zrec[:]))
                op(dve.tensor_tensor(gate[:, 1, :], e2[:], zrec[:], ALU.mult))
                if l == 1:
                    op(dve.tensor_tensor(gsum[:], gate[:, 0, :], gate[:, 1, :], ALU.add))
                    op(dve.tensor_scalar(gsum[:], gsum[:], 1e-6, None, ALU.add))
                    op(dve.reciprocal(zrec[:], gsum[:]))
                    op(dve.tensor_tensor(gate[:], gate[:], zrec[:].unsqueeze(1).to_broadcast([P, 2, NT]), ALU.mult))

                dve.wait_ge(S("inv_out"), l + 1)
                op(dve.tensor_copy(F_sb[:, :, 0:T], PS[:, SLOT_PS, 0:2 * T].rearrange("p (a t) -> p a t", a=2)))
                op(dve.scalar_tensor_tensor(sl[:, 0, 0:T], F_sb[:, 0, 0:T], float(P), F_sb[:, 1, 0:T], ALU.mult, ALU.add))
                op(dve.tensor_scalar(sl[:, 1, 0:T], F_sb[:, 0, 0:T], 0.0, 4.0 * N, ALU.is_equal, ALU.mult))
                op(dve.scalar_tensor_tensor(idx[:, 1, 0:T], sl[:, 0, 0:T], float(-P), sl[:, 1, 0:T], ALU.add, ALU.add))
                op(dve.tensor_scalar(sl[:, 2, 0:T], F_sb[:, 0, 0:T], NT + 0.5, -float(N), ALU.is_gt, ALU.mult))
                op(dve.scalar_tensor_tensor(sl[:, 3, 0:T], sl[:, 0, 0:T], float(-P), sl[:, 2, 0:T], ALU.add, ALU.add))
                op(dve.tensor_scalar(idx[:, 0, 0:T], sl[:, 3, 0:T], 0.0, None, ALU.max))
                dve.sem_inc(S("slots"), 1)

                tt = iota[0:1, 0:T].unsqueeze(2).to_broadcast([1, T, E])
                op(dve.tensor_tensor(tcmp[:, 0:T, 0:E], tend[0:1, 0:E].unsqueeze(1).to_broadcast([1, T, E]), tt, ALU.is_le))
                op(dve.tensor_reduce(tsum[:, 0, 0:T], tcmp[:, 0:T, 0:E], AX.X, ALU.add))
                op(dve.tensor_scalar(tsum[:, 0, 0:T], tsum[:, 0, 0:T], float(E - 1), None, ALU.min))
                op(dve.tensor_tensor(tcmp[:, 0:T, 0:E - 1], tstart[0:1, 0:E - 1].unsqueeze(1).to_broadcast([1, T, E - 1]),
                                     iota[0:1, 0:T].unsqueeze(2).to_broadcast([1, T, E - 1]), ALU.is_equal))
                op(dve.tensor_reduce(tsum[:, 1, 0:T], tcmp[:, 0:T, 0:E - 1], AX.X, ALU.add))
                op(dve.tensor_scalar(tsum[:, 2, 0:T], iota[0:1, 0:T], tend[0:1, E - 1:E], None, ALU.is_lt))
                op(dve.scalar_tensor_tensor(tsum[:, 1, 0:T], tsum[:, 0, 0:T], 2.0, tsum[:, 1, 0:T], ALU.mult, ALU.add))
                op(dve.tensor_copy(table[:, :, 0:T], tsum[:, 1:3, 0:T]))
                op(dve.tensor_reduce(lastf[:, 0:1], tsum[:, 2, 0:T].rearrange("p (i o) -> p i o", o=2)[:, :, 0], AX.X, ALU.add))
                op(dve.tensor_scalar(last[:, l:l + 1], lastf[:, 0:1], -1.0, None, ALU.add))

                dve.sem_inc(S("routed"), 1)

            def experts(l):
                E, T = EXPERTS[l], TILES[l]

                def split1_dyn(e, k):
                    dve.wait_ge(S(f"w1_hi{l}"), KD * (e + 1) + k + 1)
                    dve.tensor_tensor(w1lo[:, ds((e + 1) % 2, 1), k, :].rearrange("p a h -> p (a h)"), raw1[:, k, :],
                                      w1hi[:, ds((e + 1) % 2, 1), k, :].rearrange("p a h -> p (a h)").bitcast(F32),
                                      ALU.subtract).then_inc(S(f"w1_split{l}"), 1)

                def x_lo(t, odd):
                    dve.wait_ge(S(f"x_hi{l}"), t + 1)
                    dve.tensor_tensor(xTlo[:], PS[:, XG_PS[odd], 0:KD * P].rearrange("p (k t) -> p k t", k=KD),
                                      xThi[:].bitcast(F32), ALU.subtract).then_inc(S(f"x_lo{l}"), 1)

                def add_b2(pair, odd, slot):
                    dve.wait_ge(S(f"y_done{l}"), 2 * pair + odd + 1)
                    if not isinstance(pair, int) or pair > 0:
                        dve.wait_ge(S(f"y{odd}_out{l}"), 16 * pair)
                    dve.tensor_tensor(y_sb[odd][:], PS[:, Y_PS, 0:D], b2_bc[:, ds(slot, 1), :].rearrange("p a d -> p (a d)"),
                                      ALU.add).then_inc(S(f"y_ready{l}"), 1)

                def tile(pair, odd, first=False, second=False, seen=None, ahead=False):
                    t = 2 * pair + odd
                    if first:
                        e = 0
                    else:
                        (e, opens), (e_before, _) = seen or (look(dve, l, t), look(dve, l, t - 1))
                    for b in range(HB):
                        dve.wait_ge(S(f"h_done{l}"), HB * t + b + 1)
                        if first and b == 0:
                            dve.wait_ge(S(f"b_in{l}"), 32)
                        bias = b1_bc[:, ds(e % 4, 1), b * BANK:(b + 1) * BANK].rearrange("p a h -> p (a h)")
                        dve.tensor_tensor(hrow[:, b * BANK:(b + 1) * BANK], PS[:, H_PS[b], :], bias,
                                          ALU.add).then_inc(S(f"h_biased{l}"), 1)
                    x_lo(t + 1, 1 - odd)
                    seen = (look(dve, l, t + 1), (e, opens)) if ahead else None
                    if first:
                        for k in range(KD):
                            split1_dyn(0, k)
                    else:
                        with dve.If(opens == 1):
                            for k in range(KD):
                                split1_dyn(e, k)
                        add_b2(*tile_at(pair, odd, -1), e_before % 4)
                    for b in range(HB):
                        dve.wait_ge(S(f"h_hi{l}"), HB * t + b + 1)
                        dve.tensor_tensor(hTlo[:, b * HCB:(b + 1) * HCB, :],
                                          PS[:, HT_PS[b], :].rearrange("p (c t) -> p c t", c=HCB),
                                          hThi[:, b * HCB:(b + 1) * HCB, :].bitcast(F32),
                                          ALU.subtract).then_inc(S(f"h_lo{l}"), 1)
                    return seen

                x_lo(0, 0)
                tile(0, 0, first=True)
                tile(0, 1, second=True)
                seen = None
                for n in range(2 * PEEL[l]):
                    seen = tile(1 + n // 2, n % 2, seen=seen)
                with dve.Fori(1 + PEEL[l], SURE[l] // 2, 2) as first_pair:
                    seen = None
                    for n in range(4):
                        seen = tile(first_pair + n // 2, n % 2, seen=seen, ahead=n < 3)
                with dve.Fori(0, RUNS[l]) as r:
                    run_used = dve.value_load(table[0:1, 1, ds(r * (2 * RUN) + SURE[l], 1)], min_val=0, max_val=1)
                    with dve.If(run_used == 1):
                        with dve.Fori(0, RUN) as i:
                            pair = r * RUN + SURE[l] // 2 + i
                            used = dve.value_load(table[0:1, 1, ds(pair * 2, 1)], min_val=0, max_val=1)
                            with dve.If(used == 1):
                                seen = None
                                for odd in range(2):
                                    seen = tile(pair, odd, seen=seen, ahead=odd == 0)
                            dve.nop()
                    dve.nop()
                pair = dve.value_load(last[0:1, l:l + 1], min_val=SURE[l] // 2 - 1, max_val=SURE[l] // 2 + RUN * RUNS[l] - 1)
                add_b2(pair, 1, (E - 1) % 4)

            cc = Chain(dve, S("combine"))

            def block_stats(src, q):
                tiles = range(q * UB, (q + 1) * UB)
                for u, T in enumerate(tiles):
                    ins = dve.bn_stats(stats[:, u, :], src[:, T, :])
                cc.done(ins)
                for u, T in enumerate(tiles):
                    ins = dve.bn_aggr(mv[:, T, :], stats[:, u, :])
                cc.done(ins)
                four = slice(q * UB, (q + 1) * UB)
                dve.tensor_scalar(vare[:, four], mv[:, four, 1], LN_EPS, None, ALU.add).then_inc(S("cmb_vare"), 1)

            def comb_a(q):
                four = slice(q * UB, (q + 1) * UB)
                if q == 0:
                    dve.wait_ge(S(f"yc{q}_in"), 32)
                    for k in range(2):
                        for u in range(UB):
                            ins = dve.scalar_tensor_tensor(XN[:, u, :], Yc[:, q, k, u, :], gate[:, k, u:u + 1], XN[:, u, :],
                                                           ALU.mult, ALU.add)
                        cc.done(ins)
                else:
                    dve.wait_ge(S("y_sum"), q)
                    cc.done(dve.tensor_tensor(XN[:, four, :], XN[:, four, :], Yc[:, q, 0, :, :], ALU.add))
                block_stats(XN, q)

            def comb_shift(q, n):
                dve.wait_ge(S("cmb_rstd"), n)
                four = slice(q * UB, (q + 1) * UB)
                dve.scalar_tensor_tensor(cshift[:, four], mv[:, four, 0], -1.0, rstd[:, four],
                                         ALU.mult, ALU.mult).then_inc(S("y_shift"), 1)

            def comb_b(q):
                dve.wait_ge(S("y_gamma"), q + 1)
                four = slice(q * UB, (q + 1) * UB)
                cc.done(dve.tensor_tensor(R[:, four, :], R[:, four, :], XN[:, four, :], ALU.add))
                block_stats(R, q)

            def comb_c(q, n):
                dve.wait_ge(S("cmb_rstd"), n)
                four = slice(q * UB, (q + 1) * UB)
                cc.done(dve.tensor_tensor(cscale[:, four], rstd[:, four], dis[:, 1, four], ALU.mult))
                dve.scalar_tensor_tensor(cshift[:, four], mv[:, four, 0], -1.0, cscale[:, four],
                                         ALU.mult, ALU.mult).then_inc(S("x_shift"), 1)

            def combine0():
                dve.wait_ge(S("xn_in"), 32)
                dve.wait_ge(S("gb_in"), 32)
                cc.done(dve.tensor_tensor(R[:], R[:], gb_bc[:, 1, :].unsqueeze(1).to_broadcast([P, NT, D]), ALU.add))
                comb_a(0)
                comb_shift(0, 1)
                comb_a(1)
                comb_a(2)
                comb_shift(1, 2)
                comb_b(0)
                comb_a(3)
                comb_c(0, 4)
                comb_shift(2, 3)
                comb_b(1)

            def combine0_rest(j):
                if j == 0:
                    comb_c(1, 6)
                    comb_shift(3, 5)
                if j == 2:
                    comb_b(2)
                if j == 3:
                    comb_c(2, 7)
                if j == 5:
                    comb_b(3)
                if j == 7:
                    comb_c(3, 8)

            def combine1():
                for q in range(NB):
                    dve.wait_ge(S(f"yc{q}_in"), 64)
                    for k in range(2):
                        for u in range(UB):
                            T = q * UB + u
                            ins = dve.scalar_tensor_tensor(R[:, T, :], Yc[:, q, k, u, :], gate[:, k, T:T + 1], R[:, T, :],
                                                           ALU.mult, ALU.add)
                        if k == 0:
                            cc.done(ins)
                    ins.then_inc(S("final"), 1)

            end = gnn(1, gnn(0, scale_last))
            for j in range(NT):
                end(j)
            router(0)
            experts(0)
            combine0()
            end = gnn(2, combine0_rest)
            for j in range(NT):
                end(j)
            router(1)
            experts(1)
            combine1()

        @block.tensor
        def _(pe):
            pe.wait_ge(S("consts"), 1)
            for p in range(3):
                pe.sem_inc(S(f"a_free{p}"), RING[p])
                pe.sem_inc(S(f"u_done{p}"), 1)
                pe.sem_inc(S(f"u_sb{p}"), 2)
                pe.sem_inc(S(f"res{p}"), 2)

            def transposes(i, u, first):
                pe.wait_ge(S(f"stage_in{u}"), 16 * (i + 1))
                r = i * STG + u
                for q in range(4):
                    if not first:
                        pe.wait_ge(S("at_copied"), 4 * r + q - 3)
                    for k in range(4):
                        j = 4 * q + k
                        ins = pe.transpose(PS[:, 4 + q, k * P:(k + 1) * P], stage[u][:, j * P:(j + 1) * P], ident)
                    ins.then_inc(S("at_psum"), 1)

            def rows(i, first):
                for u in range(STG):
                    transposes(i, u, first and u == 0)

            rows(0, True)
            with pe.Fori(1, NT // STG) as i:
                rows(i, False)

            def gnn(p, mid_before=None):
                l = p - 1

                def steps(ib, mid=None):
                    for j in range(NT):
                        if mid is first_mid and j % UB == 0:
                            pe.wait_ge(S(f"xlo{p}"), j // UB + 1)
                        hi, lo = Ahis[p][:, j % RING[p], :], Alos[p][:, j % RING[p], :]
                        g = [PS[:, ds((ib % 2) * KD + d, 1), :].rearrange("p a n -> p (a n)") for d in range(KD)]
                        dd = [slice(d * P, (d + 1) * P) for d in range(KD)]
                        pe.wait_ge(S(f"ahi{p}"), NT * ib + j + 1)
                        for d in range(KD):
                            pe.matmul(g[d], Xhi[:, j, dd[d]], hi, start=(j == 0), stop=False)
                            pe.matmul(g[d], Xlo[:, j, dd[d]], hi, start=False, stop=False)
                        pe.wait_ge(S(f"alo{p}"), NT * ib + j + 1)
                        for d in range(KD):
                            ins = pe.matmul(g[d], Xhi[:, j, dd[d]], lo, start=False, stop=(j == NT - 1))
                        ins.then_inc(S(f"a_free{p}"), 1)
                        if mid is not None:
                            mid(j)

                def project(ib, u):
                    T = UB * ib + u
                    if u == 0:
                        pe.wait_ge(S(f"glo{p}"), KD * (ib + 1))
                    pe.wait_ge(S(f"u_sb{p}"), T + 1)
                    up = PS[:, U_PS[u % 2], 0:D]
                    tt = slice(u * P, (u + 1) * P)
                    for d in range(KD):
                        pe.matmul(up, Ghi[:, d, tt], Whi[:, d, :], start=(d == 0), stop=False)
                        pe.matmul(up, Ghi[:, d, tt], Wlo[:, d, :], start=False, stop=False)
                        ins = pe.matmul(up, Glo[:, d, tt], Whi[:, d, :], start=False, stop=(d == KD - 1))
                    ins.then_inc(S(f"u_done{p}"), 1)

                def gate_x(ib):
                    pe.wait_ge(S(f"xn_out_ready{l}"), ib + 1)
                    for h in range(2):
                        for n in range(2):
                            for k in range(KD):
                                at = (n * KD + k) * P
                                ins = pe.transpose(PS[:, XT_PS[h], at:at + P], xnb[:, 2 * h + n, k * P:(k + 1) * P], ident)
                        ins.then_inc(S(f"xt_psum{l}"), 1)

                def gate_y(ib, last):
                    E = EXPERTS[l]
                    pe.wait_ge(S(f"xnT{l}"), 2 * ib + 2)
                    for u in range(UB):
                        for k in range(KD):
                            at = ((u % 2) * KD + k) * P
                            bank = LAST_LG_PS if last else LG_PS
                            ins = pe.matmul(PS[:, bank, ds((ib * UB + u) * E, E)], xnT[:, u // 2, at:at + P], wgate[:, k, l, 0:E],
                                            start=(k == 0), stop=(k == KD - 1))
                    ins.then_inc(S(f"lg_psum{l}"), 1)

                def after(ib, last=False):
                    def mid(j):
                        if 3 <= j < 3 + UB:
                            project(ib, j - 3)
                        if p > 0 and j == 13:
                            gate_x(ib)
                        if p > 0 and j == NT - 1:
                            gate_y(ib, last)
                    return mid

                def first_mid(j):
                    if mid_before is not None:
                        mid_before(j)
                    if j == NT - 1:
                        pe.wait_ge(S("wg_split"), p + 1)

                steps(0, first_mid)
                with pe.Fori(1, NB) as ib:
                    steps(ib, after(ib - 1))
                return after(NB - 1, last=True)

            def router(l):
                E, T = EXPERTS[l], COLS[l]
                Mg = M[:, 0:E, :].rearrange("p e t -> p (e t)")
                pe.wait_ge(S("m_ready"), l + 1)
                pe.matmul(PS[:, RANK_PS, 0:E * NT], before[:], Mg, start=True, stop=True)
                pe.matmul(PS[:, TOT_PS, 0:E * NT], ones[:], Mg, start=True, stop=True).then_inc(S("rank"), 1)
                for k, (B, A) in enumerate(((Brow, Arhs), (Brow2, Arhs2))):
                    pe.wait_ge(S("inv_in"), 2 * l + k + 1)
                    for t in range(NT):
                        ins = pe.matmul(PS[:, SLOT_PS, 0:2 * T].rearrange("p (a t) -> p a t", a=2), B[:, t, :],
                                        A[:, t, :, 0:T], start=(k == 0 and t == 0), stop=(k == 1 and t == NT - 1))
                ins.then_inc(S("inv_out"), 1)

            def experts(l):
                E, T = EXPERTS[l], TILES[l]

                def up(t, slot):
                    for b in range(HB):
                        cols = slice(b * BANK, (b + 1) * BANK)
                        for k in range(KD):
                            hi = w1hi[:, ds(slot, 1), k, cols].rearrange("p a h -> p (a h)")
                            lo = w1lo[:, ds(slot, 1), k, cols].rearrange("p a h -> p (a h)")
                            pe.matmul(PS[:, H_PS[b], :], xThi[:, k, :], hi, start=(k == 0), stop=False)
                            pe.matmul(PS[:, H_PS[b], :], xThi[:, k, :], lo, start=False, stop=False)
                            ins = pe.matmul(PS[:, H_PS[b], :], xTlo[:, k, :], hi, start=False, stop=(k == KD - 1))
                        ins.then_inc(S(f"h_done{l}"), 1)

                def x_t(pair, odd):
                    pe.wait_ge(S(f"xg{odd}_in{l}"), 16 * (pair + 1))
                    for k in range(KD):
                        ins = pe.transpose(PS[:, XG_PS[odd], k * P:(k + 1) * P], xg[odd][:, k * P:(k + 1) * P], ident)
                    ins.then_inc(S(f"xt_done{l}"), 1)

                def h_t(t):
                    for b in range(HB):
                        pe.wait_ge(S(f"h_act{l}"), HB * t + b + 1)
                        for k in range(HCB):
                            cc = b * HCB + k
                            ins = pe.transpose(PS[:, HT_PS[b], k * P:(k + 1) * P], hrow[:, cc * P:(cc + 1) * P], ident)
                        ins.then_inc(S(f"ht_done{l}"), 1)

                def down(t, slot):
                    pe.wait_ge(S(f"h_lo{l}"), HB * (t + 1))
                    for k in range(HC):
                        hi = w2hi[:, ds(slot, 1), k, :].rearrange("p a h -> p (a h)")
                        lo = w2lo[:, ds(slot, 1), k, :].rearrange("p a h -> p (a h)")
                        yp = PS[:, Y_PS, 0:D]
                        pe.matmul(yp, hThi[:, k, :], hi, start=(k == 0), stop=False)
                        pe.matmul(yp, hThi[:, k, :], lo, start=False, stop=False)
                        ins = pe.matmul(yp, hTlo[:, k, :], hi, start=False, stop=(k == HC - 1))
                    ins.then_inc(S(f"y_done{l}"), 1)

                def tile(pair, odd, first=False, seen=None, ahead=False):
                    t = 2 * pair + odd
                    e_next = look(pe, l, t + 1)[0]
                    if not first:
                        e_before, e = seen or (look(pe, l, t - 1)[0], look(pe, l, t)[0] if ahead else None)
                    seen = (e, e_next) if ahead else None
                    x_t(pair + 1, odd)
                    if not first:
                        pe.wait_ge(S(f"w2_split{l}"), 2 * (e_before + 1))
                        down(t - 1, e_before % 2)
                    h_t(t)
                    pe.wait_ge(S(f"x_lo{l}"), t + 2)
                    pe.wait_ge(S(f"w1_split{l}"), KD * (e_next + 1))
                    up(t + 1, e_next % 2)
                    return seen

                x_t(0, 0)
                pe.wait_ge(S(f"x_lo{l}"), 1)
                pe.wait_ge(S(f"w1_split{l}"), KD)
                up(0, 0)
                x_t(0, 1)
                pe.wait_ge(S("routed"), l + 1)
                tile(0, 0, first=True)
                tile(0, 1)
                seen = None
                for n in range(2 * PEEL[l]):
                    seen = tile(1 + n // 2, n % 2, seen=seen)
                with pe.Fori(1 + PEEL[l], SURE[l] // 2, 2) as first_pair:
                    seen = None
                    for n in range(4):
                        seen = tile(first_pair + n // 2, n % 2, seen=seen, ahead=n < 3)
                with pe.Fori(0, RUNS[l]) as r:
                    run_used = pe.value_load(table[0:1, 1, ds(r * (2 * RUN) + SURE[l], 1)], min_val=0, max_val=1)
                    with pe.If(run_used == 1):
                        with pe.Fori(0, RUN) as i:
                            pair = r * RUN + SURE[l] // 2 + i
                            used = pe.value_load(table[0:1, 1, ds(pair * 2, 1)], min_val=0, max_val=1)
                            with pe.If(used == 1):
                                seen = None
                                for odd in range(2):
                                    seen = tile(pair, odd, seen=seen, ahead=odd == 0)
                            pe.nop()
                    pe.nop()
                pair = pe.value_load(last[0:1, l:l + 1], min_val=SURE[l] // 2 - 1, max_val=SURE[l] // 2 + RUN * RUNS[l] - 1)
                pe.wait_ge(S(f"w2_split{l}"), 2 * E)
                down(2 * pair + 1, (E - 1) % 2)

            end = gnn(1, gnn(0))
            for j in range(NT):
                end(j)
            router(0)
            experts(0)
            end = gnn(2)
            for j in range(NT):
                end(j)
            router(1)
            experts(1)


_INS = ['x', 'adj', 'L0_gnn_Wgcn1', 'L0_gnn_bgcn1', 'L0_gnn_Wgcn12', 'L0_gnn_bgcn12', 'L0_ffn_Wg', 'L0_ffn_bg',
        'L0_ffn_W1', 'L0_ffn_b1', 'L0_ffn_W2', 'L0_ffn_b2', 'L0_ffn_gamma', 'L0_ffn_beta', 'L1_gnn_W', 'L1_ffn_Wg',
        'L1_ffn_W1', 'L1_ffn_b1', 'L1_ffn_W2', 'L1_ffn_b2']


def kernel(**inputs):
    import numpy as _np
    import concourse.bacc as _bacc
    from concourse import mybir as _mybir
    from concourse.bass_utils import run_bass_kernel_spmd as _run

    nc = _bacc.Bacc("TRN2", target_bir_lowering=False, num_devices=1)
    arrays, args = {}, []
    for name in _INS:
        a = _np.ascontiguousarray(inputs[name])
        arrays[f"in_{name}_dram"] = a
        args.append(nc.dram_tensor(f"in_{name}_dram", a.shape, _mybir.dt.from_np(a.dtype), kind="ExternalInput").ap())
    out = nc.dram_tensor("out_0_dram", inputs["x"].shape, _mybir.dt.float32, kind="ExternalOutput").ap()
    moe_gnn_kernel(nc, *args, out)
    r = _run(nc, [arrays], core_ids=[0])
    return r.results[0]["out_0_dram"]
```
